# Optimizing a Trainium2 kernel written in Bass

```python
import numpy as np
import jax
import jax.numpy as jnp

def _softmax(x, axis=-1):
    return jax.nn.softmax(x, axis=axis)

def _gelu(x):
    return jax.nn.gelu(x, approximate=True)

def _silu(x):
    return jax.nn.silu(x)

def _sigmoid(x):
    return jax.nn.sigmoid(x)

def _layernorm(x, axis=-1, eps=1e-05):
    m = jnp.mean(x, axis=axis, keepdims=True)
    v = jnp.var(x, axis=axis, keepdims=True)
    return (x - m) / jnp.sqrt(v + eps)

def _scatter_add(tgt, idx, src, axis=0):
    return tgt.at[idx].add(src)

def _segment_sum(src, seg, n):
    return jax.ops.segment_sum(src, seg, n)
kernel_name = 'mk_seq_preln_d2_jaxref_r8_550270'

def setup_inputs(seed: int=0):
    np.random.seed(seed)
    _w = jnp.asarray

    def _L0_attn_setup():
        import jax, jax.numpy as jnp
        import numpy as np
        D_MODEL = 128
        IDX_HEADS = 4
        IDX_DIM = 64
        TOP_K = 32

        def _rope(x):
            B, S, D = x.shape
            half = D // 2
            inv_freq = 1.0 / 10000.0 ** (jnp.arange(half, dtype=jnp.float32) / half)
            ang = jnp.arange(S, dtype=jnp.float32)[:, None] * inv_freq[None, :]
            cos, sin = (jnp.cos(ang), jnp.sin(ang))
            x1, x2 = (x[..., :half], x[..., half:])
            return jnp.concatenate([x1 * cos - x2 * sin, x1 * sin + x2 * cos], axis=-1)
        key = jax.random.key(seed)
        ks = jax.random.split(key, 11)
        B, S, D = (2, 512, D_MODEL)
        s = 0.02
        return {'x': jax.random.normal(ks[0], (B, S, D), dtype=jnp.float32), 'w_qkv': jax.random.normal(ks[1], (3 * D, D), dtype=jnp.float32) * s, 'b_qkv': jnp.zeros((3 * D,), dtype=jnp.float32), 'w_o': jax.random.normal(ks[2], (D, D), dtype=jnp.float32) * s, 'b_o': jnp.zeros((D,), dtype=jnp.float32), 'w_iq': jax.random.normal(ks[3], (IDX_HEADS * IDX_DIM, D), dtype=jnp.float32) * s, 'b_iq': jnp.zeros((IDX_HEADS * IDX_DIM,), dtype=jnp.float32), 'w_ik': jax.random.normal(ks[4], (IDX_DIM, D), dtype=jnp.float32) * s, 'b_ik': jnp.zeros((IDX_DIM,), dtype=jnp.float32), 'w_iw': jax.random.normal(ks[5], (IDX_HEADS, D), dtype=jnp.float32) * s, 'b_iw': jnp.zeros((IDX_HEADS,), dtype=jnp.float32)}
    _L0_attn_in = _L0_attn_setup()

    def _L0_ffn_setup():
        import jax, jax.numpy as jnp
        import numpy as np
        EPS = 1e-06
        TOP_K = 2

        def rms_norm(x, scale, eps=EPS):
            xf = x.astype(jnp.float32)
            mean_sq = jnp.mean(xf * xf, axis=-1, keepdims=True)
            return (xf * (scale.astype(jnp.float32) * jax.lax.rsqrt(mean_sq + eps))).astype(x.dtype)
        key = jax.random.key(seed)
        k0, k1, k2, k3 = jax.random.split(key, 4)
        B, S, D, H, E = (2, 256, 128, 352, 8)
        x = jax.random.normal(k0, (B, S, D), dtype=jnp.float32)
        norm_scale = jnp.ones((D,), dtype=jnp.float32)
        w_router = jax.random.normal(k1, (E, D), dtype=jnp.float32) * 0.02
        w_up = jax.random.normal(k2, (E, 2 * H, D), dtype=jnp.float32) * 0.02
        w_down = jax.random.normal(k3, (E, D, H), dtype=jnp.float32) * 0.02
        return {'x': x, 'norm_scale': norm_scale, 'w_router': w_router, 'w_up': w_up, 'w_down': w_down}
    _L0_ffn_in = _L0_ffn_setup()

    def _L1_attn_setup():
        import jax, jax.numpy as jnp
        import numpy as np
        D_MODEL = 128
        D_INNER = 256
        D_STATE = 16
        DT_RANK = 64
        D_CONV = 4
        EPS = 1e-05
        B_SZ, L = (2, 256)

        def _silu(x):
            return x * jax.nn.sigmoid(x)
        key = jax.random.key(seed)
        ks = jax.random.split(key, 8)
        s = 0.02
        inp = {'x': jax.random.normal(ks[0], (B_SZ, L, D_MODEL), jnp.float32), 'in_proj_w': jax.random.normal(ks[1], (D_MODEL, 2 * D_INNER), jnp.float32) * s, 'conv_w': jax.random.normal(ks[2], (D_INNER, 1, D_CONV), jnp.float32) * s, 'conv_b': jnp.zeros((D_INNER,), jnp.float32), 'x_proj_w': jax.random.normal(ks[3], (D_INNER, DT_RANK + 2 * D_STATE), jnp.float32) * s, 'dt_proj_w': jax.random.normal(ks[4], (DT_RANK, D_INNER), jnp.float32) * s, 'dt_proj_b': jax.random.normal(ks[5], (D_INNER,), jnp.float32) * s, 'A_log': jnp.log(jnp.broadcast_to(jnp.arange(1, D_STATE + 1, dtype=jnp.float32), (D_INNER, D_STATE))), 'D': jnp.ones((D_INNER,), jnp.float32), 'out_proj_w': jax.random.normal(ks[6], (D_INNER, D_MODEL), jnp.float32) * s, 'norm_w': jnp.ones((D_MODEL,), jnp.float32)}
        return inp
    _L1_attn_in = _L1_attn_setup()

    def _L1_ffn_setup():
        import jax, jax.numpy as jnp
        import numpy as np
        from jax import lax
        D = 128
        H = 176
        E = 8
        K = 2
        ROUTER_SCALE = 1.0

        def _expert(x, w1, b1, w3, b3, w2, b2):
            h = jax.nn.silu((x @ w1 + b1) * (x @ w3 + b3))
            return h @ w2 + b2
        key = jax.random.key(seed)
        ks = jax.random.split(key, 16)
        s = 0.02
        inp = {'x': jax.random.normal(ks[0], (2, 256, D), dtype=jnp.float32), 'gate_w': jax.random.normal(ks[1], (E, D), dtype=jnp.float32) * s, 'gate_b': jax.random.normal(ks[2], (E,), dtype=jnp.float32) * s, 'w1': jax.random.normal(ks[3], (E, D, H), dtype=jnp.float32) * s, 'b1': jax.random.normal(ks[4], (E, H), dtype=jnp.float32) * s, 'w3': jax.random.normal(ks[5], (E, D, H), dtype=jnp.float32) * s, 'b3': jax.random.normal(ks[6], (E, H), dtype=jnp.float32) * s, 'w2': jax.random.normal(ks[7], (E, H, D), dtype=jnp.float32) * s, 'b2': jax.random.normal(ks[8], (E, D), dtype=jnp.float32) * s, 'sw1': jax.random.normal(ks[9], (D, H), dtype=jnp.float32) * s, 'sb1': jax.random.normal(ks[10], (H,), dtype=jnp.float32) * s, 'sw3': jax.random.normal(ks[11], (D, H), dtype=jnp.float32) * s, 'sb3': jax.random.normal(ks[12], (H,), dtype=jnp.float32) * s, 'sw2': jax.random.normal(ks[13], (H, D), dtype=jnp.float32) * s, 'sb2': jax.random.normal(ks[14], (D,), dtype=jnp.float32) * s}
        return inp
    _L1_ffn_in = _L1_ffn_setup()
    _d = {'L0_attn_x': _L0_attn_in['x'], 'L0_attn_w_qkv': _L0_attn_in['w_qkv'], 'L0_attn_b_qkv': _L0_attn_in['b_qkv'], 'L0_attn_w_o': _L0_attn_in['w_o'], 'L0_attn_b_o': _L0_attn_in['b_o'], 'L0_attn_w_iq': _L0_attn_in['w_iq'], 'L0_attn_b_iq': _L0_attn_in['b_iq'], 'L0_attn_w_ik': _L0_attn_in['w_ik'], 'L0_attn_b_ik': _L0_attn_in['b_ik'], 'L0_attn_w_iw': _L0_attn_in['w_iw'], 'L0_attn_b_iw': _L0_attn_in['b_iw'], 'L0_ffn_norm_scale': _L0_ffn_in['norm_scale'], 'L0_ffn_w_router': _L0_ffn_in['w_router'], 'L0_ffn_w_up': _L0_ffn_in['w_up'], 'L0_ffn_w_down': _L0_ffn_in['w_down'], 'L1_attn_in_proj_w': _L1_attn_in['in_proj_w'], 'L1_attn_conv_w': _L1_attn_in['conv_w'], 'L1_attn_conv_b': _L1_attn_in['conv_b'], 'L1_attn_x_proj_w': _L1_attn_in['x_proj_w'], 'L1_attn_dt_proj_w': _L1_attn_in['dt_proj_w'], 'L1_attn_dt_proj_b': _L1_attn_in['dt_proj_b'], 'L1_attn_A_log': _L1_attn_in['A_log'], 'L1_attn_D': _L1_attn_in['D'], 'L1_attn_out_proj_w': _L1_attn_in['out_proj_w'], 'L1_attn_norm_w': _L1_attn_in['norm_w'], 'L1_ffn_gate_w': _L1_ffn_in['gate_w'], 'L1_ffn_gate_b': _L1_ffn_in['gate_b'], 'L1_ffn_w1': _L1_ffn_in['w1'], 'L1_ffn_b1': _L1_ffn_in['b1'], 'L1_ffn_w3': _L1_ffn_in['w3'], 'L1_ffn_b3': _L1_ffn_in['b3'], 'L1_ffn_w2': _L1_ffn_in['w2'], 'L1_ffn_b2': _L1_ffn_in['b2'], 'L1_ffn_sw1': _L1_ffn_in['sw1'], 'L1_ffn_sb1': _L1_ffn_in['sb1'], 'L1_ffn_sw3': _L1_ffn_in['sw3'], 'L1_ffn_sb3': _L1_ffn_in['sb3'], 'L1_ffn_sw2': _L1_ffn_in['sw2'], 'L1_ffn_sb2': _L1_ffn_in['sb2']}
    _x0 = _d['L0_attn_x']
    _d['L0_attn_x'] = jax.random.normal(jax.random.fold_in(jax.random.key(seed), 1), (16, 256, 128), dtype=_x0.dtype)
    del _x0
    return _d

def reference(L0_attn_x, L0_attn_w_qkv, L0_attn_b_qkv, L0_attn_w_o, L0_attn_b_o, L0_attn_w_iq, L0_attn_b_iq, L0_attn_w_ik, L0_attn_b_ik, L0_attn_w_iw, L0_attn_b_iw, L0_ffn_norm_scale, L0_ffn_w_router, L0_ffn_w_up, L0_ffn_w_down, L1_attn_in_proj_w, L1_attn_conv_w, L1_attn_conv_b, L1_attn_x_proj_w, L1_attn_dt_proj_w, L1_attn_dt_proj_b, L1_attn_A_log, L1_attn_D, L1_attn_out_proj_w, L1_attn_norm_w, L1_ffn_gate_w, L1_ffn_gate_b, L1_ffn_w1, L1_ffn_b1, L1_ffn_w3, L1_ffn_b3, L1_ffn_w2, L1_ffn_b2, L1_ffn_sw1, L1_ffn_sb1, L1_ffn_sw3, L1_ffn_sb3, L1_ffn_sw2, L1_ffn_sb2):

    def _L0_attn_ref(x, w_qkv, b_qkv, w_o, b_o, w_iq, b_iq, w_ik, b_ik, w_iw, b_iw):
        import jax, jax.numpy as jnp
        import numpy as np
        D_MODEL = 128
        IDX_HEADS = 4
        IDX_DIM = 64
        TOP_K = 32

        def _rope(x):
            B, S, D = x.shape
            half = D // 2
            inv_freq = 1.0 / 10000.0 ** (jnp.arange(half, dtype=jnp.float32) / half)
            ang = jnp.arange(S, dtype=jnp.float32)[:, None] * inv_freq[None, :]
            cos, sin = (jnp.cos(ang), jnp.sin(ang))
            x1, x2 = (x[..., :half], x[..., half:])
            return jnp.concatenate([x1 * cos - x2 * sin, x1 * sin + x2 * cos], axis=-1)
        B, S, D = x.shape
        qkv = x @ w_qkv.T + b_qkv
        Q, K, V = jnp.split(qkv, 3, axis=-1)
        Q, K = (_rope(Q), _rope(K))
        iq = (x @ w_iq.T + b_iq).reshape(B, S, IDX_HEADS, IDX_DIM)
        ik = x @ w_ik.T + b_ik
        iw = x @ w_iw.T + b_iw
        head_scores = jax.nn.relu(jnp.einsum('bqhd,bkd->bhqk', iq, ik))
        index_scores = jnp.einsum('bhqk,bqh->bqk', head_scores, iw)
        k = min(TOP_K, S)
        _, top_idx = jax.lax.top_k(index_scores, k)
        mask = jnp.zeros((B, S, S), dtype=bool)
        mask = mask.at[jnp.arange(B)[:, None, None], jnp.arange(S)[None, :, None], top_idx].set(True)
        attn_bias = jnp.where(mask, 0.0, -jnp.inf)
        scale = 1.0 / np.sqrt(D).astype(np.float32)
        logits = jnp.einsum('bqd,bkd->bqk', Q, K) * scale + attn_bias
        attn = jax.nn.softmax(logits, axis=-1)
        attn_out = jnp.einsum('bqk,bkd->bqd', attn, V)
        return attn_out @ w_o.T + b_o

    def _L0_ffn_ref(x, norm_scale, w_router, w_up, w_down):
        import jax, jax.numpy as jnp
        import numpy as np
        EPS = 1e-06
        TOP_K = 2

        def rms_norm(x, scale, eps=EPS):
            xf = x.astype(jnp.float32)
            mean_sq = jnp.mean(xf * xf, axis=-1, keepdims=True)
            return (xf * (scale.astype(jnp.float32) * jax.lax.rsqrt(mean_sq + eps))).astype(x.dtype)
        skip = x
        xn = rms_norm(x, norm_scale)
        scores = jnp.einsum('bsd,ed->bse', xn, w_router)
        _, ids = jax.lax.top_k(scores, TOP_K)
        probs = jax.nn.softmax(scores, axis=-1)
        c = jnp.take_along_axis(probs, ids, axis=-1)
        h = jnp.einsum('bsd,ehd->bseh', xn, w_up)
        val, gate = jnp.split(h, 2, axis=-1)
        h = val * jax.nn.silu(gate)
        y = jnp.einsum('bseh,edh->bsed', h, w_down)
        yk = jnp.take_along_axis(y, ids[..., None], axis=2)
        out = jnp.sum(yk * c[..., None], axis=2)
        return out + skip

    def _L1_attn_ref(x, in_proj_w, conv_w, conv_b, x_proj_w, dt_proj_w, dt_proj_b, A_log, D, out_proj_w, norm_w):
        import jax, jax.numpy as jnp
        import numpy as np
        D_MODEL = 128
        D_INNER = 256
        D_STATE = 16
        DT_RANK = 64
        D_CONV = 4
        EPS = 1e-05
        B_SZ, L = (2, 256)

        def _silu(x):
            return x * jax.nn.sigmoid(x)
        b, l, d = x.shape
        xn = x * jax.lax.rsqrt(jnp.mean(x * x, axis=-1, keepdims=True) + EPS) * norm_w
        x_and_res = xn @ in_proj_w
        xi, res = jnp.split(x_and_res, 2, axis=-1)
        xc = jax.lax.conv_general_dilated(xi.transpose(0, 2, 1), conv_w, window_strides=(1,), padding=[(D_CONV - 1, 0)], feature_group_count=D_INNER, dimension_numbers=('NCH', 'OIH', 'NCH')) + conv_b[None, :, None]
        xi = _silu(xc.transpose(0, 2, 1))
        x_dbl = xi @ x_proj_w
        delta, Bm, Cm = jnp.split(x_dbl, [DT_RANK, DT_RANK + D_STATE], axis=-1)
        delta = jax.nn.softplus(delta @ dt_proj_w + dt_proj_b)
        A = -jnp.exp(A_log)
        deltaA = jnp.exp(delta[..., None] * A)
        deltaB_u = delta[..., None] * Bm[:, :, None, :] * xi[..., None]

        def step(state, inputs):
            dA_t, dBu_t, C_t = inputs
            state = dA_t * state + dBu_t
            y_t = jnp.einsum('bdn,bn->bd', state, C_t)
            return (state, y_t)
        state0 = jnp.zeros((b, D_INNER, D_STATE), xi.dtype)
        _, ys = jax.lax.scan(step, state0, (deltaA.transpose(1, 0, 2, 3), deltaB_u.transpose(1, 0, 2, 3), Cm.transpose(1, 0, 2)))
        y = ys.transpose(1, 0, 2) + xi * D
        y = y * _silu(res)
        out = y @ out_proj_w + x
        return out

    def _L1_ffn_ref(x, gate_w, gate_b, w1, b1, w3, b3, w2, b2, sw1, sb1, sw3, sb3, sw2, sb2):
        import jax, jax.numpy as jnp
        import numpy as np
        from jax import lax
        D = 128
        H = 176
        E = 8
        K = 2
        ROUTER_SCALE = 1.0

        def _expert(x, w1, b1, w3, b3, w2, b2):
            h = jax.nn.silu((x @ w1 + b1) * (x @ w3 + b3))
            return h @ w2 + b2
        shape = x.shape
        xf = x.reshape(-1, D)
        T = xf.shape[0]
        scores = jax.nn.softmax(xf @ gate_w.T, axis=-1)
        biased = scores + gate_b
        _, idx = lax.top_k(biased, K)
        w = jnp.take_along_axis(scores, idx, axis=-1) * ROUTER_SCALE
        rw = jnp.zeros((T, E), dtype=xf.dtype).at[jnp.arange(T)[:, None], idx].add(w)
        h = jax.nn.silu((jnp.einsum('td,edh->teh', xf, w1) + b1) * (jnp.einsum('td,edh->teh', xf, w3) + b3))
        oe = jnp.einsum('teh,ehd->ted', h, w2) + b2
        y = jnp.einsum('te,ted->td', rw, oe)
        z = _expert(xf, sw1, sb1, sw3, sb3, sw2, sb2)
        return (y + z).reshape(shape)
    x = L0_attn_x
    x = x + _L0_attn_ref(_layernorm(x, axis=-1), L0_attn_w_qkv, L0_attn_b_qkv, L0_attn_w_o, L0_attn_b_o, L0_attn_w_iq, L0_attn_b_iq, L0_attn_w_ik, L0_attn_b_ik, L0_attn_w_iw, L0_attn_b_iw)
    x = x + _L0_ffn_ref(_layernorm(x, axis=-1), L0_ffn_norm_scale, L0_ffn_w_router, L0_ffn_w_up, L0_ffn_w_down)
    x = x + _L1_attn_ref(_layernorm(x, axis=-1), L1_attn_in_proj_w, L1_attn_conv_w, L1_attn_conv_b, L1_attn_x_proj_w, L1_attn_dt_proj_w, L1_attn_dt_proj_b, L1_attn_A_log, L1_attn_D, L1_attn_out_proj_w, L1_attn_norm_w)
    x = x + _L1_ffn_ref(_layernorm(x, axis=-1), L1_ffn_gate_w, L1_ffn_gate_b, L1_ffn_w1, L1_ffn_b1, L1_ffn_w3, L1_ffn_b3, L1_ffn_w2, L1_ffn_b2, L1_ffn_sw1, L1_ffn_sb1, L1_ffn_sw3, L1_ffn_sb3, L1_ffn_sw2, L1_ffn_sb2)
    return x

_drawn_inputs = setup_inputs


def setup_inputs(seed=0):
    import zlib

    import numpy as np

    out = dict(_drawn_inputs(seed))
    spreads = {'L0_attn_b_qkv': (0.0, 0.308),
     'L0_attn_b_o': (0.0, 0.1),
     'L0_attn_b_iq': (0.0, 0.8),
     'L0_attn_b_ik': (0.0, 0.8),
     'L0_attn_b_iw': (0.0, 0.8),
     'L0_ffn_norm_scale': (1.0, 0.6),
     'L1_attn_conv_b': (0.0, 0.8),
     'L1_attn_D': (1.0, 0.6),
     'L1_attn_norm_w': (1.0, 0.6)}
    factors = {'L0_attn_w_qkv': 4.921,
     'L0_attn_w_iq': 5.297,
     'L0_attn_w_ik': 5.044,
     'L0_attn_w_iw': 5.963,
     'L0_ffn_w_router': 8.0,
     'L0_ffn_w_up': 8.0,
     'L0_ffn_w_down': 8.0,
     'L1_attn_in_proj_w': 8.0,
     'L1_attn_conv_w': 8.0,
     'L1_attn_x_proj_w': 8.0,
     'L1_attn_dt_proj_w': 8.0,
     'L1_attn_dt_proj_b': 8.0,
     'L1_attn_A_log': 8.0,
     'L1_attn_out_proj_w': 8.0,
     'L1_ffn_gate_w': 24.69,
     'L1_ffn_gate_b': 182.869,
     'L1_ffn_w1': 31.11,
     'L1_ffn_b1': 200.0,
     'L1_ffn_w3': 31.374,
     'L1_ffn_b3': 200.0,
     'L1_ffn_w2': 22.958,
     'L1_ffn_b2': 200.0,
     'L1_ffn_sw1': 8.0,
     'L1_ffn_sb1': 64.0,
     'L1_ffn_sw3': 8.0,
     'L1_ffn_sb3': 64.0,
     'L1_ffn_sw2': 8.0,
     'L1_ffn_sb2': 200.0}
    for name, (base, spread) in spreads.items():
        noise = np.random.default_rng([zlib.crc32(name.encode()), seed]).standard_normal(out[name].shape)
        drawn = base * np.exp(spread * noise) if base else spread * noise
        out[name] = jnp.asarray(drawn.astype(out[name].dtype))
    for name, factor in factors.items():
        out[name] = (out[name] * factor).astype(out[name].dtype)
    return out
```

```python
import math
from contextlib import ExitStack

import numpy as np
import concourse.bass as bass
from concourse import mybir

F32 = mybir.dt.float32
BF16 = mybir.dt.bfloat16
I32 = mybir.dt.int32
ALU = mybir.AluOpType
ACT = mybir.ActivationFunctionType
AX = mybir.AxisListType

B, S, D = 16, 256, 128
P = 128
T = B * S // P
TOPK = 32
IH, ID = 4, 64
E = 8
H0, H1 = 352, 176
NT = 2 * B * S // P + E
DI, N, DT = 256, 16, 64
BIG = 3.0e38
ds = bass.ds


class Signal:

    def __init__(self, sem, per):
        self.sem, self.per = sem, per

    def after(self, unit, k=None):
        return unit * self.per + (self.per if k is None else k)


class Chain:

    def __init__(self, eng, sem):
        self.eng, self.sem, self.n = eng, sem, 0

    def __call__(self, ins):
        ins.then_inc(self.sem, 1)
        self.n += 1
        self.eng.wait_ge(self.sem, self.n)


class Maker:
    def __init__(self, nc, ctx, tag):
        self.nc, self.ctx, self.tag = nc, ctx, tag

    def sb(self, name, shape, dt=F32):
        return self.ctx.enter_context(self.nc.sbuf_tensor(self.tag + name, shape, dt))

    def ps(self, name, shape, dt=F32):
        return self.ctx.enter_context(self.nc.psum_tensor(self.tag + name, shape, dt))

    def sem(self, name):
        return self.ctx.enter_context(self.nc.semaphore(self.tag + name))

    def sig(self, name, per=1):
        return Signal(self.sem(name), per)


def load(nc, tag, pairs):
    with ExitStack() as ctx:
        arrived = Maker(nc, ctx, tag).sem("arrived")
        with nc.Block() as block:
            @block.sync
            def _(sp):
                for dst, src in pairs:
                    sp.dma_start(dst, src).then_inc(arrived, 16)
                sp.wait_ge(arrived, 16 * len(pairs))


def row_stats(nc, tag, X, mean, rstd, rms, eps2):
    with ExitStack() as ctx:
        m = Maker(nc, ctx, tag)
        st = m.sb("st", [P, T, 6])
        mv = m.sb("mv", [P, T, 2])
        ve, t1, t2 = m.sb("ve", [P, T]), m.sb("t1", [P, T]), m.sb("t2", [P, T])
        chain, shifted, rooted = m.sem("chain"), m.sig("shifted"), m.sig("rooted")
        rounds = [(1e-5, rstd)] + ([(eps2, rms)] if rms is not None else [])
        with nc.Block() as block:
            @block.vector
            def _(dve):
                link = Chain(dve, chain)
                for t in range(T):
                    ins = nc.vector.bn_stats(st[:, t, :], X[:, t * D:(t + 1) * D])
                link(ins)
                for t in range(T):
                    ins = nc.vector.bn_aggr(mv[:, t, :], st[:, t, :])
                link(ins)
                link(nc.vector.tensor_copy(mean[:], mv[:, :, 0]))
                var = mv[:, :, 1]
                for k, (eps, out) in enumerate(rounds):
                    if k == 1:
                        link(nc.vector.tensor_tensor(t1[:], rstd[:], rstd[:], ALU.mult))
                        link(nc.vector.tensor_tensor(t1[:], t1[:], var, ALU.mult))
                        var = t1[:]
                    nc.vector.tensor_scalar(ve[:], var, eps, None, ALU.add).then_inc(shifted.sem, 1)
                    dve.wait_ge(rooted.sem, k + 1)
                    link(nc.vector.reciprocal(out[:], t2[:]))
                    link(nc.vector.tensor_tensor(t2[:], out[:], out[:], ALU.mult))
                    link(nc.vector.tensor_tensor(t2[:], t2[:], ve[:], ALU.mult))
                    link(nc.vector.tensor_scalar(t2[:], t2[:], -0.5, 1.5, ALU.mult, ALU.add))
                    link(nc.vector.tensor_tensor(out[:], out[:], t2[:], ALU.mult))
                if rms is not None:
                    link(nc.vector.tensor_tensor(rms[:], rms[:], rstd[:], ALU.mult))

            @block.scalar
            def _(act):
                for k in range(len(rounds)):
                    act.wait_ge(shifted.sem, k + 1)
                    nc.scalar.activation(t2[:], ve[:], ACT.Sqrt).then_inc(rooted.sem, 1)


def attention(nc, X, mean, rstd, ident, w, bias, b_iw, rope):
    with ExitStack() as ctx:
        m = Maker(nc, ctx, "at_")
        W2 = 2 * P
        Xn = [m.sb(f"Xn{v}", [P, W2]) for v in range(2)]
        xT = [m.sb(f"xT{v}", [P, W2]) for v in range(2)]
        RP = [m.sb(f"RP{v}", [P, 4 * S]) for v in range(2)]
        QK = [m.sb(f"QK{v}", [P, 2 * S]) for v in range(2)]
        IQ = [m.sb(f"IQ{v}", [P, 2 * S]) for v in range(2)]
        IKV = [m.sb(f"IKV{v}", [P, 2 * S]) for v in range(2)]
        VO = [m.sb(f"VO{v}", [P, 2 * D]) for v in range(2)]
        IW = [m.sb(f"IW{v}", [P, 2, IH]) for v in range(2)]
        R = [m.sb(f"R{t}", [P, IH * S]) for t in range(2)]
        WK = [m.sb(f"WK{v}", [P, 2 * S]) for v in range(2)]
        MK = [m.sb(f"MK{v}", [P, 2 * S]) for v in range(2)]
        PR = [m.sb(f"PR{v}", [P, 2 * S]) for v in range(2)]
        PT = [m.sb(f"PT{v}", [P, 2 * S]) for v in range(2)]
        M8 = m.sb("M8", [P, 2, 8])
        mx = [m.sb(f"mx{v}", [P, 2]) for v in range(2)]
        rsum = [m.sb(f"rsum{v}", [P, 2]) for v in range(2)]
        rinv = [m.sb(f"rinv{v}", [P, 2]) for v in range(2)]
        bank = [m.ps(f"b{k}", [P, 512]) for k in range(5)]
        SC0 = m.ps("SC0", [P, 1024])
        LG = m.ps("LG", [P, 512])
        b0, b12a, b12b, b3, b4 = bank
        scale = float(1.0 / np.sqrt(np.float32(D)))

        xn_ready = m.sig("xn_ready", 2)
        xT_ready = m.sig("xT_ready")
        xT_copied = m.sig("xT_copied")
        qk_ready = m.sig("qk_ready")
        iq_ready = m.sig("iq_ready")
        ikv_ready = m.sig("ikv_ready")
        rope_parts = m.sig("rope_parts", 4)
        qk_sum = m.sig("qk_sum")
        iq_copied = m.sig("iq_copied", 2)
        ikv_copied = m.sig("ikv_copied", 2)
        vo_ready = m.sig("vo_ready")
        vo_copied = m.sig("vo_copied")
        iw_copied = m.sig("iw_copied")
        scores_ready = m.sig("scores_ready", 2)
        relu_ready = m.sig("relu_ready", 2)
        logits_ready = m.sig("logits_ready")
        idx = m.sig("idx", 8)
        topk = m.sig("topk", 16)
        penalty = m.sig("penalty")
        masked = m.sig("masked", 2)
        negmax = m.sig("negmax")
        probs_ready = m.sig("probs_ready", 2)
        rinv_ready = m.sig("rinv_ready")
        pT_ready = m.sig("pT_ready")
        pT_copied = m.sig("pT_copied")
        av_ready = m.sig("av_ready")
        x_updated = m.sig("x_updated", 2)
        passed = m.sem("passed")

        def steps(eng, step):
            step(0, 0, True, False, False)
            step(1, 1, True, True, False)
            with eng.Fori(0, B // 2 - 1) as i:
                step(2 * i + 2, 0, True, True, True)
                step(2 * i + 3, 1, True, True, True)
            step(B, 0, False, True, True)
            step(B + 1, 1, False, False, True)

        def col(k):
            return w[:, k * P:(k + 1) * P]

        with nc.Block() as block:
            @block.tensor
            def _(pe):
                def step(s, v, front, middle, tail):
                    first = isinstance(s, int)
                    if front:
                        pe.wait_ge(xn_ready.sem, xn_ready.after(s))
                        if not (first and s < 1):
                            pe.wait_ge(iw_copied.sem, iw_copied.after(s - 1))
                        for t in range(2):
                            ins = nc.tensor.transpose(b0[:, t * P:(t + 1) * P], Xn[v][:, t * P:(t + 1) * P], ident[:])
                        ins.then_inc(xT_ready.sem, 1)
                        pe.wait_ge(xT_copied.sem, xT_copied.after(s))
                        if not (first and s < 1):
                            pe.wait_ge(relu_ready.sem, relu_ready.after(s - 1, 2))
                        for k in range(4):
                            dst = (b12a, b12b)[k // 2][:, k % 2 * S:(k % 2 + 1) * S]
                            ins = nc.tensor.matmul(dst, col(k), xT[v][:], start=True, stop=True)
                        ins.then_inc(qk_ready.sem, 1)
                        if not (first and s < 2):
                            pe.wait_ge(pT_copied.sem, pT_copied.after(s - 2))
                        for k in range(2):
                            ins = nc.tensor.matmul(b3[:, k * S:(k + 1) * S], col(4 + k), xT[v][:], start=True, stop=True)
                        ins.then_inc(iq_ready.sem, 1)
                        for k in range(2):
                            ins = nc.tensor.matmul(b0[:, k * S:(k + 1) * S], col(6 + k), xT[v][:], start=True, stop=True)
                        ins.then_inc(ikv_ready.sem, 1)
                        pe.wait_ge(ikv_copied.sem, ikv_copied.after(s))
                        for t in range(2):
                            nc.tensor.matmul(b0[:, t * D:(t + 1) * D], IKV[v][:, S + t * P:S + (t + 1) * P],
                                             w[:, 8 * P + IH:9 * P + IH], start=True, stop=True)
                        for t in range(2):
                            ins = nc.tensor.matmul(b0[:, W2 + t * IH:W2 + (t + 1) * IH], xT[v][:, t * P:(t + 1) * P],
                                                   w[:, 8 * P:8 * P + IH], start=True, stop=True)
                        ins.then_inc(vo_ready.sem, 1)
                        pe.wait_ge(iq_copied.sem, iq_copied.after(s))
                        for t in range(2):
                            if t == 0:
                                if not (first and s < 1):
                                    pe.wait_ge(relu_ready.sem, relu_ready.after(s - 1, 1))
                            else:
                                pe.wait_ge(rope_parts.sem, rope_parts.after(s))
                            for h in range(IH):
                                r, c = h % 2 * ID, h // 2 * S
                                dst = SC0[:, h % 2 * 512 + c:h % 2 * 512 + c + S] if t == 0 else (b12a, b12b)[h % 2][:, c:c + S]
                                ins = nc.tensor.matmul(dst, IQ[v][r:r + ID, h // 2 * S + t * P:h // 2 * S + (t + 1) * P],
                                                       IKV[v][r:r + ID, 0:S], start=True, stop=True)
                            ins.then_inc(scores_ready.sem, 1)
                        pe.wait_ge(qk_sum.sem, qk_sum.after(s))
                        if not (first and s < 1):
                            pe.wait_ge(masked.sem, masked.after(s - 1))
                        for t in range(2):
                            ins = nc.tensor.matmul(LG[:, t * S:(t + 1) * S], QK[v][:, t * P:(t + 1) * P],
                                                   QK[v][:, S:2 * S], start=True, stop=True)
                        ins.then_inc(logits_ready.sem, 1)
                    if middle:
                        u = 1 - v
                        if front:
                            pe.wait_ge(iq_copied.sem, iq_copied.after(s))
                        for t in range(2):
                            pe.wait_ge(probs_ready.sem, probs_ready.after(s - 1, t + 1))
                            for c in range(2):
                                ins = nc.tensor.transpose(b3[:, c * S + t * P:c * S + (t + 1) * P],
                                                          PR[u][:, t * S + c * P:t * S + (c + 1) * P], ident[:])
                        ins.then_inc(pT_ready.sem, 1)
                        pe.wait_ge(pT_copied.sem, pT_copied.after(s - 1))
                        if not (first and s < 2):
                            pe.wait_ge(x_updated.sem, x_updated.after(s - 2))
                        for t in range(2):
                            for c in range(2):
                                ins = nc.tensor.matmul(b4[:, t * D:(t + 1) * D], PT[u][:, c * S + t * P:c * S + (t + 1) * P],
                                                       VO[u][:, c * D:(c + 1) * D], start=c == 0, stop=c == 1)
                        ins.then_inc(av_ready.sem, 1)

                steps(pe, step)

            @block.scalar
            def _(act):
                def step(s, v, front, middle, tail):
                    first = isinstance(s, int)
                    if front:
                        act.wait_ge(xT_ready.sem, xT_ready.after(s))
                        nc.scalar.activation(xT[v][:], b0[:, 0:W2], ACT.Copy).then_inc(xT_copied.sem, 1)
                        act.wait_ge(iq_ready.sem, iq_ready.after(s))
                        for k in range(2):
                            nc.scalar.activation(IQ[v][:, k * S:(k + 1) * S], b3[:, k * S:(k + 1) * S], ACT.Identity,
                                                 bias=bias[:, 4 + k:5 + k]).then_inc(iq_copied.sem, 1)
                        act.wait_ge(ikv_ready.sem, ikv_ready.after(s))
                        for k in range(2):
                            nc.scalar.activation(IKV[v][:, k * S:(k + 1) * S], b0[:, k * S:(k + 1) * S], ACT.Identity,
                                                 bias=bias[:, 6 + k:7 + k]).then_inc(ikv_copied.sem, 1)
                        act.wait_ge(vo_ready.sem, vo_ready.after(s))
                        nc.scalar.activation(VO[v][:], b0[:, 0:W2], ACT.Copy).then_inc(vo_copied.sem, 1)
                        for t in range(2):
                            act.wait_ge(scores_ready.sem, scores_ready.after(s, t + 1))
                            if not (first and s < 1):
                                act.wait_ge(idx.sem, idx.after(s - 1, 7 + t))
                            if t == 0:
                                nc.scalar.activation(R[t][:], SC0[:], ACT.Relu).then_inc(relu_ready.sem, 1)
                            else:
                                nc.scalar.activation(R[t][:, 0:512], b12a[:], ACT.Relu)
                                nc.scalar.activation(R[t][:, 512:1024], b12b[:], ACT.Relu).then_inc(relu_ready.sem, 1)
                    if middle:
                        u = 1 - v
                        act.wait_ge(negmax.sem, negmax.after(s - 1))
                        for t in range(2):
                            nc.scalar.activation(PR[u][:, t * S:(t + 1) * S], MK[u][:, t * S:(t + 1) * S], ACT.Exp,
                                                 bias=mx[u][:, t:t + 1], scale=scale,
                                                 accum_out=rsum[u][:, t:t + 1]).then_inc(probs_ready.sem, 1)
                        act.wait_ge(pT_ready.sem, pT_ready.after(s - 1))
                        nc.scalar.activation(PT[u][:], b3[:], ACT.Copy).then_inc(pT_copied.sem, 1)

                steps(act, step)

            @block.vector
            def _(dve):
                def normalise(s, v):
                    for t in range(2):
                        nc.vector.tensor_scalar(Xn[v][:, t * D:(t + 1) * D], X[:, ds(s * W2 + t * D, D)],
                                                mean[:, ds(s * 2 + t, 1)], rstd[:, ds(s * 2 + t, 1)],
                                                ALU.subtract, ALU.mult).then_inc(xn_ready.sem, 1)

                def rotate(s, v):
                    dve.wait_ge(qk_ready.sem, qk_ready.after(s))
                    for k in range(4):
                        nc.vector.scalar_tensor_tensor(RP[v][:, k * S:(k + 1) * S],
                                                       (b12a, b12b)[k // 2][:, k % 2 * S:(k % 2 + 1) * S],
                                                       bias[:, k:k + 1], rope[:, k // 2 * S:(k // 2 + 1) * S],
                                                       ALU.add, ALU.mult).then_inc(rope_parts.sem, 1)

                def head_weights(s, v):
                    dve.wait_ge(vo_copied.sem, vo_copied.after(s))
                    nc.vector.tensor_tensor(IW[v][:], b0[:, W2:W2 + 2 * IH].rearrange("p (t h) -> p t h", h=IH),
                                            b_iw[:, :].unsqueeze(1).to_broadcast([P, 2, IH]), ALU.add).then_inc(iw_copied.sem, 1)

                def index_scores(s, v):
                    dve.wait_ge(iw_copied.sem, iw_copied.after(s))
                    for h in range(IH):
                        for t in range(2):
                            dst = WK[v][:, t * S:(t + 1) * S]
                            src = R[t][:, h % 2 * 512 + h // 2 * S:h % 2 * 512 + (h // 2 + 1) * S]
                            if h == 0:
                                dve.wait_ge(relu_ready.sem, relu_ready.after(s, t + 1))
                                ins = nc.vector.tensor_scalar(dst, src, IW[v][:, t, h:h + 1], None, ALU.mult)
                            else:
                                dve.wait_ge(idx.sem, idx.after(s, 2 * h - 1 + t))
                                ins = nc.vector.scalar_tensor_tensor(dst, src, IW[v][:, t, h:h + 1], dst, ALU.mult, ALU.add)
                            ins.then_inc(idx.sem, 1)

                def choose(s, v, rounds):
                    for k in rounds:
                        for t in range(2):
                            dst = WK[v][:, t * S:(t + 1) * S]
                            if k == 0:
                                dve.wait_ge(idx.sem, idx.after(s, 7 + t))
                                dve.sem_inc(passed, 1)
                            else:
                                dve.wait_ge(topk.sem, topk.after(s, 4 * k - 1 + t))
                                dve.sem_inc(passed, 1)
                            nc.vector.max(M8[:, t, :], dst).then_inc(topk.sem, 1)
                        for t in range(2):
                            dst = WK[v][:, t * S:(t + 1) * S]
                            dve.wait_ge(topk.sem, topk.after(s, 4 * k + 1 + t))
                            dve.sem_inc(passed, 1)
                            nc.vector.match_replace(dst, M8[:, t, :], dst, -BIG).then_inc(topk.sem, 1)

                def mask(s, v):
                    dve.wait_ge(topk.sem, topk.after(s))
                    nc.vector.tensor_scalar(WK[v][:], WK[v][:], -BIG, -BIG, ALU.is_gt, ALU.mult).then_inc(penalty.sem, 1)
                    dve.wait_ge(penalty.sem, penalty.after(s))
                    dve.wait_ge(logits_ready.sem, logits_ready.after(s))
                    dve.sem_inc(passed, 1)
                    for t in range(2):
                        c = slice(t * S, (t + 1) * S)
                        nc.vector.tensor_tensor_reduce(MK[v][:, c], WK[v][:, c], LG[:, c], 1.0, -BIG, ALU.add, ALU.max,
                                                       accum_out=mx[v][:, t:t + 1]).then_inc(masked.sem, 1)
                    dve.wait_ge(masked.sem, masked.after(s))
                    nc.vector.tensor_scalar(mx[v][:], mx[v][:], -scale, None, ALU.mult).then_inc(negmax.sem, 1)

                def update(s, v):
                    dve.wait_ge(probs_ready.sem, probs_ready.after(s))
                    nc.vector.reciprocal(rinv[v][:], rsum[v][:]).then_inc(rinv_ready.sem, 1)
                    dve.wait_ge(rinv_ready.sem, rinv_ready.after(s))
                    dve.wait_ge(av_ready.sem, av_ready.after(s))
                    for t in range(2):
                        x = X[:, ds(s * W2 + t * D, D)]
                        nc.vector.scalar_tensor_tensor(x, b4[:, t * D:(t + 1) * D], rinv[v][:, t:t + 1], x,
                                                       ALU.mult, ALU.add).then_inc(x_updated.sem, 1)

                def step(s, v, front, middle, tail):
                    u = 1 - v
                    if front:
                        normalise(s, v)
                    if middle:
                        index_scores(s - 1, u)
                        choose(s - 1, u, range(0, 2))
                    if front:
                        rotate(s, v)
                        head_weights(s, v)
                    if middle:
                        choose(s - 1, u, range(2, TOPK // 8))
                        mask(s - 1, u)
                    if tail:
                        update(s - 2, v)

                steps(dve, step)

            @block.gpsimd
            def _(pool):
                def step(s, v, front, middle, tail):
                    if front:
                        pool.wait_ge(rope_parts.sem, rope_parts.after(s))
                        nc.gpsimd.tensor_tensor(QK[v][:], RP[v][:, 0:2 * S], RP[v][:, 2 * S:4 * S], ALU.add).then_inc(qk_sum.sem, 1)

                steps(pool, step)


class Routing:

    def __init__(self, m):
        self.c = [m.sb(f"c{k}", [P, T]) for k in range(2)]
        self.slot = [m.sb(f"slot{k}", [P, T], I32) for k in range(2)]
        self.tile_expert = m.sb("tile_expert", [1, NT], I32)


def route(nc, tag, LGT, gate_b, rt, tri, ones, rev, start128, row_of_tile):
    with ExitStack() as ctx:
        m = Maker(nc, ctx, tag)
        shape = [P, T, E]
        ex, pr, eq = m.sb("ex", shape), m.sb("pr", shape), m.sb("eq", shape)
        oh = [m.sb(f"oh{k}", shape) for k in range(2)]
        mt = m.sb("mt", shape, BF16)
        scan = [m.sb(f"scan{k}", shape) for k in range(2)]
        tot = m.sb("tot", shape)
        mx, sm = m.sb("mx", [P, T]), m.sb("sm", [P, T])
        n_i, ct, end, st128 = m.sb("n_i", [P, E], I32), m.sb("ct", [P, E]), m.sb("end", [P, E]), m.sb("st128", [P, E])
        one8 = m.sb("one8", [P, E])
        cmp = m.sb("cmp", [1, NT, E])
        te = m.sb("te", [1, NT])
        RK = m.ps("RK", [P, T * E])
        TT = m.ps("TT", [P, T * E])
        chain, shifted, powered, marks, ranked = (m.sem("chain"), m.sem("shifted"), m.sem("powered"),
                                                  m.sem("marks"), m.sem("ranked"))

        def each(a):
            return a[:, :].unsqueeze(2).to_broadcast(shape)

        def every(a):
            return a[:, :].unsqueeze(1).to_broadcast(shape)

        with nc.Block() as block:
            @block.vector
            def _(dve):
                v = nc.vector
                link = Chain(dve, chain)
                link(v.tensor_reduce(mx[:], LGT[:], AX.X, ALU.max))
                v.tensor_tensor(ex[:], LGT[:], each(mx), ALU.subtract).then_inc(shifted, 1)
                dve.wait_ge(powered, 1)
                link(v.tensor_reduce(sm[:], ex[:], AX.X, ALU.add))
                link(v.reciprocal(sm[:], sm[:]))
                link(v.tensor_tensor(pr[:], ex[:], each(sm), ALU.mult))
                key = LGT
                if gate_b is not None:
                    link(v.tensor_tensor(ex[:], pr[:], every(gate_b), ALU.add))
                    key = ex
                for k in range(2):
                    link(v.tensor_reduce(mx[:], key[:], AX.X, ALU.max))
                    link(v.tensor_tensor(eq[:], key[:], each(mx), ALU.is_equal))
                    link(v.tensor_tensor(eq[:], eq[:], every(rev), ALU.mult))
                    link(v.tensor_reduce(mx[:], eq[:], AX.X, ALU.max))
                    link(v.tensor_tensor(oh[k][:], eq[:], each(mx), ALU.is_equal))
                    link(v.tensor_tensor(eq[:], pr[:], oh[k][:], ALU.mult))
                    link(v.tensor_reduce(rt.c[k][:], eq[:], AX.X, ALU.add))
                    if k == 0:
                        link(v.scalar_tensor_tensor(ex[:], oh[0][:], -BIG, key[:], ALU.mult, ALU.add))
                        key = ex
                v.tensor_tensor(mt[:], oh[0][:], oh[1][:], ALU.add).then_inc(marks, 1)
                dve.wait_ge(ranked, 1)
                nc.vector.tensor_copy(tot[:], TT[:].rearrange("p (t e) -> p t e", e=E))
                link(nc.vector.tensor_copy(scan[0][:], TT[:].rearrange("p (t e) -> p t e", e=E)))
                a, b, k = scan[0], scan[1], 1
                while k < T:
                    v.tensor_copy(b[:, 0:k, :], a[:, 0:k, :])
                    link(v.tensor_tensor(b[:, k:T, :], a[:, k:T, :], a[:, 0:T - k, :], ALU.add))
                    a, b, k = b, a, 2 * k
                link(v.tensor_scalar(n_i[:], a[:, T - 1, :], float(P - 1), None, ALU.add))
                link(v.tensor_scalar(n_i[:], n_i[:], int(math.log2(P)), None, ALU.arith_shift_right))
                link(v.tensor_copy(ct[:], n_i[:]))
                link(v.memset(one8[:], 1.0))
                link(v.tensor_tensor_scan(end[:], one8[:], ct[:], 0.0, ALU.mult, ALU.add))
                link(v.tensor_tensor(st128[:], end[:], ct[:], ALU.subtract))
                link(v.tensor_scalar(st128[:], st128[:], float(P), None, ALU.mult))
                link(v.tensor_tensor(b[:], a[:], tot[:], ALU.subtract))
                link(v.tensor_tensor(b[:], b[:], RK[:].rearrange("p (t e) -> p t e", e=E), ALU.add))
                link(v.tensor_tensor(b[:], b[:], every(st128), ALU.add))
                for k in range(2):
                    link(v.tensor_tensor(eq[:], oh[k][:], b[:], ALU.mult))
                    link(v.tensor_reduce(mx[:], eq[:], AX.X, ALU.add))
                    link(v.tensor_copy(rt.slot[k][:], mx[:]))
                link(v.tensor_tensor(cmp[:], end[0:1, :].unsqueeze(1).to_broadcast([1, NT, E]),
                                     row_of_tile[:, :].unsqueeze(2).to_broadcast([1, NT, E]), ALU.is_le))
                link(v.tensor_reduce(te[:], cmp[:], AX.X, ALU.add))
                link(v.tensor_scalar(rt.tile_expert[:], te[:], float(E - 1), None, ALU.min))

            @block.scalar
            def _(act):
                act.wait_ge(shifted, 1)
                nc.scalar.activation(ex[:], ex[:], ACT.Exp).then_inc(powered, 1)

            @block.tensor
            def _(pe):
                pe.wait_ge(marks, 1)
                flat = mt[:].rearrange("p t e -> p (t e)")
                nc.tensor.matmul(RK[:], tri[:], flat, start=True, stop=True)
                nc.tensor.matmul(TT[:], ones[:], flat, start=True, stop=True).then_inc(ranked, 1)


def router(nc, tag, X, XL, XS, add_skip, mean, rstd, rms, scale_col, w_router, ident, LGT):
    G = 4
    with ExitStack() as ctx:
        m = Maker(nc, ctx, tag)
        xT = [m.sb(f"xT{v}", [P, G * P]) for v in range(2)]
        TP = [m.ps(f"TP{v}", [P, G * P]) for v in range(2)]
        RP = [m.ps(f"RP{v}", [P, G * E]) for v in range(2)]
        rows = m.sig("rows", 2 * G)
        added = m.sig("added")
        turned = m.sig("turned")
        copied = m.sig("copied")
        scored = m.sig("scored")
        kept = m.sig("kept")
        staged = m.sig("staged")
        ST = [m.sb(f"ST{v}", [P, G * P]) for v in range(2)]
        GN = T // G

        with nc.Block() as block:
            @block.vector
            def _(dve):
                def keep(g, v):
                    dve.wait_ge(scored.sem, scored.after(g))
                    nc.vector.tensor_copy(LGT[:, ds(g * G, G), :], RP[v][:].rearrange("p (t e) -> p t e", e=E)).then_inc(kept.sem, 1)

                def rows_of(g):
                    for t in range(G):
                        x = X[:, ds((g * G + t) * D, D)]
                        st = ds(g * G + t, 1)
                        nc.vector.tensor_scalar(XL[:, ds((g * G + t) * D, D)], x, mean[:, st], rstd[:, st],
                                                ALU.subtract, ALU.mult).then_inc(rows.sem, 1)
                        nc.vector.tensor_scalar(XS[:, ds((g * G + t) * D, D)], x, mean[:, st], (rms if rms is not None else rstd)[:, st],
                                                ALU.subtract, ALU.mult).then_inc(rows.sem, 1)

                rows_of(0)
                rows_of(1)
                with dve.Fori(0, (GN - 2) // 2) as i:
                    for v in range(2):
                        keep(2 * i + v, v)
                        rows_of(2 * i + 2 + v)
                for v in range(2):
                    keep(GN - 2 + v, v)

            @block.gpsimd
            def _(pool):
                if add_skip:
                    with pool.Fori(0, GN) as g:
                        pool.wait_ge(rows.sem, rows.after(g))
                        x = X[:, ds(g * G * D, G * D)]
                        nc.gpsimd.tensor_tensor(x, x, XL[:, ds(g * G * D, G * D)], ALU.add).then_inc(added.sem, 1)

            @block.tensor
            def _(pe):
                def step(g, v, first):
                    pe.wait_ge(staged.sem, staged.after(g))
                    if not first:
                        pe.wait_ge(copied.sem, copied.after(g - 2))
                    for t in range(G):
                        ins = nc.tensor.transpose(TP[v][:, t * P:(t + 1) * P], ST[v][:, t * P:(t + 1) * P], ident[:])
                    ins.then_inc(turned.sem, 1)
                    pe.wait_ge(copied.sem, copied.after(g))
                    if not first:
                        pe.wait_ge(kept.sem, kept.after(g - 2))
                    for t in range(G):
                        ins = nc.tensor.matmul(RP[v][:, t * E:(t + 1) * E], xT[v][:, t * P:(t + 1) * P], w_router[:],
                                               start=True, stop=True)
                    ins.then_inc(scored.sem, 1)

                step(0, 0, True)
                step(1, 1, True)
                with pe.Fori(0, (GN - 2) // 2) as i:
                    for v in range(2):
                        step(2 * i + 2 + v, v, False)

            @block.scalar
            def _(act):
                def step(g, v, first):
                    act.wait_ge(rows.sem, rows.after(g))
                    if not first:
                        act.wait_ge(turned.sem, turned.after(g - 2))
                    nc.scalar.activation(ST[v][:], XS[:, ds(g * G * D, G * D)], ACT.Copy).then_inc(staged.sem, 1)
                    act.wait_ge(turned.sem, turned.after(g))
                    if not first:
                        act.wait_ge(scored.sem, scored.after(g - 2))
                    if scale_col is not None:
                        ins = nc.scalar.activation(xT[v][:], TP[v][:], ACT.Copy, scale=scale_col[:, 0:1])
                    else:
                        ins = nc.scalar.activation(xT[v][:], TP[v][:], ACT.Copy)
                    ins.then_inc(copied.sem, 1)

                step(0, 0, True)
                step(1, 1, True)
                with act.Fori(0, (GN - 2) // 2) as i:
                    for v in range(2):
                        step(2 * i + 2 + v, v, False)


def scatter_rows(nc, tag, XS, rt, XG):
    with ExitStack() as ctx:
        m = Maker(nc, ctx, tag)
        sent = m.sem("sent")
        with nc.Block() as block:
            @block.gpsimd
            def _(pool):
                for t in range(T):
                    for k in range(2):
                        nc.gpsimd.indirect_dma_start(XG, bass.IndirectOffsetOnAxis(rt.slot[k][:, t:t + 1], 0),
                                                     XS[:, t * D:(t + 1) * D], None).then_inc(sent, 16)
                pool.wait_ge(sent, 16 * 2 * T)


def combine(nc, tag, X, rt, Y, YS):
    DEEP = 4
    with ExitStack() as ctx:
        m = Maker(nc, ctx, tag)
        n = 3 if YS is not None else 2
        G = [[m.sb(f"G{v}_{k}", [P, D]) for k in range(n)] for v in range(DEEP)]
        got = [m.sem(f"got{v}") for v in range(DEEP)]
        used = m.sem("used")
        shared = [m.sem(f"shared{v}") for v in range(DEEP)]
        with nc.Block() as block:
            @block.gpsimd
            def _(pool):
                for t in range(T):
                    v = t % DEEP
                    if t >= DEEP:
                        pool.wait_ge(used, n * (t - DEEP + 1))
                    for k in range(2):
                        nc.gpsimd.indirect_dma_start(G[v][k][:], None, Y,
                                                     bass.IndirectOffsetOnAxis(rt.slot[k][:, t:t + 1], 0)).then_inc(got[v], 16)

            @block.sync
            def _(sp):
                if YS is not None:
                    for t in range(T):
                        v = t % DEEP
                        if t >= DEEP:
                            sp.wait_ge(used, n * (t - DEEP + 1))
                        sp.dma_start(G[v][2][:], YS[t * P:(t + 1) * P, :]).then_inc(shared[v], 16)

            @block.vector
            def _(dve):
                c = 0
                for t in range(T):
                    v = t % DEEP
                    dve.wait_ge(got[v], 32 * (t // DEEP + 1))
                    x = X[:, t * D:(t + 1) * D]
                    for k in range(n):
                        if k == 2:
                            dve.wait_ge(shared[v], 16 * (t // DEEP + 1))
                            ins = nc.vector.tensor_tensor(x, x, G[v][2][:], ALU.add)
                        else:
                            ins = nc.vector.scalar_tensor_tensor(x, G[v][k][:], rt.c[k][:, t:t + 1], x, ALU.mult, ALU.add)
                        ins.then_inc(used, 1)
                        c += 1
                        dve.wait_ge(used, c)


def experts(nc, tag, rt, XG, Y, n_shared, scale_col, w_up, w_down, H, gated, b_up, b_down, ident):
    NX = NT + n_shared
    chunks = [(c, min(P, H - c)) for c in range(0, H, P)]
    NC = len(chunks)
    WU = 2 * H
    WD = NC * D
    two = WU > 512
    U = 4
    LAG = 7

    class Tile:

        def __init__(self, j, v, shared, known):
            self.j, self.v, self.shared, self.known = j, v, shared, known

        def has(self, back):
            return self.known is None or self.known >= back

        def raised(self, back):
            if self.known is not None:
                return ((self.known - back) // U + 1) * 16
            return (self.j - back - self.v) * (16 // U) + 16

    with ExitStack() as ctx:
        m = Maker(nc, ctx, tag)
        G = [m.sb(f"G{v}", [P, D]) for v in range(U)]
        gT = [m.sb(f"gT{v}", [P, P]) for v in range(2)]
        hid = [m.sb(f"hid{v}", [P, H]) for v in range(2)]
        sg = [m.sb(f"sg{v}", [P, WU]) for v in range(2)]
        hT = [m.sb(f"hT{v}", [P, NC * P]) for v in range(2)]
        YO = [m.sb(f"YO{v}", [P, D]) for v in range(U)]
        UP = [m.ps(f"UP{v}", [P, 1024 if two else 512]) for v in range(2)]
        TP = m.ps("TP", [P, 512])
        HP = m.ps("HP", [P, 512])
        DP = m.ps("DP", [P, 512])
        arrived = [m.sem(f"arrived{v}") for v in range(U)]
        stored = [m.sem(f"stored{v}") for v in range(U)]
        turned = m.sig("turned")
        t_copied = m.sig("t_copied")
        up_ready = m.sig("up_ready")
        biased = m.sig("biased")
        multiplied = m.sig("multiplied")
        silu_ready = m.sig("silu_ready")
        h_ready = multiplied if gated else silu_ready
        h_turned = m.sig("h_turned")
        h_copied = m.sig("h_copied")
        down_ready = m.sig("down_ready")
        y_ready = m.sig("y_ready")
        up_cols = [(0, 0, H), (512, H, H)] if two else [(0, 0, WU)]
        up_free = multiplied if gated else biased

        def expert_of(eng, t):
            if t.shared:
                return E
            return eng.value_load(rt.tile_expert[0:1, ds(t.j, 1)], min_val=0, max_val=E - 1)

        with nc.Block() as block:
            def walk(eng, step):
                def known(s):
                    return lambda lag: Tile(s - lag, (s - lag) % U, s - lag >= NT, s - lag) if 0 <= s - lag < NX else None

                for s in range(U + LAG):
                    step(known(s))
                at = U + LAG
                for end in ([NT, NX] if n_shared else [NX]):
                    full = (end - at) // U
                    if full > 0:
                        with eng.Fori(0, full) as i:
                            for q in range(U):
                                step(lambda lag: Tile(at + i * U + (q - lag), (at + q - lag) % U, end > NT, None))
                        at += full * U
                    if end != NX:
                        for s in range(at, at + U):
                            step(known(s))
                        at += U
                for s in range(at, NX + LAG):
                    step(known(s))

            @block.sync
            def _(sp):
                def fetch(t):
                    j, v = t.j, t.v
                    if t.has(U):
                        sp.wait_ge(turned.sem, turned.after(j - U))
                    sp.dma_start(G[v][:], XG[ds(j * P, P), :]).then_inc(arrived[v], 16)

                def store(t):
                    j, v = t.j, t.v
                    sp.wait_ge(y_ready.sem, y_ready.after(j))
                    sp.dma_start(Y[ds(j * P, P), :], YO[v][:]).then_inc(stored[v], 16)

                def step(tile):
                    if tile(0):
                        fetch(tile(0))
                    if tile(LAG):
                        store(tile(LAG))

                walk(sp, step)
                for v in range(U):
                    sp.wait_ge(stored[v], 16 * ((NX - 1 - v) // U + 1))

            @block.tensor
            def _(pe):
                def turn(t):
                    j, v = t.j, t.v
                    pe.wait_ge(arrived[v], t.raised(0))
                    if t.has(1):
                        pe.wait_ge(t_copied.sem, t_copied.after(j - 1))
                    nc.tensor.transpose(TP[:, 0:P], G[v][:], ident[:]).then_inc(turned.sem, 1)

                def up(t):
                    j, v = t.j, t.v
                    e = expert_of(pe, t)
                    pe.wait_ge(t_copied.sem, t_copied.after(j))
                    if t.has(2):
                        pe.wait_ge(up_free.sem, up_free.after(j - 2))
                    for at, c, n in up_cols:
                        ins = nc.tensor.matmul(UP[v % 2][:, at:at + n], gT[v % 2][:], w_up[:, ds(e * WU + c, n)],
                                               start=True, stop=True)
                    ins.then_inc(up_ready.sem, 1)

                def turn_h(t):
                    j, v = t.j, t.v
                    pe.wait_ge(h_ready.sem, h_ready.after(j))
                    if t.has(1):
                        pe.wait_ge(h_copied.sem, h_copied.after(j - 1))
                    for c, (c0, n) in enumerate(chunks):
                        ins = nc.tensor.transpose(HP[0:n, c * P:(c + 1) * P], hid[v % 2][:, c0:c0 + n], ident[:])
                    ins.then_inc(h_turned.sem, 1)

                def down(t):
                    j, v = t.j, t.v
                    e = expert_of(pe, t)
                    pe.wait_ge(h_copied.sem, h_copied.after(j))
                    if t.has(1):
                        pe.wait_ge(y_ready.sem, y_ready.after(j - 1))
                    for c, (c0, n) in enumerate(chunks):
                        ins = nc.tensor.matmul(DP[:, 0:D], hT[v % 2][0:n, c * P:(c + 1) * P],
                                               w_down[0:n, ds(e * WD + c * D, D)], start=c == 0, stop=c == NC - 1)
                    ins.then_inc(down_ready.sem, 1)

                def step(tile):
                    if tile(3):
                        turn(tile(3))
                    if tile(4):
                        up(tile(4))
                    if tile(6):
                        down(tile(6))
                    if tile(5):
                        turn_h(tile(5))

                walk(pe, step)

            @block.scalar
            def _(act):
                def copy_t(t):
                    j, v = t.j, t.v
                    act.wait_ge(turned.sem, turned.after(j))
                    if t.has(2):
                        act.wait_ge(up_ready.sem, up_ready.after(j - 2))
                    if scale_col is not None:
                        ins = nc.scalar.activation(gT[v % 2][:], TP[:, 0:P], ACT.Copy, scale=scale_col[:, 0:1])
                    else:
                        ins = nc.scalar.activation(gT[v % 2][:], TP[:, 0:P], ACT.Copy)
                    ins.then_inc(t_copied.sem, 1)

                def silu(t):
                    j, v = t.j, t.v
                    if gated:
                        act.wait_ge(up_ready.sem, up_ready.after(j))
                        if t.has(2):
                            act.wait_ge(multiplied.sem, multiplied.after(j - 2))
                        ins = nc.scalar.activation(sg[v % 2][:, 0:H], UP[v % 2][:, 512:512 + H], ACT.Silu)
                    else:
                        act.wait_ge(multiplied.sem, multiplied.after(j))
                        if t.has(2):
                            act.wait_ge(h_turned.sem, h_turned.after(j - 2))
                        ins = nc.scalar.activation(hid[v % 2][:], sg[v % 2][:, 0:H], ACT.Silu)
                    ins.then_inc(silu_ready.sem, 1)

                def copy_h(t):
                    j, v = t.j, t.v
                    act.wait_ge(h_turned.sem, h_turned.after(j))
                    if t.has(2):
                        act.wait_ge(down_ready.sem, down_ready.after(j - 2))
                    for c, (c0, n) in enumerate(chunks):
                        if n == P:
                            continue
                        ins = nc.scalar.activation(hT[v % 2][0:n, c * P:(c + 1) * P], HP[0:n, c * P:(c + 1) * P], ACT.Copy)
                    full = H // P * P
                    ins = nc.scalar.activation(hT[v % 2][:, 0:full], HP[:, 0:full], ACT.Copy)
                    ins.then_inc(h_copied.sem, 1)

                def step(tile):
                    if tile(3):
                        copy_t(tile(3))
                    if tile(4):
                        silu(tile(4))
                    if tile(5):
                        copy_h(tile(5))

                walk(act, step)

            @block.vector
            def _(dve):
                def multiply(t):
                    j, v = t.j, t.v
                    if gated:
                        dve.wait_ge(silu_ready.sem, silu_ready.after(j))
                        if t.has(2):
                            dve.wait_ge(h_turned.sem, h_turned.after(j - 2))
                        nc.vector.tensor_tensor(hid[v % 2][:], UP[v % 2][:, 0:H], sg[v % 2][:, 0:H], ALU.mult).then_inc(multiplied.sem, 1)
                    else:
                        e = expert_of(dve, t)
                        dve.wait_ge(up_ready.sem, up_ready.after(j))
                        if t.has(2):
                            dve.wait_ge(silu_ready.sem, silu_ready.after(j - 2))
                        nc.vector.tensor_tensor(sg[v % 2][:], UP[v % 2][:, 0:WU], b_up[:, ds(e * WU, WU)], ALU.add).then_inc(biased.sem, 1)
                        dve.wait_ge(biased.sem, biased.after(j))
                        nc.vector.tensor_tensor(sg[v % 2][:, 0:H], sg[v % 2][:, 0:H], sg[v % 2][:, H:WU], ALU.mult).then_inc(multiplied.sem, 1)

                def output(t):
                    j, v = t.j, t.v
                    e = None if b_down is None else expert_of(dve, t)
                    dve.wait_ge(down_ready.sem, down_ready.after(j))
                    if t.has(U):
                        dve.wait_ge(stored[v], t.raised(U))
                    if b_down is None:
                        ins = nc.vector.tensor_copy(YO[v][:], DP[:, 0:D])
                    else:
                        ins = nc.vector.tensor_tensor(YO[v][:], DP[:, 0:D], b_down[:, ds(e * D, D)], ALU.add)
                    ins.then_inc(y_ready.sem, 1)

                def step(tile):
                    if tile(4):
                        multiply(tile(4))
                    if tile(6):
                        output(tile(6))

                walk(dve, step)


def state_space(nc, X, XL, mean, rstd, rms, ident, norm_w, w_in, conv_w, conv_b, w_lr, w_bc, w_dt, dt_b, A, Dp, w_out, sel):
    CH = 2 * S
    NCH = B * S // CH
    G = CH // P
    L = S + 1
    K = 3
    with ExitStack() as ctx:
        m = Maker(nc, ctx, "ss_")
        XS = m.sb("XS", [P, CH])
        xT = m.sb("xT", [P, CH])
        xpad = m.sb("xpad", [P, 2, 2, K + S])
        cv = m.sb("cv", [P, 2, CH])
        xi = m.sb("xi", [P, 2, CH])
        gate = m.sb("gate", [P, 2, CH])
        lr = m.sb("lr", [DT, CH])
        part = m.sb("part", [3 * 2 * N, CH], BF16)
        p1 = m.sb("p1", [3 * 2 * N, CH], BF16)
        r1 = m.sb("r1", [3 * 2 * N, CH])
        ab, ln = m.sb("ab", [P, 2, CH]), m.sb("ln", [P, 2, CH])
        delta = m.sb("delta", [P, 2, CH])
        du = m.sb("du", [P, 2, CH])
        dA = [m.sb(f"dA{v}", [P, 2, 2, L]) for v in range(2)]
        dBu = [m.sb(f"dBu{v}", [P, 2, 2, L]) for v in range(2)]
        Hs = m.sb("Hs", [P, 2, 2, L])
        HC = [m.sb(f"HC{v}", [P, 2, CH]) for v in range(2)]
        yg = m.sb("yg", [P, 2, CH])
        Yp = [m.ps(f"Y{h}", [P, CH]) for h in range(2)]
        Bp = [m.ps(f"B{v}", [P, CH]) for v in range(2)]
        Cp = [m.ps(f"C{v}", [P, CH]) for v in range(2)]
        Q = [m.ps(f"Q{v}", [P, CH]) for v in range(2)]

        cleared = m.sem("cleared")
        rows = m.sig("rows", 2 * G)
        x_added = m.sig("x_added")
        turned, xT_copied = m.sig("turned"), m.sig("xT_copied")
        in_ready = m.sig("in_ready", 4)
        in_copied = m.sig("in_copied", 4)
        conv = m.sig("conv", 8)
        xi_ready = m.sig("xi_ready", 2)
        dbl_ready = m.sig("dbl_ready", 2)
        lr_copied = m.sig("lr_copied")
        split = m.sig("split", 4)
        dt_ready = m.sig("dt_ready", 2)
        sp_act = m.sig("sp_act", 7)
        sp_dve = m.sig("sp_dve", 6)
        bc_ready = m.sig("bc_ready", 2 * N)
        dA_ready = m.sig("dA_ready", N)
        dBu_ready = m.sig("dBu_ready", N)
        scanned = m.sig("scanned", N)
        hc_ready = m.sig("hc_ready", N)
        summed = m.sig("summed", N)
        finish = m.sig("finish", 4)
        out_ready = m.sig("out_ready")
        x_updated = m.sig("x_updated")

        with nc.Block() as block:
            @block.tensor
            def _(pe):
                pe.wait_ge(cleared, 3)
                with pe.Fori(0, NCH) as c:
                    pe.wait_ge(rows.sem, rows.after(c))
                    for t in range(G):
                        ins = nc.tensor.transpose(Q[0][:, t * P:(t + 1) * P], XS[:, t * P:(t + 1) * P], ident[:])
                    ins.then_inc(turned.sem, 1)
                    pe.wait_ge(xT_copied.sem, xT_copied.after(c))
                    for k in range(4):
                        if k >= 2:
                            pe.wait_ge(in_copied.sem, in_copied.after(c, k - 1))
                        nc.tensor.matmul(Q[k % 2][:], w_in[:, k * P:(k + 1) * P], xT[:], start=True, stop=True).then_inc(in_ready.sem, 1)
                    pe.wait_ge(xi_ready.sem, xi_ready.after(c))
                    pe.wait_ge(in_copied.sem, in_copied.after(c, 4))
                    for h in range(2):
                        ins = nc.tensor.matmul(Q[0][0:DT, :], w_lr[:, h, :], xi[:, h, :], start=h == 0, stop=h == 1)
                    ins.then_inc(dbl_ready.sem, 1)
                    for h in range(2):
                        ins = nc.tensor.matmul(Q[1][0:6 * N, :], w_bc[:, h, :], xi[:, h, :], start=h == 0, stop=h == 1)
                    ins.then_inc(dbl_ready.sem, 1)
                    pe.wait_ge(lr_copied.sem, lr_copied.after(c))
                    nc.tensor.matmul(Q[0][:], w_dt[:, 0:P], lr[:], start=True, stop=True).then_inc(dt_ready.sem, 1)
                    pe.wait_ge(split.sem, split.after(c, 2))
                    nc.tensor.matmul(Q[1][:], w_dt[:, P:2 * P], lr[:], start=True, stop=True).then_inc(dt_ready.sem, 1)
                    pe.wait_ge(split.sem, split.after(c, 4))

                    def spread(n):
                        v = n % 2
                        if n >= 2:
                            pe.wait_ge(dBu_ready.sem, dBu_ready.after(c, n - 1))
                        nc.tensor.matmul(Bp[v][:], sel[:, n, :], part[:], start=True, stop=True).then_inc(bc_ready.sem, 1)
                        if n >= 2:
                            pe.wait_ge(hc_ready.sem, hc_ready.after(c, n - 1))
                        nc.tensor.matmul(Cp[v][:], sel[:, N + n, :], part[:], start=True, stop=True).then_inc(bc_ready.sem, 1)

                    spread(0)
                    for n in range(N):
                        if n + 1 < N:
                            spread(n + 1)
                        pe.wait_ge(hc_ready.sem, hc_ready.after(c, n + 1))
                        for h in range(2):
                            ins = nc.tensor.matmul(Yp[h][:], ident[:], HC[n % 2][:, h, :], start=n == 0, stop=n == N - 1)
                        ins.then_inc(summed.sem, 1)
                    pe.wait_ge(finish.sem, finish.after(c, 4))
                    for t in range(G):
                        for h in range(2):
                            ins = nc.tensor.matmul(Q[0][:, t * D:(t + 1) * D], yg[:, h, t * P:(t + 1) * P],
                                                   w_out[:, h, :], start=h == 0, stop=h == 1)
                    ins.then_inc(out_ready.sem, 1)

            @block.scalar
            def _(act):
                with act.Fori(0, NCH) as c:
                    act.wait_ge(turned.sem, turned.after(c))
                    nc.scalar.activation(xT[:], Q[0][:], ACT.Copy, scale=norm_w[:, 0:1]).then_inc(xT_copied.sem, 1)
                    for k in range(4):
                        act.wait_ge(in_ready.sem, in_ready.after(c, k + 1))
                        src = Q[k % 2][:]
                        if k < 2:
                            ins = nc.scalar.activation(xpad[:, k, :, K:K + S], src.rearrange("p (s t) -> p s t", s=2), ACT.Copy)
                        else:
                            ins = nc.scalar.activation(gate[:, k - 2, :], src, ACT.Silu)
                        ins.then_inc(in_copied.sem, 1)
                    for h in range(2):
                        act.wait_ge(conv.sem, conv.after(c, 4 * h + 4))
                        nc.scalar.activation(xi[:, h, :], cv[:, h, :], ACT.Silu, bias=conv_b[:, h:h + 1]).then_inc(xi_ready.sem, 1)
                    act.wait_ge(dbl_ready.sem, dbl_ready.after(c, 1))
                    nc.scalar.activation(lr[:], Q[0][0:DT, :], ACT.Copy).then_inc(lr_copied.sem, 1)
                    act.wait_ge(dbl_ready.sem, dbl_ready.after(c, 2))
                    nc.scalar.activation(p1[:], Q[1][0:6 * N, :], ACT.Copy).then_inc(sp_act.sem, 1)
                    for h in range(2):
                        act.wait_ge(dt_ready.sem, dt_ready.after(c, h + 1))
                        nc.scalar.activation(ab[:, h, :], Q[h][:], ACT.Abs, bias=dt_b[:, h:h + 1]).then_inc(sp_act.sem, 1)
                        nc.scalar.activation(delta[:, h, :], Q[h][:], ACT.Relu, bias=dt_b[:, h:h + 1]).then_inc(sp_act.sem, 1)
                    act.wait_ge(sp_act.sem, sp_act.after(c, 5))
                    nc.scalar.activation(ab[:], ab[:], ACT.Exp, scale=-1.0).then_inc(sp_act.sem, 1)
                    act.wait_ge(sp_dve.sem, sp_dve.after(c, 1))
                    nc.scalar.activation(ln[:], du[:], ACT.Ln).then_inc(sp_act.sem, 1)
                    act.wait_ge(sp_dve.sem, sp_dve.after(c, 6))
                    for n in range(N):
                        if n >= 2:
                            act.wait_ge(scanned.sem, scanned.after(c, n - 1))
                        for h in range(2):
                            ins = nc.scalar.activation(dA[n % 2][:, h, :, 1:L], delta[:, h, :].rearrange("p (s t) -> p s t", s=2),
                                                       ACT.Exp, scale=A[:, h, n:n + 1])
                        ins.then_inc(dA_ready.sem, 1)

            @block.gpsimd
            def _(pool):
                nc.gpsimd.memset(xpad[:], 0.0).then_inc(cleared, 1)
                with pool.Fori(0, NCH) as c:
                    pool.wait_ge(rows.sem, rows.after(c))
                    x = X[:, ds(c * CH, CH)]
                    nc.gpsimd.tensor_tensor(x, x, XL[:], ALU.add).then_inc(x_added.sem, 1)

            @block.vector
            def _(dve):
                v_ = nc.vector
                for v in range(2):
                    v_.memset(dA[v][:], 0.0)
                    v_.memset(dBu[v][:], 0.0).then_inc(cleared, 1)
                dve.wait_ge(cleared, 3)
                with dve.Fori(0, NCH) as c:
                    for t in range(G):
                        x = X[:, ds(c * CH + t * D, D)]
                        st = ds(c * G + t, 1)
                        v_.tensor_scalar(XL[:, t * D:(t + 1) * D], x, mean[:, st], rstd[:, st], ALU.subtract, ALU.mult).then_inc(rows.sem, 1)
                        v_.tensor_scalar(XS[:, t * D:(t + 1) * D], x, mean[:, st], rms[:, st], ALU.subtract, ALU.mult).then_inc(rows.sem, 1)
                    for h in range(2):
                        dve.wait_ge(in_copied.sem, in_copied.after(c, h + 1))
                        dst = cv[:, h, :].rearrange("p (s t) -> p s t", s=2)
                        for k in range(4):
                            src = xpad[:, h, :, k:k + S]
                            if k == 0:
                                ins = v_.tensor_scalar(dst, src, conv_w[:, h, k:k + 1], None, ALU.mult)
                            else:
                                dve.wait_ge(conv.sem, conv.after(c, 4 * h + k))
                                ins = v_.scalar_tensor_tensor(dst, src, conv_w[:, h, k:k + 1], dst, ALU.mult, ALU.add)
                            ins.then_inc(conv.sem, 1)
                    dve.wait_ge(sp_act.sem, sp_act.after(c, 1))
                    v_.tensor_copy(part[0:2 * N, :], p1[0:2 * N, :])
                    v_.tensor_tensor(r1[:], Q[1][0:6 * N, :], p1[:], ALU.subtract).then_inc(split.sem, 1)
                    dve.wait_ge(split.sem, split.after(c, 1))
                    v_.tensor_copy(p1[:], r1[:]).then_inc(split.sem, 1)
                    dve.wait_ge(split.sem, split.after(c, 2))
                    v_.tensor_copy(part[2 * N:4 * N, :], p1[2 * N:4 * N, :])
                    v_.tensor_tensor(r1[:], r1[:], p1[:], ALU.subtract).then_inc(split.sem, 1)
                    dve.wait_ge(split.sem, split.after(c, 3))
                    v_.tensor_copy(part[4 * N:6 * N, :], r1[4 * N:6 * N, :]).then_inc(split.sem, 1)
                    dve.wait_ge(sp_act.sem, sp_act.after(c, 6))
                    v_.tensor_scalar(du[:], ab[:], 1.0, None, ALU.add).then_inc(sp_dve.sem, 1)
                    dve.wait_ge(sp_dve.sem, sp_dve.after(c, 1))
                    v_.scalar_tensor_tensor(ab[:], du[:], 1.0, ab[:], ALU.subtract, ALU.subtract).then_inc(sp_dve.sem, 1)
                    dve.wait_ge(sp_dve.sem, sp_dve.after(c, 2))
                    v_.tensor_tensor(delta[:], delta[:], ab[:], ALU.subtract).then_inc(sp_dve.sem, 1)
                    dve.wait_ge(sp_dve.sem, sp_dve.after(c, 3))
                    dve.wait_ge(sp_act.sem, sp_act.after(c, 7))
                    v_.tensor_tensor(delta[:], delta[:], ln[:], ALU.add).then_inc(sp_dve.sem, 1)
                    dve.wait_ge(sp_dve.sem, sp_dve.after(c, 4))
                    v_.tensor_tensor(du[:], delta[:], xi[:], ALU.mult).then_inc(sp_dve.sem, 2)
                    dve.wait_ge(sp_dve.sem, sp_dve.after(c, 6))
                    for n in range(N):
                        v = n % 2
                        dve.wait_ge(bc_ready.sem, bc_ready.after(c, 2 * n + 1))
                        v_.tensor_tensor(dBu[v][:, :, :, 1:L], du[:].rearrange("p h (s t) -> p h s t", s=2),
                                         Bp[v][:].rearrange("p (s t) -> p s t", s=2).unsqueeze(1).to_broadcast([P, 2, 2, S]),
                                         ALU.mult).then_inc(dBu_ready.sem, 1)
                        dve.wait_ge(dBu_ready.sem, dBu_ready.after(c, n + 1))
                        dve.wait_ge(dA_ready.sem, dA_ready.after(c, n + 1))
                        flat = lambda a: a[:].rearrange("p h s t -> p (h s t)")
                        if n:
                            dve.wait_ge(hc_ready.sem, hc_ready.after(c, n))
                        v_.tensor_tensor_scan(flat(Hs), flat(dA[v]), flat(dBu[v]), 0.0, ALU.mult, ALU.add).then_inc(scanned.sem, 1)
                        dve.wait_ge(scanned.sem, scanned.after(c, n + 1))
                        dve.wait_ge(bc_ready.sem, bc_ready.after(c, 2 * n + 2))
                        if n >= 2:
                            dve.wait_ge(summed.sem, summed.after(c, n - 1))
                        v_.tensor_tensor(HC[v][:].rearrange("p h (s t) -> p h s t", s=2), Hs[:, :, :, 1:L],
                                         Cp[v][:].rearrange("p (s t) -> p s t", s=2).unsqueeze(1).to_broadcast([P, 2, 2, S]),
                                         ALU.mult).then_inc(hc_ready.sem, 1)
                    dve.wait_ge(summed.sem, summed.after(c))
                    for h in range(2):
                        v_.scalar_tensor_tensor(yg[:, h, :], xi[:, h, :], Dp[:, h:h + 1], Yp[h][:], ALU.mult, ALU.add).then_inc(finish.sem, 1)
                    dve.wait_ge(finish.sem, finish.after(c, 2))
                    v_.tensor_tensor(yg[:], yg[:], gate[:], ALU.mult).then_inc(finish.sem, 2)
                    dve.wait_ge(out_ready.sem, out_ready.after(c))
                    dve.wait_ge(x_added.sem, x_added.after(c))
                    x = X[:, ds(c * CH, CH)]
                    v_.tensor_tensor(x, x, Q[0][:], ALU.add).then_inc(x_updated.sem, 1)


def build(nc, a, out):
    XG0 = nc.dram_tensor("rows0", [NT * P, D], F32, kind="Internal").ap()
    Y0 = nc.dram_tensor("out_rows0", [NT * P, D], F32, kind="Internal").ap()
    XG1 = nc.dram_tensor("rows1", [(NT + T) * P, D], F32, kind="Internal").ap()
    Y1 = nc.dram_tensor("out_rows1", [(NT + T) * P, D], F32, kind="Internal").ap()
    with ExitStack() as outer:
        g = Maker(nc, outer, "g_")
        X = g.sb("X", [P, T * D])
        mean, rstd, rms = g.sb("mean", [P, T]), g.sb("rstd", [P, T]), g.sb("rms", [P, T])
        ident = g.sb("ident", [P, P])
        tri, ones = g.sb("tri", [P, P], BF16), g.sb("ones", [P, P], BF16)
        rev = g.sb("rev", [P, E])
        row_of_tile = g.sb("row_of_tile", [1, NT])
        Z = g.sb("Z", [P, D])
        cleared, zeroed = g.sem("cleared"), g.sem("zeroed")
        with ExitStack() as ctx:
            m = Maker(nc, ctx, "a_")
            w = m.sb("w", [P, 9 * P + IH])
            bias, b_iw, rope = m.sb("bias", [P, 8]), m.sb("b_iw", [P, IH]), m.sb("rope", [P, 2 * S])
            b_o = m.sb("b_o", [P, D])
            xd = a["x"].rearrange("(t p) d -> p t d", p=P)
            load(nc, "l0_", [(X[:, t * D:(t + 8) * D].rearrange("p (t d) -> p t d", d=D), xd[:, t:t + 8, :])
                             for t in range(0, T, 8)] + [
                             (ident[:], a["ident"]), (tri[:], a["tri"]), (ones[:], a["ones"]), (rev[:], a["rev"]),
                             (row_of_tile[:], a["row_of_tile"]),
                             (w[:], a["w_attn"]), (bias[:], a["b_attn"]), (b_iw[:], a["b_iw"]), (rope[:], a["rope"]),
                             (b_o[:], a["b_o"])])
            with nc.Block() as block:
                @block.gpsimd
                def _(pool):
                    nc.gpsimd.memset(Z[:], 0.0).then_inc(cleared, 1)

                @block.sync
                def _(sp):
                    sp.wait_ge(cleared, 1)
                    for XG in (XG0, XG1[0:NT * P, :]):
                        sp.dma_start(XG.rearrange("(t p) d -> p t d", p=P),
                                     Z[:].unsqueeze(1).to_broadcast([P, NT, D])).then_inc(zeroed, 16)
                    sp.wait_ge(zeroed, 32)
            row_stats(nc, "n0_", X, mean, rstd, None, None)
            attention(nc, X, mean, rstd, ident, w, bias, b_iw, rope)
            with nc.Block() as block:
                @block.vector
                def _(dve):
                    x = X[:].rearrange("p (t d) -> p t d", d=D)
                    nc.vector.tensor_tensor(x, x, b_o[:].unsqueeze(1).to_broadcast([P, T, D]), ALU.add)
        LGT = g.sb("LGT", [P, T, E])

        def mixture(tag, two, XG, Y, skip, norm, w_router, gate_b, weights, n_shared, H, gated, biases):
            with ExitStack() as ctx:
                m = Maker(nc, ctx, tag)
                rt = Routing(m)
                NC = -(-H // P)
                ne = E + bool(n_shared)
                wr = m.sb("wr", [P, E])
                wu, wd = m.sb("wu", [P, ne * 2 * H]), m.sb("wd", [P, ne * NC * D])
                pairs = [(wr[:], a[w_router]), (wu[:], a[weights[0]])]
                tail = H - (NC - 1) * P
                wd4 = wd[:].rearrange("p (e c d) -> p e c d", e=ne, c=NC)
                src = a[weights[1]]
                for c in range(NC):
                    n = P if c < NC - 1 else tail
                    pairs.append((wd4[0:n, :, c, :], src[:, c * P:c * P + n, :].rearrange("e p d -> p e d")))
                ns = gb = bu = bd = None
                if norm:
                    ns = m.sb("ns", [P, 1])
                    pairs.append((ns[:], a[norm]))
                if gate_b:
                    gb = m.sb("gb", [P, E])
                    pairs.append((gb[:], a[gate_b]))
                if biases:
                    bu, bd = m.sb("bu", [P, ne * 2 * H]), m.sb("bd", [P, ne * D])
                    pairs += [(bu[:], a[biases[0]]), (bd[:], a[biases[1]])]
                load(nc, tag + "l_", pairs)
                row_stats(nc, tag + "n_", X, mean, rstd, rms if norm else None, 1e-6)
                XS = m.sb("XS", [P, T * D])
                XL = m.sb("XL", [P, T * D])
                router(nc, tag + "r_", X, XL, XS, skip, mean, rstd, rms if norm else None, ns, wr, ident, LGT)
                route(nc, tag + "q_", LGT, gb, rt, tri, ones, rev, None, row_of_tile)
                scatter_rows(nc, tag + "s_", XS, rt, XG)
                if n_shared:
                    put = m.sem("put")
                    with nc.Block() as block:
                        @block.sync
                        def _(sp):
                            sp.dma_start(XG[NT * P:(NT + T) * P, :].rearrange("(t p) d -> p t d", p=P),
                                         XS[:].rearrange("p (t d) -> p t d", d=D)).then_inc(put, 16)
                            sp.wait_ge(put, 16)
                experts(nc, tag + "x_", rt, XG, Y, n_shared, ns, wu, wd, H, gated, bu, bd, ident)
                combine(nc, tag + "c_", X, rt, Y[0:NT * P, :], Y[NT * P:(NT + T) * P, :] if n_shared else None)

        mixture("m0_", True, XG0, Y0, True, "norm0", "w_router0", None, ("w_up0", "w_down0"), 0, H0, True, None)
        with ExitStack() as ctx:
            m = Maker(nc, ctx, "s_")
            w_in, conv_w, conv_b = m.sb("w_in", [P, 4 * P]), m.sb("conv_w", [P, 2, 4]), m.sb("conv_b", [P, 2])
            w_lr, w_bc, w_dt = m.sb("w_lr", [P, 2, DT]), m.sb("w_bc", [P, 2, 6 * N]), m.sb("w_dt", [DT, DI])
            dt_b, A, Dp, w_out = m.sb("dt_b", [P, 2]), m.sb("A", [P, 2, N]), m.sb("Dp", [P, 2]), m.sb("w_out", [P, 2, D])
            norm_w = m.sb("norm_w", [P, 1])
            sel = m.sb("sel", [6 * N, 2 * N, P], BF16)
            XL = m.sb("XL", [P, 2 * S])
            load(nc, "sl_", [(w_in[:], a["w_in"]), (conv_w[:], a["conv_w"]), (conv_b[:], a["conv_b"]), (w_lr[:], a["w_lr"]),
                             (w_bc[:], a["w_bc"]), (w_dt[:], a["w_dt"]), (dt_b[:], a["dt_b"]), (A[:], a["A_log"]),
                             (Dp[:], a["Dp"]), (w_out[:], a["w_out"]), (norm_w[:], a["norm_w"]), (sel[:], a["sel"])])
            powered = m.sem("powered")
            with nc.Block() as block:
                @block.scalar
                def _(act):
                    nc.scalar.activation(A[:], A[:], ACT.Exp).then_inc(powered, 1)

                @block.vector
                def _(dve):
                    dve.wait_ge(powered, 1)
                    nc.vector.tensor_scalar(A[:], A[:], -1.0, None, ALU.mult)
            row_stats(nc, "sn_", X, mean, rstd, rms, 1e-5)
            state_space(nc, X, XL, mean, rstd, rms, ident, norm_w, w_in, conv_w, conv_b, w_lr, w_bc, w_dt, dt_b, A, Dp, w_out, sel)
        mixture("m1_", False, XG1, Y1, False, None, "w_router1", "gate_b1", ("w_up1", "w_down1"), T, H1, False, ("b_up1", "b_down1"))
        done = g.sem("done")
        with nc.Block() as block:
            @block.sync
            def _(sp):
                sp.dma_start(out.rearrange("(t p) d -> p t d", p=P), X[:].rearrange("p (t d) -> p t d", d=D)).then_inc(done, 16)
                sp.wait_ge(done, 16)


def kernel(**inputs):
    import ml_dtypes
    import concourse.bacc as bacc
    from concourse.bass_utils import run_bass_kernel_spmd as run

    i = {k: np.asarray(v) for k, v in inputs.items()}
    f = np.float32
    c = np.ascontiguousarray

    def rows(v):
        return np.broadcast_to(v.reshape(1, -1), (P, v.size))

    def halves(v):
        return v.reshape((2, P) + v.shape[1:]).swapaxes(0, 1)

    wqkv, bqkv = i["L0_attn_w_qkv"], i["L0_attn_b_qkv"]
    swap = np.roll(np.arange(D), -(D // 2))
    q, k, v = wqkv[0:D], wqkv[D:2 * D], wqkv[2 * D:3 * D]
    bq, bk, bv = bqkv[0:D], bqkv[D:2 * D], bqkv[2 * D:3 * D]
    wiq, wik = i["L0_attn_w_iq"], i["L0_attn_w_ik"]
    biq, bik = i["L0_attn_b_iq"], i["L0_attn_b_ik"]
    w_attn = np.concatenate([q, k, q[swap], k[swap], wiq, wik, wik, v, i["L0_attn_w_iw"], i["L0_attn_w_o"]], 0).T
    b_attn = np.stack([bq, bk, bq[swap], bk[swap], biq[0:D], biq[D:2 * D], np.concatenate([bik, bik]), bv], 1)
    half = D // 2
    inv_freq = (f(1.0) / f(10000.0) ** (np.arange(half, dtype=f) / f(half))).astype(f)
    ang = (np.arange(S, dtype=f)[:, None] * inv_freq[None, :]).astype(f)
    cos, sin = np.cos(ang).T.astype(f), np.sin(ang).T.astype(f)
    rope = np.concatenate([np.concatenate([cos, cos], 0), np.concatenate([-sin, sin], 0)], 1)
    sel = np.zeros((6 * N, 2 * N, P), ml_dtypes.bfloat16)
    for n in range(2 * N):
        sel[n::2 * N, n, :] = 1
    xp = i["L1_attn_x_proj_w"]
    bc = xp[:, DT:DT + 2 * N]
    w13 = np.concatenate([np.concatenate([i["L1_ffn_w1"], i["L1_ffn_w3"]], 2),
                          np.concatenate([i["L1_ffn_sw1"], i["L1_ffn_sw3"]], 1)[None]], 0)
    b13 = np.concatenate([np.concatenate([i["L1_ffn_b1"], i["L1_ffn_b3"]], 1),
                          np.concatenate([i["L1_ffn_sb1"], i["L1_ffn_sb3"]], 0)[None]], 0)
    arrays = {
        "x": i["L0_attn_x"].reshape(B * S, D),
        "ident": np.eye(P, dtype=f),
        "tri": np.triu(np.ones((P, P), f), 1).astype(ml_dtypes.bfloat16),
        "ones": np.ones((P, P), ml_dtypes.bfloat16),
        "rev": rows(np.arange(E, 0, -1).astype(f)),
        "row_of_tile": np.arange(NT, dtype=f).reshape(1, NT),
        "w_attn": w_attn, "b_attn": b_attn, "b_iw": rows(i["L0_attn_b_iw"]), "rope": rope, "b_o": rows(i["L0_attn_b_o"]),
        "norm0": i["L0_ffn_norm_scale"].reshape(P, 1),
        "w_router0": i["L0_ffn_w_router"].T,
        "w_up0": i["L0_ffn_w_up"].transpose(2, 0, 1).reshape(D, E * 2 * H0),
        "w_down0": i["L0_ffn_w_down"].transpose(0, 2, 1),
        "w_in": i["L1_attn_in_proj_w"],
        "conv_w": halves(i["L1_attn_conv_w"][:, 0, :]),
        "conv_b": halves(i["L1_attn_conv_b"]),
        "w_lr": halves(xp[:, 0:DT]),
        "w_bc": halves(np.concatenate([bc, bc, bc], 1)),
        "w_dt": i["L1_attn_dt_proj_w"],
        "dt_b": halves(i["L1_attn_dt_proj_b"]),
        "A_log": halves(i["L1_attn_A_log"]),
        "Dp": halves(i["L1_attn_D"]),
        "w_out": halves(i["L1_attn_out_proj_w"]),
        "norm_w": i["L1_attn_norm_w"].reshape(P, 1),
        "sel": sel,
        "w_router1": i["L1_ffn_gate_w"].T,
        "gate_b1": rows(i["L1_ffn_gate_b"]),
        "w_up1": w13.transpose(1, 0, 2).reshape(D, (E + 1) * 2 * H1),
        "w_down1": np.concatenate([i["L1_ffn_w2"], i["L1_ffn_sw2"][None]], 0),
        "b_up1": rows(b13), "b_down1": rows(np.concatenate([i["L1_ffn_b2"], i["L1_ffn_sb2"][None]], 0)),
    }
    nc = bacc.Bacc("TRN2", target_bir_lowering=False, num_devices=1)
    arrays = {"in_" + n: c(v) for n, v in arrays.items()}
    a = {n[3:]: nc.dram_tensor(n, v.shape, mybir.dt.from_np(v.dtype), kind="ExternalInput").ap() for n, v in arrays.items()}
    out = nc.dram_tensor("out", [B * S, D], F32, kind="ExternalOutput").ap()
    build(nc, a, out)
    r = run(nc, [arrays], core_ids=[0])
    return r.results[0]["out"].reshape(B, S, D)
```

```python
import math
from contextlib import ExitStack

import numpy as np
import concourse.bass as bass
from concourse import mybir

F32 = mybir.dt.float32
BF16 = mybir.dt.bfloat16
I32 = mybir.dt.int32
ALU = mybir.AluOpType
ACT = mybir.ActivationFunctionType
AX = mybir.AxisListType

B, S, D = 16, 256, 128
P = 128
T = B * S // P
TOPK = 32
IH, ID = 4, 64
E = 8
H0, H1 = 352, 176
NT = 2 * B * S // P + E
DI, N, DT = 256, 16, 64
BIG = 3.0e38
EPS = 1e-5
ds = bass.ds


class Signal:

    def __init__(self, sem, per):
        self.sem, self.per, self.base = sem, per, 0

    def after(self, unit, k=None):
        return self.base + unit * self.per + (self.per if k is None else k)

    def over(self, units):
        self.base += units * self.per


class Chain:

    def __init__(self, eng, done):
        self.eng, self.done = eng, done

    def __call__(self, ins):
        ins.then_inc(self.done.sem, 1)
        self.eng.wait_ge(self.done.sem, self.done.after(0))
        self.done.over(1)


class Maker:
    def __init__(self, nc, ctx, tag):
        self.nc, self.ctx, self.tag = nc, ctx, tag

    def sb(self, name, shape, dt=F32):
        return self.ctx.enter_context(self.nc.sbuf_tensor(self.tag + name, shape, dt))

    def ps(self, name, shape, dt=F32):
        return self.ctx.enter_context(self.nc.psum_tensor(self.tag + name, shape, dt))

    def sem(self, name):
        return self.ctx.enter_context(self.nc.semaphore(self.tag + name))

    def sig(self, name, per=1):
        return Signal(self.sem(name), per)


def wait_loaded(nc, loaded, count):
    with nc.Block() as block:
        @block.sync
        def _(sp):
            sp.wait_ge(loaded.sem, loaded.after(count - 1))


def row_stats(nc, tag, chain, shifted, rooted, X, mean, scales, eps2):
    n = 1 if eps2 is None else 2
    with ExitStack() as ctx:
        m = Maker(nc, ctx, tag)
        st, mv = m.sb("st", [P, T, 6]), m.sb("mv", [P, T, 2])
        ve, t2 = m.sb("ve", [P, n, T]), m.sb("t2", [P, n, T])
        with nc.Block() as block:
            @block.vector
            def _(dve):
                link = Chain(dve, chain)
                for t in range(T):
                    ins = nc.vector.bn_stats(st[:, t, :], X[:, t * D:(t + 1) * D])
                link(ins)
                for t in range(T):
                    ins = nc.vector.bn_aggr(mv[:, t, :], st[:, t, :])
                link(ins)
                if n == 2:
                    nc.vector.tensor_scalar(ve[:, 1, :], mv[:, :, 1], 1.0 + eps2, eps2 * EPS, ALU.mult, ALU.add)
                nc.vector.tensor_scalar(ve[:, 0, :], mv[:, :, 1], EPS, None, ALU.add).then_inc(shifted.sem, 1)
                nc.vector.tensor_copy(mean[:], mv[:, :, 0])
                out = scales[:, 0:n, :]
                dve.wait_ge(rooted.sem, rooted.after(0))
                link(nc.vector.reciprocal(out, t2[:]))
                link(nc.vector.tensor_tensor(t2[:], out, out, ALU.mult))
                link(nc.vector.tensor_tensor(t2[:], t2[:], ve[:], ALU.mult))
                link(nc.vector.tensor_scalar(t2[:], t2[:], -0.5, 1.5, ALU.mult, ALU.add))
                link(nc.vector.tensor_tensor(out, out, t2[:], ALU.mult))

            @block.scalar
            def _(act):
                act.wait_ge(shifted.sem, shifted.after(0))
                nc.scalar.activation(t2[:], ve[:], ACT.Sqrt).then_inc(rooted.sem, 1)
        shifted.over(1)
        rooted.over(1)


def attention(nc, X, mean, scales, ident, w, bias, b_iw, rope):
    with ExitStack() as ctx:
        m = Maker(nc, ctx, "at_")
        W2 = 2 * P
        Xn = [m.sb(f"Xn{v}", [P, W2]) for v in range(2)]
        xT = [m.sb(f"xT{v}", [P, W2]) for v in range(2)]
        RP = [m.sb(f"RP{v}", [P, 4 * S]) for v in range(2)]
        QK = [m.sb(f"QK{v}", [P, 2 * S]) for v in range(2)]
        IQ = [m.sb(f"IQ{v}", [P, 2 * S]) for v in range(2)]
        IKV = [m.sb(f"IKV{v}", [P, 2 * S]) for v in range(2)]
        VO = [m.sb(f"VO{q}", [P, 2 * D]) for q in range(4)]
        IW = [m.sb(f"IW{v}", [P, 2, IH]) for v in range(2)]
        R = [m.sb(f"R{t}", [P, IH * S]) for t in range(2)]
        WK = [m.sb(f"WK{v}", [P, 2 * S]) for v in range(2)]
        MK = [m.sb(f"MK{v}", [P, 2 * S]) for v in range(2)]
        PR = [m.sb(f"PR{v}", [P, 2 * S]) for v in range(2)]
        PT = [m.sb(f"PT{v}", [P, 2 * S]) for v in range(2)]
        M8 = m.sb("M8", [P, 2, 8])
        mx = [m.sb(f"mx{v}", [P, 2]) for v in range(2)]
        rsum = [m.sb(f"rsum{v}", [P, 2]) for v in range(2)]
        rinv = [m.sb(f"rinv{v}", [P, 2]) for v in range(2)]
        bank = [m.ps(f"b{k}", [P, 512]) for k in range(5)]
        SC0 = m.ps("SC0", [P, 1024])
        LG = m.ps("LG", [P, 512])
        b0, b12a, b12b, b3, b4 = bank
        scale = float(1.0 / np.sqrt(np.float32(D)))

        xn_ready = m.sig("xn_ready", 2)
        xT_ready = m.sig("xT_ready")
        xT_copied = m.sig("xT_copied")
        qk_ready = m.sig("qk_ready")
        iq_ready = m.sig("iq_ready")
        ikv_ready = m.sig("ikv_ready")
        rope_parts = m.sig("rope_parts", 4)
        qk_sum = m.sig("qk_sum")
        iq_copied = m.sig("iq_copied", 2)
        ikv_copied = m.sig("ikv_copied", 2)
        vo_ready = m.sig("vo_ready")
        vo_copied = m.sig("vo_copied")
        iw_copied = m.sig("iw_copied")
        scores_ready = m.sig("scores_ready", 2)
        relu_ready = m.sig("relu_ready", 2)
        logits_ready = m.sig("logits_ready")
        idx = m.sig("idx", 8)
        topk = m.sig("topk", 16)
        penalty = m.sig("penalty")
        masked = m.sig("masked", 2)
        negmax = m.sig("negmax")
        probs_ready = m.sig("probs_ready", 2)
        rinv_ready = m.sig("rinv_ready")
        pT_ready = m.sig("pT_ready")
        pT_copied = m.sig("pT_copied")
        av_ready = m.sig("av_ready")
        x_updated = m.sig("x_updated", 2)
        passed = m.sem("passed")

        def steps(eng, step):
            step(0, 0, True, False, False)
            step(1, 1, True, True, False)
            with eng.Fori(0, (B - 4) // 4) as i:
                for k in range(4):
                    step(4 * i + 2 + k, (2 + k) % 4, True, True, True)
            step(B - 2, 2, True, True, True)
            step(B - 1, 3, True, True, True)
            step(B, 0, False, True, True)
            step(B + 1, 1, False, False, True)

        def col(k):
            return w[:, k * P:(k + 1) * P]

        with nc.Block() as block:
            @block.tensor
            def _(pe):
                def step(s, q, front, middle, tail):
                    v = q % 2
                    first = isinstance(s, int)
                    if front:
                        pe.wait_ge(xn_ready.sem, xn_ready.after(s))
                        if not (first and s < 1):
                            pe.wait_ge(iw_copied.sem, iw_copied.after(s - 1))
                        for t in range(2):
                            ins = nc.tensor.transpose(b0[:, t * P:(t + 1) * P], Xn[v][:, t * P:(t + 1) * P], ident[:])
                        ins.then_inc(xT_ready.sem, 1)
                        pe.wait_ge(xT_copied.sem, xT_copied.after(s))
                        if not (first and s < 1):
                            pe.wait_ge(relu_ready.sem, relu_ready.after(s - 1, 2))
                        for k in range(4):
                            dst = (b12a, b12b)[k // 2][:, k % 2 * S:(k % 2 + 1) * S]
                            ins = nc.tensor.matmul(dst, col(k), xT[v][:], start=True, stop=True)
                        ins.then_inc(qk_ready.sem, 1)
                        if not (first and s < 3):
                            pe.wait_ge(pT_copied.sem, pT_copied.after(s - 3))
                        for k in range(2):
                            ins = nc.tensor.matmul(b3[:, k * S:(k + 1) * S], col(4 + k), xT[v][:], start=True, stop=True)
                        ins.then_inc(iq_ready.sem, 1)
                        for k in range(2):
                            ins = nc.tensor.matmul(b0[:, k * S:(k + 1) * S], col(6 + k), xT[v][:], start=True, stop=True)
                        ins.then_inc(ikv_ready.sem, 1)
                    if middle:
                        u = 1 - v
                        pe.wait_ge(qk_sum.sem, qk_sum.after(s - 1))
                        if not (first and s < 2):
                            pe.wait_ge(masked.sem, masked.after(s - 2))
                        for t in range(2):
                            ins = nc.tensor.matmul(LG[:, t * S:(t + 1) * S], QK[u][:, t * P:(t + 1) * P],
                                                   QK[u][:, S:2 * S], start=True, stop=True)
                        ins.then_inc(logits_ready.sem, 1)
                    if front:
                        pe.wait_ge(ikv_copied.sem, ikv_copied.after(s))
                        for t in range(2):
                            nc.tensor.matmul(b0[:, t * D:(t + 1) * D], IKV[v][:, S + t * P:S + (t + 1) * P],
                                             w[:, 8 * P + IH:9 * P + IH], start=True, stop=True)
                        for t in range(2):
                            ins = nc.tensor.matmul(b0[:, W2 + t * IH:W2 + (t + 1) * IH], xT[v][:, t * P:(t + 1) * P],
                                                   w[:, 8 * P:8 * P + IH], start=True, stop=True)
                        ins.then_inc(vo_ready.sem, 1)
                        pe.wait_ge(iq_copied.sem, iq_copied.after(s))
                        for t in range(2):
                            if t == 0:
                                if not (first and s < 1):
                                    pe.wait_ge(relu_ready.sem, relu_ready.after(s - 1, 1))
                            else:
                                pe.wait_ge(rope_parts.sem, rope_parts.after(s))
                            for h in range(IH):
                                r, c = h % 2 * ID, h // 2 * S
                                dst = SC0[:, h % 2 * 512 + c:h % 2 * 512 + c + S] if t == 0 else (b12a, b12b)[h % 2][:, c:c + S]
                                ins = nc.tensor.matmul(dst, IQ[v][r:r + ID, h // 2 * S + t * P:h // 2 * S + (t + 1) * P],
                                                       IKV[v][r:r + ID, 0:S], start=True, stop=True)
                            ins.then_inc(scores_ready.sem, 1)
                    if tail:
                        if front:
                            pe.wait_ge(iq_copied.sem, iq_copied.after(s))
                        pe.wait_ge(probs_ready.sem, probs_ready.after(s - 2))
                        for t in range(2):
                            for c in range(2):
                                ins = nc.tensor.transpose(b3[:, c * S + t * P:c * S + (t + 1) * P],
                                                          PR[v][:, t * S + c * P:t * S + (c + 1) * P], ident[:])
                        ins.then_inc(pT_ready.sem, 1)
                        pe.wait_ge(pT_copied.sem, pT_copied.after(s - 2))
                        if not (first and s < 3):
                            pe.wait_ge(x_updated.sem, x_updated.after(s - 3))
                        for t in range(2):
                            for c in range(2):
                                ins = nc.tensor.matmul(b4[:, t * D:(t + 1) * D], PT[v][:, c * S + t * P:c * S + (t + 1) * P],
                                                       VO[(q + 2) % 4][:, c * D:(c + 1) * D], start=c == 0, stop=c == 1)
                        ins.then_inc(av_ready.sem, 1)

                steps(pe, step)

            @block.scalar
            def _(act):
                def step(s, q, front, middle, tail):
                    v = q % 2
                    first = isinstance(s, int)
                    if front:
                        act.wait_ge(xT_ready.sem, xT_ready.after(s))
                        nc.scalar.activation(xT[v][:], b0[:, 0:W2], ACT.Copy).then_inc(xT_copied.sem, 1)
                        act.wait_ge(iq_ready.sem, iq_ready.after(s))
                        for k in range(2):
                            nc.scalar.activation(IQ[v][:, k * S:(k + 1) * S], b3[:, k * S:(k + 1) * S], ACT.Identity,
                                                 bias=bias[:, 4 + k:5 + k]).then_inc(iq_copied.sem, 1)
                        act.wait_ge(ikv_ready.sem, ikv_ready.after(s))
                        for k in range(2):
                            nc.scalar.activation(IKV[v][:, k * S:(k + 1) * S], b0[:, k * S:(k + 1) * S], ACT.Identity,
                                                 bias=bias[:, 6 + k:7 + k]).then_inc(ikv_copied.sem, 1)
                        act.wait_ge(vo_ready.sem, vo_ready.after(s))
                        nc.scalar.activation(VO[q][:], b0[:, 0:W2], ACT.Copy).then_inc(vo_copied.sem, 1)
                    if tail:
                        act.wait_ge(negmax.sem, negmax.after(s - 2))
                        for t in range(2):
                            nc.scalar.activation(PR[v][:, t * S:(t + 1) * S], MK[v][:, t * S:(t + 1) * S], ACT.Exp,
                                                 bias=mx[v][:, t:t + 1], scale=scale,
                                                 accum_out=rsum[v][:, t:t + 1]).then_inc(probs_ready.sem, 1)
                    if front:
                        for t in range(2):
                            act.wait_ge(scores_ready.sem, scores_ready.after(s, t + 1))
                            if not (first and s < 1):
                                act.wait_ge(idx.sem, idx.after(s - 1, 7 + t))
                            if t == 0:
                                nc.scalar.activation(R[t][:], SC0[:], ACT.Relu).then_inc(relu_ready.sem, 1)
                            else:
                                nc.scalar.activation(R[t][:, 0:512], b12a[:], ACT.Relu)
                                nc.scalar.activation(R[t][:, 512:1024], b12b[:], ACT.Relu).then_inc(relu_ready.sem, 1)
                    if tail:
                        act.wait_ge(pT_ready.sem, pT_ready.after(s - 2))
                        nc.scalar.activation(PT[v][:], b3[:], ACT.Copy).then_inc(pT_copied.sem, 1)

                steps(act, step)

            @block.vector
            def _(dve):
                def normalise(s, v):
                    for t in range(2):
                        nc.vector.tensor_scalar(Xn[v][:, t * D:(t + 1) * D], X[:, ds(s * W2 + t * D, D)],
                                                mean[:, ds(s * 2 + t, 1)], scales[:, 0, ds(s * 2 + t, 1)],
                                                ALU.subtract, ALU.mult).then_inc(xn_ready.sem, 1)

                def rotate(s, v):
                    dve.wait_ge(qk_ready.sem, qk_ready.after(s))
                    for k in range(4):
                        nc.vector.scalar_tensor_tensor(RP[v][:, k * S:(k + 1) * S],
                                                       (b12a, b12b)[k // 2][:, k % 2 * S:(k % 2 + 1) * S],
                                                       bias[:, k:k + 1], rope[:, k // 2 * S:(k // 2 + 1) * S],
                                                       ALU.add, ALU.mult).then_inc(rope_parts.sem, 1)

                def head_weights(s, v):
                    dve.wait_ge(vo_copied.sem, vo_copied.after(s))
                    nc.vector.tensor_tensor(IW[v][:], b0[:, W2:W2 + 2 * IH].rearrange("p (t h) -> p t h", h=IH),
                                            b_iw[:, :].unsqueeze(1).to_broadcast([P, 2, IH]), ALU.add).then_inc(iw_copied.sem, 1)

                def index_scores(s, v):
                    dve.wait_ge(iw_copied.sem, iw_copied.after(s))
                    for h in range(IH):
                        for t in range(2):
                            dst = WK[v][:, t * S:(t + 1) * S]
                            src = R[t][:, h % 2 * 512 + h // 2 * S:h % 2 * 512 + (h // 2 + 1) * S]
                            if h == 0:
                                dve.wait_ge(relu_ready.sem, relu_ready.after(s, t + 1))
                                ins = nc.vector.tensor_scalar(dst, src, IW[v][:, t, h:h + 1], None, ALU.mult)
                            else:
                                dve.wait_ge(idx.sem, idx.after(s, 2 * h - 1 + t))
                                ins = nc.vector.scalar_tensor_tensor(dst, src, IW[v][:, t, h:h + 1], dst, ALU.mult, ALU.add)
                            ins.then_inc(idx.sem, 1)

                def choose(s, v, rounds):
                    for k in rounds:
                        for t in range(2):
                            dst = WK[v][:, t * S:(t + 1) * S]
                            if k == 0:
                                dve.wait_ge(idx.sem, idx.after(s, 7 + t))
                                dve.sem_inc(passed, 1)
                            else:
                                dve.wait_ge(topk.sem, topk.after(s, 4 * k - 1 + t))
                                dve.sem_inc(passed, 1)
                            nc.vector.max(M8[:, t, :], dst).then_inc(topk.sem, 1)
                        for t in range(2):
                            dst = WK[v][:, t * S:(t + 1) * S]
                            dve.wait_ge(topk.sem, topk.after(s, 4 * k + 1 + t))
                            dve.sem_inc(passed, 1)
                            nc.vector.match_replace(dst, M8[:, t, :], dst, -BIG).then_inc(topk.sem, 1)

                def mask(s, v):
                    dve.wait_ge(topk.sem, topk.after(s))
                    nc.vector.tensor_scalar(WK[v][:], WK[v][:], -BIG, -BIG, ALU.is_gt, ALU.mult).then_inc(penalty.sem, 1)
                    dve.wait_ge(penalty.sem, penalty.after(s))
                    dve.wait_ge(logits_ready.sem, logits_ready.after(s))
                    dve.sem_inc(passed, 1)
                    for t in range(2):
                        c = slice(t * S, (t + 1) * S)
                        nc.vector.tensor_tensor_reduce(MK[v][:, c], WK[v][:, c], LG[:, c], 1.0, -BIG, ALU.add, ALU.max,
                                                       accum_out=mx[v][:, t:t + 1]).then_inc(masked.sem, 1)
                    dve.wait_ge(masked.sem, masked.after(s))
                    nc.vector.tensor_scalar(mx[v][:], mx[v][:], -scale, None, ALU.mult).then_inc(negmax.sem, 1)

                def update(s, v):
                    dve.wait_ge(probs_ready.sem, probs_ready.after(s))
                    nc.vector.reciprocal(rinv[v][:], rsum[v][:]).then_inc(rinv_ready.sem, 1)
                    dve.wait_ge(rinv_ready.sem, rinv_ready.after(s))
                    dve.wait_ge(av_ready.sem, av_ready.after(s))
                    for t in range(2):
                        x = X[:, ds(s * W2 + t * D, D)]
                        nc.vector.scalar_tensor_tensor(x, b4[:, t * D:(t + 1) * D], rinv[v][:, t:t + 1], x,
                                                       ALU.mult, ALU.add).then_inc(x_updated.sem, 1)

                def step(s, q, front, middle, tail):
                    v = q % 2
                    u = 1 - v
                    if middle:
                        index_scores(s - 1, u)
                        choose(s - 1, u, range(0, 1))
                    if front:
                        rotate(s, v)
                    if middle:
                        choose(s - 1, u, range(1, 3))
                    if front and not (isinstance(s, int) and s == B - 1):
                        normalise(s + 1, u)
                    if middle:
                        choose(s - 1, u, range(3, TOPK // 8))
                    if front:
                        head_weights(s, v)
                    if middle:
                        mask(s - 1, u)
                    if tail:
                        update(s - 2, v)

                normalise(0, 0)
                steps(dve, step)

            @block.gpsimd
            def _(pool):
                def step(s, q, front, middle, tail):
                    v = q % 2
                    if front:
                        pool.wait_ge(rope_parts.sem, rope_parts.after(s))
                        if not (isinstance(s, int) and s < 2):
                            pool.wait_ge(logits_ready.sem, logits_ready.after(s - 2))
                        nc.gpsimd.tensor_tensor(QK[v][:], RP[v][:, 0:2 * S], RP[v][:, 2 * S:4 * S], ALU.add).then_inc(qk_sum.sem, 1)

                steps(pool, step)


class MixtureWeights:

    def __init__(self, g, tag, a, norm, w_router, gate_b, weights, n_shared, H, biases):
        self.H, self.n_shared = H, n_shared
        self.loaded = g.sig(tag + "loaded", 16)
        NC = -(-H // P)
        ne = E + bool(n_shared)
        self.wr = g.sb(tag + "wr", [P, E])
        self.wu, self.wd = g.sb(tag + "wu", [P, ne * 2 * H]), g.sb(tag + "wd", [P, ne * NC * D])
        self.pairs = [(self.wr[:], a[w_router]), (self.wu[:], a[weights[0]])]
        tail = H - (NC - 1) * P
        wd4 = self.wd[:].rearrange("p (e c d) -> p e c d", e=ne, c=NC)
        src = a[weights[1]]
        for c in range(NC):
            n = P if c < NC - 1 else tail
            self.pairs.append((wd4[0:n, :, c, :], src[:, c * P:c * P + n, :].rearrange("e p d -> p e d")))
        self.ns = self.gb = self.bu = self.bd = None
        if norm:
            self.ns = g.sb(tag + "ns", [P, 1])
            self.pairs.append((self.ns[:], a[norm]))
        if gate_b:
            self.gb = g.sb(tag + "gb", [P, E])
            self.pairs.append((self.gb[:], a[gate_b]))
        if biases:
            self.bu, self.bd = g.sb(tag + "bu", [P, ne * 2 * H]), g.sb(tag + "bd", [P, ne * D])
            self.pairs += [(self.bu[:], a[biases[0]]), (self.bd[:], a[biases[1]])]


class Routing:

    def __init__(self, m):
        self.c = [m.sb(f"c{k}", [P, T]) for k in range(2)]
        self.slot = [m.sb(f"slot{k}", [P, T], I32) for k in range(2)]
        self.tile_expert = m.sb("tile_expert", [1, NT], I32)


def route(nc, tag, chain, LGT, gate_b, rt, tri, ones, rev, start128, row_of_tile):
    with ExitStack() as ctx:
        m = Maker(nc, ctx, tag)
        shape = [P, T, E]
        ex, pr, eq = m.sb("ex", shape), m.sb("pr", shape), m.sb("eq", shape)
        oh = [m.sb(f"oh{k}", shape) for k in range(2)]
        mt = m.sb("mt", shape, BF16)
        scan = [m.sb(f"scan{k}", shape) for k in range(2)]
        tot = m.sb("tot", shape)
        mx, sm = m.sb("mx", [P, T]), m.sb("sm", [P, T])
        n_i, ct, end, st128 = m.sb("n_i", [P, E], I32), m.sb("ct", [P, E]), m.sb("end", [P, E]), m.sb("st128", [P, E])
        one8 = m.sb("one8", [P, E])
        cmp = m.sb("cmp", [1, NT, E])
        te = m.sb("te", [1, NT])
        RK = m.ps("RK", [P, T * E])
        TT = m.ps("TT", [P, T * E])
        shifted, powered, marks, ranked = m.sem("shifted"), m.sem("powered"), m.sem("marks"), m.sem("ranked")

        def each(a):
            return a[:, :].unsqueeze(2).to_broadcast(shape)

        def every(a):
            return a[:, :].unsqueeze(1).to_broadcast(shape)

        with nc.Block() as block:
            @block.vector
            def _(dve):
                v = nc.vector
                link = Chain(dve, chain)
                link(v.tensor_reduce(mx[:], LGT[:], AX.X, ALU.max))
                v.tensor_tensor(ex[:], LGT[:], each(mx), ALU.subtract).then_inc(shifted, 1)
                dve.wait_ge(powered, 1)
                link(v.tensor_reduce(sm[:], ex[:], AX.X, ALU.add))
                link(v.reciprocal(sm[:], sm[:]))
                link(v.tensor_tensor(pr[:], ex[:], each(sm), ALU.mult))
                key = LGT
                if gate_b is not None:
                    link(v.tensor_tensor(ex[:], pr[:], every(gate_b), ALU.add))
                    key = ex
                for k in range(2):
                    link(v.tensor_reduce(mx[:], key[:], AX.X, ALU.max))
                    link(v.tensor_tensor(eq[:], key[:], each(mx), ALU.is_equal))
                    link(v.tensor_tensor(eq[:], eq[:], every(rev), ALU.mult))
                    link(v.tensor_reduce(mx[:], eq[:], AX.X, ALU.max))
                    link(v.tensor_tensor(oh[k][:], eq[:], each(mx), ALU.is_equal))
                    link(v.tensor_tensor(eq[:], pr[:], oh[k][:], ALU.mult))
                    link(v.tensor_reduce(rt.c[k][:], eq[:], AX.X, ALU.add))
                    if k == 0:
                        link(v.scalar_tensor_tensor(ex[:], oh[0][:], -BIG, key[:], ALU.mult, ALU.add))
                        key = ex
                v.tensor_tensor(mt[:], oh[0][:], oh[1][:], ALU.add).then_inc(marks, 1)
                dve.wait_ge(ranked, 1)
                nc.vector.tensor_copy(tot[:], TT[:].rearrange("p (t e) -> p t e", e=E))
                link(nc.vector.tensor_copy(scan[0][:], TT[:].rearrange("p (t e) -> p t e", e=E)))
                a, b, k = scan[0], scan[1], 1
                while k < T:
                    v.tensor_copy(b[:, 0:k, :], a[:, 0:k, :])
                    link(v.tensor_tensor(b[:, k:T, :], a[:, k:T, :], a[:, 0:T - k, :], ALU.add))
                    a, b, k = b, a, 2 * k
                link(v.tensor_scalar(n_i[:], a[:, T - 1, :], float(P - 1), None, ALU.add))
                link(v.tensor_scalar(n_i[:], n_i[:], int(math.log2(P)), None, ALU.arith_shift_right))
                link(v.tensor_copy(ct[:], n_i[:]))
                link(v.memset(one8[:], 1.0))
                link(v.tensor_tensor_scan(end[:], one8[:], ct[:], 0.0, ALU.mult, ALU.add))
                link(v.tensor_tensor(st128[:], end[:], ct[:], ALU.subtract))
                link(v.tensor_scalar(st128[:], st128[:], float(P), None, ALU.mult))
                link(v.tensor_tensor(b[:], a[:], tot[:], ALU.subtract))
                link(v.tensor_tensor(b[:], b[:], RK[:].rearrange("p (t e) -> p t e", e=E), ALU.add))
                link(v.tensor_tensor(b[:], b[:], every(st128), ALU.add))
                for k in range(2):
                    link(v.tensor_tensor(eq[:], oh[k][:], b[:], ALU.mult))
                    link(v.tensor_reduce(mx[:], eq[:], AX.X, ALU.add))
                    link(v.tensor_copy(rt.slot[k][:], mx[:]))
                link(v.tensor_tensor(cmp[:], end[0:1, :].unsqueeze(1).to_broadcast([1, NT, E]),
                                     row_of_tile[:, :].unsqueeze(2).to_broadcast([1, NT, E]), ALU.is_le))
                link(v.tensor_reduce(te[:], cmp[:], AX.X, ALU.add))
                link(v.tensor_scalar(rt.tile_expert[:], te[:], float(E - 1), None, ALU.min))

            @block.scalar
            def _(act):
                act.wait_ge(shifted, 1)
                nc.scalar.activation(ex[:], ex[:], ACT.Exp).then_inc(powered, 1)

            @block.tensor
            def _(pe):
                pe.wait_ge(marks, 1)
                flat = mt[:].rearrange("p t e -> p (t e)")
                nc.tensor.matmul(RK[:], tri[:], flat, start=True, stop=True)
                nc.tensor.matmul(TT[:], ones[:], flat, start=True, stop=True).then_inc(ranked, 1)


def router(nc, tag, X, XL, XS, add_skip, mean, scales, rms, scale_col, w_router, ident, LGT):
    G = 4
    with ExitStack() as ctx:
        m = Maker(nc, ctx, tag)
        xT = [m.sb(f"xT{v}", [P, G * P]) for v in range(2)]
        TP = [m.ps(f"TP{v}", [P, G * P]) for v in range(2)]
        RP = [m.ps(f"RP{v}", [P, G * E]) for v in range(2)]
        rows = m.sig("rows", 2 * G if add_skip else G)
        added = m.sig("added")
        turned = m.sig("turned")
        copied = m.sig("copied")
        scored = m.sig("scored")
        kept = m.sig("kept")
        staged = m.sig("staged")
        ST = [m.sb(f"ST{v}", [P, G * P]) for v in range(2)]
        GN = T // G
        AHEAD = 4

        with nc.Block() as block:
            @block.vector
            def _(dve):
                def keep(g, v):
                    dve.wait_ge(scored.sem, scored.after(g))
                    nc.vector.tensor_copy(LGT[:, ds(g * G, G), :], RP[v][:].rearrange("p (t e) -> p t e", e=E)).then_inc(kept.sem, 1)

                def rows_of(g):
                    for t in range(G):
                        x = X[:, ds((g * G + t) * D, D)]
                        st = ds(g * G + t, 1)
                        if add_skip:
                            nc.vector.tensor_scalar(XL[:, ds((g * G + t) * D, D)], x, mean[:, st], scales[:, 0, st],
                                                    ALU.subtract, ALU.mult).then_inc(rows.sem, 1)
                        nc.vector.tensor_scalar(XS[:, ds(g * G + t, 1), 0:D], x.unsqueeze(1), mean[:, st], scales[:, int(rms), st],
                                                ALU.subtract, ALU.mult).then_inc(rows.sem, 1)

                for g in range(AHEAD):
                    rows_of(g)
                with dve.Fori(0, (GN - AHEAD) // 2) as i:
                    for v in range(2):
                        rows_of(2 * i + AHEAD + v)
                        keep(2 * i + v, v)
                for g in range(GN - AHEAD, GN):
                    keep(g, g % 2)

            @block.gpsimd
            def _(pool):
                if add_skip:
                    with pool.Fori(0, GN) as g:
                        pool.wait_ge(rows.sem, rows.after(g))
                        x = X[:, ds(g * G * D, G * D)]
                        nc.gpsimd.tensor_tensor(x, x, XL[:, ds(g * G * D, G * D)], ALU.add).then_inc(added.sem, 1)

            @block.tensor
            def _(pe):
                def step(g, v, first):
                    pe.wait_ge(staged.sem, staged.after(g))
                    if not first:
                        pe.wait_ge(copied.sem, copied.after(g - 2))
                    for t in range(G):
                        ins = nc.tensor.transpose(TP[v][:, t * P:(t + 1) * P], ST[v][:, t * P:(t + 1) * P], ident[:])
                    ins.then_inc(turned.sem, 1)
                    pe.wait_ge(copied.sem, copied.after(g))
                    if not first:
                        pe.wait_ge(kept.sem, kept.after(g - 2))
                    for t in range(G):
                        ins = nc.tensor.matmul(RP[v][:, t * E:(t + 1) * E], xT[v][:, t * P:(t + 1) * P], w_router[:],
                                               start=True, stop=True)
                    ins.then_inc(scored.sem, 1)

                step(0, 0, True)
                step(1, 1, True)
                with pe.Fori(0, (GN - 2) // 2) as i:
                    for v in range(2):
                        step(2 * i + 2 + v, v, False)

            @block.scalar
            def _(act):
                def step(g, v, first):
                    act.wait_ge(rows.sem, rows.after(g))
                    if not first:
                        act.wait_ge(turned.sem, turned.after(g - 2))
                    nc.scalar.activation(ST[v][:].rearrange("p (t d) -> p t d", d=D), XS[:, ds(g * G, G), 0:D], ACT.Copy).then_inc(staged.sem, 1)
                    act.wait_ge(turned.sem, turned.after(g))
                    if not first:
                        act.wait_ge(scored.sem, scored.after(g - 2))
                    if scale_col is not None:
                        ins = nc.scalar.activation(xT[v][:], TP[v][:], ACT.Copy, scale=scale_col[:, 0:1])
                    else:
                        ins = nc.scalar.activation(xT[v][:], TP[v][:], ACT.Copy)
                    ins.then_inc(copied.sem, 1)

                step(0, 0, True)
                step(1, 1, True)
                with act.Fori(0, (GN - 2) // 2) as i:
                    for v in range(2):
                        step(2 * i + 2 + v, v, False)


def combine(nc, tag, X, rt, Y, out):
    DEEP = 4
    W = 4
    with ExitStack() as ctx:
        m = Maker(nc, ctx, tag)
        G = [[m.sb(f"G{v}_{k}", [P, D]) for k in range(2)] for v in range(DEEP)]
        got = [m.sem(f"got{v}") for v in range(DEEP)]
        used = m.sem("used")
        stored = m.sem("stored")
        with nc.Block() as block:
            @block.gpsimd
            def _(pool):
                for t in range(T):
                    v = t % DEEP
                    if t >= DEEP:
                        pool.wait_ge(used, 2 * (t - DEEP + 1))
                    for k in range(2):
                        nc.gpsimd.indirect_dma_start(G[v][k][:], None, Y,
                                                     bass.IndirectOffsetOnAxis(rt.slot[k][:, t:t + 1], 0)).then_inc(got[v], 16)

            @block.vector
            def _(dve):
                for t in range(T):
                    v = t % DEEP
                    dve.wait_ge(got[v], 32 * (t // DEEP + 1))
                    x = X[:, t * D:(t + 1) * D]
                    for k in range(2):
                        nc.vector.scalar_tensor_tensor(x, G[v][k][:], rt.c[k][:, t:t + 1], x, ALU.mult, ALU.add).then_inc(used, 1)
                        dve.wait_ge(used, 2 * t + k + 1)

            @block.sync
            def _(sp):
                rows = out.rearrange("(t p) d -> p t d", p=P)
                for t in range(0, T, W):
                    sp.wait_ge(used, 2 * (t + W))
                    sp.dma_start(rows[:, t:t + W, :], X[:, t * D:(t + W) * D].rearrange("p (t d) -> p t d", d=D)).then_inc(stored, 16)
                sp.wait_ge(stored, 16 * (T // W))


def experts(nc, tag, X, XS, rt, XG, Y, n_shared, scale_col, w_up, w_down, H, gated, b_up, b_down, ident):
    NX = NT + n_shared
    chunks = [(c, min(P, H - c)) for c in range(0, H, P)]
    NC = len(chunks)
    WU = 2 * H
    WD = NC * D
    two = WU > 512
    weighted = gated
    W = D + 1 if weighted else D
    U = 4
    LAG = 7
    R = 2 * U

    class Tile:

        def __init__(self, j, v, shared, known, name):
            self.j, self.v, self.shared, self.known, self.name = j, v, shared, known, name

        def has(self, back):
            return self.known is None or self.known >= back

        def raised(self, back):
            if self.known is not None:
                return ((self.known - back) // U + 1) * 16
            return (self.j - back - self.v) * (16 // U) + 16

    with ExitStack() as ctx:
        m = Maker(nc, ctx, tag)
        G = [m.sb(f"G{v}", [P, W]) for v in range(U)]
        gT = [m.sb(f"gT{v}", [P, P]) for v in range(2)]
        hid = [m.sb(f"hid{v}", [P, H]) for v in range(2)]
        sg = [m.sb(f"sg{v}", [P, WU]) for v in range(2)]
        hT = [m.sb(f"hT{v}", [P, NC * P]) for v in range(2)]
        YO = [m.sb(f"YO{v}", [P, D]) for v in range(U)]
        UP = [m.ps(f"UP{v}", [P, 1024 if two else 512]) for v in range(2)]
        TP = m.ps("TP", [P, 512])
        HP = m.ps("HP", [P, 512])
        DP = m.ps("DP", [P, 512])
        sent, reweighted = m.sem("sent"), m.sem("reweighted")
        x_added = m.sig("x_added")
        arrived = [m.sem(f"arrived{v}") for v in range(U)]
        stored = [m.sem(f"stored{v}") for v in range(U)]
        turned = m.sig("turned")
        t_copied = m.sig("t_copied")
        up_ready = m.sig("up_ready")
        biased = m.sig("biased")
        multiplied = m.sig("multiplied")
        silu_ready = m.sig("silu_ready")
        h_ready = multiplied if gated else silu_ready
        h_turned = m.sig("h_turned")
        h_copied = m.sig("h_copied")
        down_ready = m.sig("down_ready")
        y_ready = m.sig("y_ready")
        up_cols = [(0, 0, H), (512, H, H)] if two else [(0, 0, WU)]
        def expert_of(eng, t, held, last):
            if t.shared:
                return E
            e = held.pop(t.name, None)
            if e is None:
                e = eng.value_load(rt.tile_expert[0:1, ds(t.j - n_shared, 1)], min_val=0, max_val=E - 1)
            if not last:
                held[t.name] = e
            return e

        up_free = multiplied if gated else biased

        with nc.Block() as block:
            def walk(eng, step):
                def straight(first, end):
                    held = {}
                    for s in range(first, end):
                        step(lambda lag: Tile(s - lag, (s - lag) % U, s - lag < n_shared, s - lag, s - lag) if 0 <= s - lag < NX else None, held)

                straight(0, U + LAG)
                at = U + LAG
                for end in ([n_shared, NX] if n_shared else [NX]):
                    full = (end - at) // R
                    if full > 0:
                        with eng.Fori(0, full) as i:
                            held = {}
                            for q in range(R):
                                step(lambda lag: Tile(at + i * R + (q - lag), (at + q - lag) % U, end != NX, None, q - lag), held)
                        at += full * R
                    if end != NX:
                        straight(at, end + LAG)
                        at = end + LAG
                straight(at, NX + LAG)

            @block.sync
            def _(sp):
                def fetch(t):
                    j, v = t.j, t.v
                    if t.has(U):
                        if weighted:
                            sp.wait_ge(multiplied.sem, multiplied.after(j - U))
                        else:
                            sp.wait_ge(turned.sem, turned.after(j - U))
                    if t.known == n_shared:
                        sp.wait_ge(sent, 16 * 2 * T)
                    src = XS[:, ds(j, 1), :] if t.shared else XG[ds((j - n_shared) * P, P), :]
                    dst = G[v][:].unsqueeze(1) if t.shared else G[v][:]
                    sp.dma_start(dst, src).then_inc(arrived[v], 16)

                def store(t):
                    j, v = t.j, t.v
                    sp.wait_ge(y_ready.sem, y_ready.after(j))
                    sp.dma_start(Y[ds((j - n_shared) * P, P), :], YO[v][:]).then_inc(stored[v], 16)

                def step(tile, held):
                    if tile(0):
                        fetch(tile(0))
                    if tile(LAG) and not tile(LAG).shared:
                        store(tile(LAG))

                walk(sp, step)
                for v in range(U):
                    sp.wait_ge(stored[v], 16 * ((NT - 1 - v) // U + 1))

            @block.gpsimd
            def _(pool):
                for k in range(2):
                    if weighted:
                        if k == 1:
                            pool.wait_ge(sent, 16 * T)
                        nc.gpsimd.tensor_copy(XS[:, :, D], rt.c[k][:]).then_inc(reweighted, 1)
                        pool.wait_ge(reweighted, k + 1)
                    for t in range(T):
                        nc.gpsimd.indirect_dma_start(XG, bass.IndirectOffsetOnAxis(rt.slot[k][:, t:t + 1], 0),
                                                     XS[:, t, :], None).then_inc(sent, 16)

            @block.tensor
            def _(pe):
                def turn(t):
                    j, v = t.j, t.v
                    pe.wait_ge(arrived[v], t.raised(0))
                    if t.has(1):
                        pe.wait_ge(t_copied.sem, t_copied.after(j - 1))
                    nc.tensor.transpose(TP[:, 0:P], G[v][:, 0:D], ident[:]).then_inc(turned.sem, 1)

                def up(t, held):
                    j, v = t.j, t.v
                    e = expert_of(pe, t, held, False)
                    pe.wait_ge(t_copied.sem, t_copied.after(j))
                    if t.has(2):
                        pe.wait_ge(up_free.sem, up_free.after(j - 2))
                    for at, c, n in up_cols:
                        ins = nc.tensor.matmul(UP[v % 2][:, at:at + n], gT[v % 2][:], w_up[:, ds(e * WU + c, n)],
                                               start=True, stop=True)
                    ins.then_inc(up_ready.sem, 1)

                def turn_h(t):
                    j, v = t.j, t.v
                    pe.wait_ge(h_ready.sem, h_ready.after(j))
                    if t.has(1):
                        pe.wait_ge(h_copied.sem, h_copied.after(j - 1))
                    for c, (c0, n) in enumerate(chunks):
                        ins = nc.tensor.transpose(HP[0:n, c * P:(c + 1) * P], hid[v % 2][:, c0:c0 + n], ident[:])
                    ins.then_inc(h_turned.sem, 1)

                def down(t, held):
                    j, v = t.j, t.v
                    e = expert_of(pe, t, held, True)
                    pe.wait_ge(h_copied.sem, h_copied.after(j))
                    if t.has(1):
                        pe.wait_ge(y_ready.sem, y_ready.after(j - 1))
                    for c, (c0, n) in enumerate(chunks):
                        ins = nc.tensor.matmul(DP[:, 0:D], hT[v % 2][0:n, c * P:(c + 1) * P],
                                               w_down[0:n, ds(e * WD + c * D, D)], start=c == 0, stop=c == NC - 1)
                    ins.then_inc(down_ready.sem, 1)

                def step(tile, held):
                    if tile(3):
                        turn(tile(3))
                    if tile(4):
                        up(tile(4), held)
                    if tile(6):
                        down(tile(6), held)
                    if tile(5):
                        turn_h(tile(5))

                walk(pe, step)

            @block.scalar
            def _(act):
                def copy_t(t):
                    j, v = t.j, t.v
                    act.wait_ge(turned.sem, turned.after(j))
                    if t.has(2):
                        act.wait_ge(up_ready.sem, up_ready.after(j - 2))
                    if scale_col is not None:
                        ins = nc.scalar.activation(gT[v % 2][:], TP[:, 0:P], ACT.Copy, scale=scale_col[:, 0:1])
                    else:
                        ins = nc.scalar.activation(gT[v % 2][:], TP[:, 0:P], ACT.Copy)
                    ins.then_inc(t_copied.sem, 1)

                def silu(t):
                    j, v = t.j, t.v
                    if gated:
                        act.wait_ge(up_ready.sem, up_ready.after(j))
                        if t.has(2):
                            act.wait_ge(multiplied.sem, multiplied.after(j - 2))
                        ins = nc.scalar.activation(sg[v % 2][:, 0:H], UP[v % 2][:, 512:512 + H], ACT.Silu)
                    else:
                        act.wait_ge(multiplied.sem, multiplied.after(j))
                        if t.has(2):
                            act.wait_ge(h_turned.sem, h_turned.after(j - 2))
                        ins = nc.scalar.activation(hid[v % 2][:], sg[v % 2][:, 0:H], ACT.Silu)
                    ins.then_inc(silu_ready.sem, 1)

                def copy_h(t):
                    j, v = t.j, t.v
                    act.wait_ge(h_turned.sem, h_turned.after(j))
                    if t.has(2):
                        act.wait_ge(down_ready.sem, down_ready.after(j - 2))
                    for c, (c0, n) in enumerate(chunks):
                        if n == P:
                            continue
                        ins = nc.scalar.activation(hT[v % 2][0:n, c * P:(c + 1) * P], HP[0:n, c * P:(c + 1) * P], ACT.Copy)
                    full = H // P * P
                    ins = nc.scalar.activation(hT[v % 2][:, 0:full], HP[:, 0:full], ACT.Copy)
                    ins.then_inc(h_copied.sem, 1)

                def step(tile, held):
                    if tile(3):
                        copy_t(tile(3))
                    if tile(4):
                        silu(tile(4))
                    if tile(5):
                        copy_h(tile(5))

                walk(act, step)

            @block.vector
            def _(dve):
                def multiply(t, held):
                    j, v = t.j, t.v
                    if gated:
                        dve.wait_ge(silu_ready.sem, silu_ready.after(j))
                        if t.has(2):
                            dve.wait_ge(h_turned.sem, h_turned.after(j - 2))
                        nc.vector.scalar_tensor_tensor(hid[v % 2][:], UP[v % 2][:, 0:H], G[v][:, D:D + 1], sg[v % 2][:, 0:H],
                                                       ALU.mult, ALU.mult).then_inc(multiplied.sem, 1)
                    else:
                        e = expert_of(dve, t, held, False)
                        dve.wait_ge(up_ready.sem, up_ready.after(j))
                        if t.has(2):
                            dve.wait_ge(silu_ready.sem, silu_ready.after(j - 2))
                        nc.vector.tensor_tensor(sg[v % 2][:], UP[v % 2][:, 0:WU], b_up[:, ds(e * WU, WU)], ALU.add).then_inc(biased.sem, 1)
                        dve.wait_ge(biased.sem, biased.after(j))
                        nc.vector.tensor_tensor(sg[v % 2][:, 0:H], sg[v % 2][:, 0:H], sg[v % 2][:, H:WU], ALU.mult).then_inc(multiplied.sem, 1)

                def output(t, held):
                    j, v = t.j, t.v
                    e = None if b_down is None else expert_of(dve, t, held, True)
                    dve.wait_ge(down_ready.sem, down_ready.after(j))
                    if not t.shared and t.has(n_shared + U):
                        dve.wait_ge(stored[v], t.raised(n_shared + U))
                    if n_shared and t.has(1) and (t.shared or t.known == n_shared):
                        dve.wait_ge(x_added.sem, x_added.after(j - 1))
                    if b_down is None:
                        ins = nc.vector.tensor_copy(YO[v][:], DP[:, 0:D])
                    else:
                        ins = nc.vector.tensor_tensor(YO[v][:], DP[:, 0:D], b_down[:, ds(e * D, D)], ALU.add)
                    ins.then_inc(y_ready.sem, 1)
                    if t.shared:
                        dve.wait_ge(y_ready.sem, y_ready.after(j))
                        x = X[:, ds(j * D, D)]
                        nc.vector.tensor_tensor(x, x, YO[v][:], ALU.add).then_inc(x_added.sem, 1)

                def step(tile, held):
                    if tile(4):
                        multiply(tile(4), held)
                    if tile(6):
                        output(tile(6), held)

                walk(dve, step)


def state_space(nc, X, rt, Y, mean, scales, ident, norm_w, w_in, w_conv, conv_b, w_lr, w_bc, w_dt, dt_b, A, Dp, w_out, sel):
    CH = 2 * S
    NCH = B * S // CH
    G = CH // P
    L = S + 1
    NA = 4
    K = 3
    with ExitStack() as ctx:
        m = Maker(nc, ctx, "ss_")
        XL, XS = m.sb("XL", [P, CH]), m.sb("XS", [P, CH])
        st, mv = m.sb("st", [P, G, 6]), m.sb("mv", [P, G, 2])
        ve, lv, nw = m.sb("ve", [P, 2, G]), m.sb("lv", [P, 2, G]), m.sb("nw", [P, 2, G])
        xT = m.sb("xT", [P, CH])
        xpad = m.sb("xpad", [P, 2, 2, K + S])
        xi = [m.sb(f"xi{v}", [P, 2, CH]) for v in range(2)]
        gate = [m.sb(f"gate{v}", [P, 2, CH]) for v in range(2)]
        delta = [m.sb(f"delta{v}", [P, 2, CH]) for v in range(2)]
        du = [m.sb(f"du{v}", [P, 2, CH]) for v in range(2)]
        part = [m.sb(f"part{v}", [3 * 2 * N, CH], BF16) for v in range(2)]
        lr = m.sb("lr", [DT, CH])
        p1, p2 = m.sb("p1", [3 * 2 * N, CH], BF16), m.sb("p2", [3 * 2 * N, CH], BF16)
        r1 = m.sb("r1", [3 * 2 * N, CH])
        ez, ln, tz = m.sb("ez", [P, 2, CH]), m.sb("ln", [P, 2, CH]), m.sb("tz", [P, 2, CH])
        dA = [m.sb(f"dA{v}", [P, 2, 2, L]) for v in range(NA)]
        dBu = [m.sb(f"dBu{v}", [P, 2, 2, L]) for v in range(2)]
        Hs = [m.sb(f"Hs{v}", [P, 2, 2, L]) for v in range(2)]
        HC = [m.sb(f"HC{v}", [P, 2, CH]) for v in range(2)]
        yg = m.sb("yg", [P, 2, CH])
        Yp = [m.ps(f"Y{h}", [P, CH]) for h in range(2)]
        Bp = [m.ps(f"B{v}", [P, CH]) for v in range(2)]
        Cp = [m.ps(f"C{v}", [P, CH]) for v in range(2)]
        Q = [m.ps(f"Q{v}", [P, CH]) for v in range(2)]

        slot = [m.sb(f"slot{k}", [P, G], I32) for k in range(2)]
        pair = m.sb("pair", [P, CH])
        shift = m.sb("shift", [P, 2, T])
        dve_passed = m.sem("dve_passed")
        passed, joined = m.sem("passed"), m.sig("joined")
        cleared = m.sem("cleared")
        slots_ready = m.sig("slots_ready", 2)
        gathered = m.sig("gathered", 2 * G * 16)
        stats = m.sig("stats", 10)
        log_ready, root_ready = m.sig("log_ready"), m.sig("root_ready")
        rows = m.sig("rows", 2 * G)
        x_added = m.sig("x_added")
        turned, xT_copied = m.sig("turned"), m.sig("xT_copied")
        in_ready = m.sig("in_ready", 4)
        in_copied = m.sig("in_copied", 4)
        conv_ready = m.sig("conv_ready", 2)
        xi_ready = m.sig("xi_ready", 2)
        gate_ready = m.sig("gate_ready")
        dbl_ready = m.sig("dbl_ready", 2)
        lr_copied = m.sig("lr_copied")
        p1_copied = m.sig("p1_copied", 2)
        r1_ready = m.sig("r1_ready")
        p2_copied = m.sig("p2_copied", 2)
        r2_ready = m.sig("r2_ready")
        split = m.sig("split")
        dt_ready = m.sig("dt_ready", 2)
        z_copied = m.sig("z_copied", 4)
        ez_ready = m.sig("ez_ready")
        tz_ready = m.sig("tz_ready")
        ln_ready = m.sig("ln_ready")
        softplus = m.sig("softplus", 3)
        du_ready = m.sig("du_ready")
        b_ready, c_ready = m.sig("b_ready", N), m.sig("c_ready", N)
        dA_ready = m.sig("dA_ready", N)
        dBu_ready = m.sig("dBu_ready", N)
        scanned = m.sig("scanned", N)
        hc_ready = m.sig("hc_ready", N)
        summed = m.sig("summed", N)
        finish = m.sig("finish", 3)
        out_ready = m.sig("out_ready")
        x_updated = m.sig("x_updated")

        def seqs(a):
            return a.rearrange("p (s t) -> p s t", s=2)

        def both(a):
            return a.rearrange("p h (s t) -> p h s t", s=2)

        def flat(a):
            return a[:].rearrange("p h s t -> p (h s t)")

        def no_stats(k, c):
            pass

        def chunks(eng, scan, inputs, first=None, stats=no_stats):
            for k in range(N):
                stats(k, 0)
            stats(0, 1)
            for k in range(N):
                inputs(k, 0, 0)
            for k in range(1, N):
                stats(k, 1)
            if first is not None:
                first()
            scan(0, 0, 2)
            with eng.Fori(0, (NCH - 4) // 2) as i:
                scan(2 * i + 1, 1, 2)
                scan(2 * i + 2, 0, 2)
            scan(NCH - 3, 1, 2)
            scan(NCH - 2, 0, 1)
            scan(NCH - 1, 1, 0)

        with nc.Block() as block:
            @block.tensor
            def _(pe):
                pe.wait_ge(cleared, NA + 3)

                def inputs(k, c, v):
                    static = isinstance(c, int)
                    if k == 1:
                        pe.wait_ge(rows.sem, rows.after(c))
                        if not (static and c < 1):
                            pe.wait_ge(z_copied.sem, z_copied.after(c - 1))
                        for t in range(G):
                            ins = nc.tensor.transpose(Q[1][:, t * P:(t + 1) * P], XS[:, t * P:(t + 1) * P], ident[:])
                        ins.then_inc(turned.sem, 1)
                    if k == 2:
                        pe.wait_ge(xT_copied.sem, xT_copied.after(c))
                        if not (static and c < 2):
                            pe.wait_ge(x_updated.sem, x_updated.after(c - 2))
                        for q in range(2):
                            nc.tensor.matmul(Q[q][:], w_in[:, q * P:(q + 1) * P], xT[:], start=True, stop=True).then_inc(in_ready.sem, 1)
                    if k == 3:
                        for q in range(2, 4):
                            pe.wait_ge(in_copied.sem, in_copied.after(c, q - 1))
                            nc.tensor.matmul(Q[q - 2][:], w_in[:, q * P:(q + 1) * P], xT[:], start=True, stop=True).then_inc(in_ready.sem, 1)
                    if k in (5, 6):
                        h = k - 5
                        pe.wait_ge(in_copied.sem, in_copied.after(c, 3 + h))
                        for q in range(K + 1):
                            ins = nc.tensor.matmul(Q[h][:], w_conv[:, h, q, :], xpad[:, h, :, q:q + S], start=q == 0, stop=q == K)
                        ins.then_inc(conv_ready.sem, 1)
                    if k == 8:
                        pe.wait_ge(xi_ready.sem, xi_ready.after(c))
                        for h in range(2):
                            ins = nc.tensor.matmul(Q[0][0:DT, :], w_lr[:, h, :], xi[v][:, h, :], start=h == 0, stop=h == 1)
                        ins.then_inc(dbl_ready.sem, 1)
                        for h in range(2):
                            ins = nc.tensor.matmul(Q[1][0:6 * N, :], w_bc[:, h, :], xi[v][:, h, :], start=h == 0, stop=h == 1)
                        ins.then_inc(dbl_ready.sem, 1)
                    if k == 10:
                        pe.wait_ge(lr_copied.sem, lr_copied.after(c))
                        nc.tensor.matmul(Q[0][:], w_dt[:, 0:P], lr[:], start=True, stop=True).then_inc(dt_ready.sem, 1)
                        pe.wait_ge(r1_ready.sem, r1_ready.after(c))
                        nc.tensor.matmul(Q[1][:], w_dt[:, P:2 * P], lr[:], start=True, stop=True).then_inc(dt_ready.sem, 1)

                def spread_b(n, c, v):
                    if n >= 2:
                        pe.wait_ge(dBu_ready.sem, dBu_ready.after(c, n - 1))
                    elif not (isinstance(c, int) and c < 1):
                        pe.wait_ge(dBu_ready.sem, dBu_ready.after(c - 1, N - 1 + n))
                    nc.tensor.matmul(Bp[n % 2][:], sel[:, n, :], part[v][:], start=True, stop=True).then_inc(b_ready.sem, 1)

                def spread_c(n, c, v):
                    if n >= 2:
                        pe.wait_ge(hc_ready.sem, hc_ready.after(c, n - 1))
                    elif not (isinstance(c, int) and c < 1):
                        pe.wait_ge(hc_ready.sem, hc_ready.after(c - 1, N - 1 + n))
                    nc.tensor.matmul(Cp[n % 2][:], sel[:, N + n, :], part[v][:], start=True, stop=True).then_inc(c_ready.sem, 1)

                def output(c):
                    pe.wait_ge(finish.sem, finish.after(c))
                    for t in range(G):
                        for h in range(2):
                            ins = nc.tensor.matmul(Q[0][:, t * D:(t + 1) * D], yg[:, h, t * P:(t + 1) * P],
                                                   w_out[:, h, :], start=h == 0, stop=h == 1)
                    ins.then_inc(out_ready.sem, 1)

                def scan(c, v, more):
                    static = isinstance(c, int)
                    for n in range(N):
                        if n == N - 2 and more:
                            pe.wait_ge(split.sem, split.after(c + 1))
                        if n + 2 < N:
                            spread_b(n + 2, c, v)
                        elif more:
                            spread_b(n + 2 - N, c + 1, 1 - v)
                        if n + 1 < N:
                            spread_c(n + 1, c, v)
                        elif more:
                            spread_c(0, c + 1, 1 - v)
                        if more:
                            inputs(n, c + 1, 1 - v)
                        if n == 0 and not (static and c < 1):
                            pe.wait_ge(finish.sem, finish.after(c - 1, 2))
                        pe.wait_ge(hc_ready.sem, hc_ready.after(c, n + 1))
                        for h in range(2):
                            ins = nc.tensor.matmul(Yp[h][:], ident[:], HC[n % 2][:, h, :], start=n == 0, stop=n == N - 1)
                        ins.then_inc(summed.sem, 1)
                        if n == 0 and not (static and c < 1):
                            pe.wait_ge(z_copied.sem, z_copied.after(c))
                            output(c - 1)

                def first():
                    pe.wait_ge(split.sem, split.after(0))
                    spread_b(0, 0, 0)
                    spread_b(1, 0, 0)
                    spread_c(0, 0, 0)

                chunks(pe, scan, inputs, first)
                output(NCH - 1)

            @block.scalar
            def _(act):
                def inputs(k, c, v):
                    if k == 0:
                        if not (isinstance(c, int) and c < 1):
                            act.wait_ge(x_added.sem, x_added.after(c - 1))
                            act.wait_ge(turned.sem, turned.after(c - 1))
                        act.wait_ge(stats.sem, stats.after(c))
                        for t in range(G):
                            for q, dst in enumerate((XL, XS)):
                                nc.scalar.activation(dst[:, t * D:(t + 1) * D], X[:, ds(c * CH + t * D, D)], ACT.Identity,
                                                     bias=shift[:, q, ds(c * G + t, 1)],
                                                     scale=scales[:, q, ds(c * G + t, 1)]).then_inc(rows.sem, 1)
                    if k == 2:
                        act.wait_ge(turned.sem, turned.after(c))
                        nc.scalar.activation(xT[:], Q[1][:], ACT.Copy, scale=norm_w[:, 0:1]).then_inc(xT_copied.sem, 1)
                    if k in (3, 4):
                        for q in range(2 * k - 6, 2 * k - 4):
                            act.wait_ge(in_ready.sem, in_ready.after(c, q + 1))
                            dst = xpad[:, q, :, K:K + S] if q < 2 else seqs(gate[v][:, q - 2, :])
                            nc.scalar.activation(dst, seqs(Q[q % 2][:]), ACT.Copy).then_inc(in_copied.sem, 1)
                    if k == 7:
                        for h in range(2):
                            act.wait_ge(conv_ready.sem, conv_ready.after(c, h + 1))
                            nc.scalar.activation(xi[v][:, h, :], Q[h][:], ACT.Silu, bias=conv_b[:, h:h + 1]).then_inc(xi_ready.sem, 1)
                        act.wait_ge(in_copied.sem, in_copied.after(c))
                        nc.scalar.activation(gate[v][:], gate[v][:], ACT.Silu).then_inc(gate_ready.sem, 1)
                    if k == 9:
                        act.wait_ge(dbl_ready.sem, dbl_ready.after(c, 1))
                        nc.scalar.activation(lr[:], Q[0][0:DT, :], ACT.Copy).then_inc(lr_copied.sem, 1)
                        act.wait_ge(dbl_ready.sem, dbl_ready.after(c, 2))
                        nc.scalar.activation(p1[:], Q[1][0:6 * N, :], ACT.Copy).then_inc(p1_copied.sem, 1)
                        nc.scalar.activation(part[v][0:2 * N, :], Q[1][0:2 * N, :], ACT.Copy).then_inc(p1_copied.sem, 1)
                    if k == 10:
                        act.wait_ge(r1_ready.sem, r1_ready.after(c))
                        nc.scalar.activation(p2[:], r1[:], ACT.Copy).then_inc(p2_copied.sem, 1)
                        nc.scalar.activation(part[v][2 * N:4 * N, :], r1[2 * N:4 * N, :], ACT.Copy).then_inc(p2_copied.sem, 1)
                    if k == 12:
                        act.wait_ge(r2_ready.sem, r2_ready.after(c))
                        nc.scalar.activation(part[v][4 * N:6 * N, :], r1[4 * N:6 * N, :], ACT.Copy).then_inc(split.sem, 1)
                    if k == 11:
                        for h in range(2):
                            act.wait_ge(dt_ready.sem, dt_ready.after(c, h + 1))
                            nc.scalar.activation(ez[:, h, :], Q[h][:], ACT.Abs, bias=dt_b[:, h:h + 1]).then_inc(z_copied.sem, 1)
                            nc.scalar.activation(delta[v][:, h, :], Q[h][:], ACT.Relu, bias=dt_b[:, h:h + 1]).then_inc(z_copied.sem, 1)
                        act.wait_ge(z_copied.sem, z_copied.after(c))
                        nc.scalar.activation(ez[:], ez[:], ACT.Exp, scale=-1.0).then_inc(ez_ready.sem, 1)
                        act.wait_ge(ez_ready.sem, ez_ready.after(c))
                        nc.scalar.activation(ln[:], ez[:], ACT.Ln, bias=1.0).then_inc(ln_ready.sem, 1)

                def roots(k, c):
                    if k == 11:
                        act.wait_ge(stats.sem, stats.after(c, 4))
                        nc.scalar.activation(lv[:], ve[:], ACT.Ln).then_inc(log_ready.sem, 1)
                    if k == 12:
                        act.wait_ge(log_ready.sem, log_ready.after(c))
                        nc.scalar.activation(scales[:, :, ds(c * G, G)], lv[:], ACT.Exp, scale=-0.5).then_inc(root_ready.sem, 1)

                def powers(n, c, v):
                    if n >= NA:
                        act.wait_ge(scanned.sem, scanned.after(c, n - NA + 1))
                    elif not (isinstance(c, int) and c < 1):
                        act.wait_ge(scanned.sem, scanned.after(c - 1, N - NA + n + 1))
                    for h in range(2):
                        ins = nc.scalar.activation(dA[n % NA][:, h, :, 1:L], seqs(delta[v][:, h, :]), ACT.Exp, scale=A[:, h, n:n + 1])
                    ins.then_inc(dA_ready.sem, 1)

                def first():
                    act.wait_ge(softplus.sem, softplus.after(0))
                    for n in range(NA - 1):
                        powers(n, 0, 0)

                def scan(c, v, more):
                    for n in range(N):
                        ahead = n + NA - 1
                        if ahead == N and more:
                            act.wait_ge(softplus.sem, softplus.after(c + 1))
                        if ahead < N:
                            powers(ahead, c, v)
                        elif more:
                            powers(ahead - N, c + 1, 1 - v)
                        if more:
                            inputs(n, c + 1, 1 - v)
                        if more > 1:
                            roots(n, c + 2)

                chunks(act, scan, inputs, first, roots)

            @block.gpsimd
            def _(pool):
                nc.gpsimd.memset(xpad[:], 0.0).then_inc(cleared, 1)

                def gather(c):
                    if not (isinstance(c, int) and c < 1):
                        pool.wait_ge(joined.sem, joined.after(c - 1))
                    pool.wait_ge(slots_ready.sem, slots_ready.after(c))
                    pool.sem_inc(passed, 1)
                    for t in range(G):
                        nc.gpsimd.indirect_dma_start(pair[:, t * D:(t + 1) * D], None, Y,
                                                     bass.IndirectOffsetOnAxis(slot[0][:, t:t + 1], 0)).then_inc(gathered.sem, 16)
                    pool.wait_ge(gathered.sem, gathered.after(c, G * 16))
                    pool.sem_inc(passed, 1)
                    for t in range(G):
                        nc.gpsimd.indirect_dma_start(pair[:, t * D:(t + 1) * D], None, Y,
                                                     bass.IndirectOffsetOnAxis(slot[1][:, t:t + 1], 0),
                                                     compute_op=ALU.add).then_inc(gathered.sem, 16)
                    pool.wait_ge(gathered.sem, gathered.after(c))
                    pool.sem_inc(passed, 1)
                    x = X[:, ds(c * CH, CH)]
                    nc.gpsimd.tensor_tensor(x, x, pair[:], ALU.add).then_inc(joined.sem, 1)

                def skip(c):
                    pool.wait_ge(rows.sem, rows.after(c))
                    pool.sem_inc(passed, 1)
                    x = X[:, ds(c * CH, CH)]
                    nc.gpsimd.tensor_tensor(x, x, XL[:], ALU.add).then_inc(x_added.sem, 1)

                def inputs(c, v):
                    pool.wait_ge(p2_copied.sem, p2_copied.after(c))
                    nc.gpsimd.tensor_tensor(r1[:], r1[:], p2[:], ALU.subtract).then_inc(r2_ready.sem, 1)
                    pool.wait_ge(tz_ready.sem, tz_ready.after(c))
                    nc.gpsimd.tensor_tensor(tz[:], ez[:], tz[:], ALU.subtract).then_inc(softplus.sem, 1)
                    pool.wait_ge(softplus.sem, softplus.after(c, 1))
                    nc.gpsimd.tensor_tensor(delta[v][:], delta[v][:], tz[:], ALU.add).then_inc(softplus.sem, 1)
                    pool.wait_ge(softplus.sem, softplus.after(c, 2))
                    pool.wait_ge(ln_ready.sem, ln_ready.after(c))
                    nc.gpsimd.tensor_tensor(delta[v][:], delta[v][:], ln[:], ALU.add).then_inc(softplus.sem, 1)
                    pool.wait_ge(softplus.sem, softplus.after(c))
                    nc.gpsimd.tensor_tensor(du[v][:], delta[v][:], xi[v][:], ALU.mult).then_inc(du_ready.sem, 1)

                gather(0)
                for c in range(2):
                    skip(c)
                    gather(c + 1)
                    inputs(c, c)
                with pool.Fori(0, (NCH - 4) // 2) as i:
                    for v in range(2):
                        skip(2 * i + 2 + v)
                        gather(2 * i + 3 + v)
                        inputs(2 * i + 2 + v, v)
                for c in range(NCH - 2, NCH):
                    skip(c)
                    if c + 1 < NCH:
                        gather(c + 1)
                    inputs(c, c % 2)

            @block.vector
            def _(dve):
                v_ = nc.vector
                for v in range(NA):
                    v_.memset(dA[v][:], 0.0).then_inc(cleared, 1)
                for v in range(2):
                    v_.memset(dBu[v][:], 0.0).then_inc(cleared, 1)
                dve.wait_ge(cleared, NA + 3)

                def scales_of(k, c):
                    y = scales[:, :, ds(c * G, G)]
                    if k == 0:
                        if not (isinstance(c, int) and c < 1):
                            dve.wait_ge(gathered.sem, gathered.after(c - 1))
                        for q in range(2):
                            v_.tensor_copy(slot[q][:], rt.slot[q][:, ds(c * G, G)]).then_inc(slots_ready.sem, 1)
                    if k == 7:
                        dve.wait_ge(joined.sem, joined.after(c))
                        for t in range(G):
                            ins = v_.bn_stats(st[:, t, :], X[:, ds((c * G + t) * D, D)])
                        ins.then_inc(stats.sem, 1)
                    if k == 8:
                        dve.wait_ge(stats.sem, stats.after(c, 1))
                        dve.sem_inc(dve_passed, 1)
                        for t in range(G):
                            ins = v_.bn_aggr(mv[:, t, :], st[:, t, :])
                        ins.then_inc(stats.sem, 1)
                    if k == 9:
                        dve.wait_ge(stats.sem, stats.after(c, 2))
                        v_.tensor_scalar(ve[:, 0, :], mv[:, :, 1], EPS, None, ALU.add).then_inc(stats.sem, 1)
                        v_.tensor_scalar(ve[:, 1, :], mv[:, :, 1], 1.0 + EPS, EPS * EPS, ALU.mult, ALU.add).then_inc(stats.sem, 1)
                        v_.tensor_copy(mean[:, ds(c * G, G)], mv[:, :, 0]).then_inc(stats.sem, 1)
                    if k == 13:
                        dve.wait_ge(root_ready.sem, root_ready.after(c))
                        v_.tensor_tensor(nw[:], y, y, ALU.mult).then_inc(stats.sem, 1)
                        dve.wait_ge(stats.sem, stats.after(c, 6))
                        v_.tensor_tensor(nw[:], nw[:], ve[:], ALU.mult).then_inc(stats.sem, 1)
                    if k == 14:
                        dve.wait_ge(stats.sem, stats.after(c, 7))
                        v_.tensor_scalar(nw[:], nw[:], -0.5, 1.5, ALU.mult, ALU.add).then_inc(stats.sem, 1)
                        dve.wait_ge(stats.sem, stats.after(c, 8))
                        v_.tensor_tensor(y, y, nw[:], ALU.mult).then_inc(stats.sem, 1)
                        dve.wait_ge(stats.sem, stats.after(c, 9))
                        v_.scalar_tensor_tensor(shift[:, :, ds(c * G, G)], mean[:, ds(c * G, G)].unsqueeze(1).to_broadcast([P, 2, G]),
                                                -1.0, y, ALU.mult, ALU.mult).then_inc(stats.sem, 1)

                def inputs(k, c, v):
                    static = isinstance(c, int)
                    if k == 9:
                        dve.wait_ge(p1_copied.sem, p1_copied.after(c))
                        if not (static and c < 1):
                            dve.wait_ge(split.sem, split.after(c - 1))
                        v_.tensor_tensor(r1[:], Q[1][0:6 * N, :], p1[:], ALU.subtract).then_inc(r1_ready.sem, 1)
                    if k == 11:
                        dve.wait_ge(ez_ready.sem, ez_ready.after(c))
                        if not (static and c < 1):
                            dve.wait_ge(softplus.sem, softplus.after(c - 1))
                        v_.tensor_scalar(tz[:], ez[:], 1.0, 1.0, ALU.add, ALU.subtract).then_inc(tz_ready.sem, 1)

                def times_b(n, c, v):
                    q = n % 2
                    if n == 0:
                        dve.wait_ge(du_ready.sem, du_ready.after(c))
                    dve.wait_ge(b_ready.sem, b_ready.after(c, n + 1))
                    v_.tensor_tensor(dBu[q][:, :, :, 1:L], both(du[v][:]), seqs(Bp[q][:]).unsqueeze(1).to_broadcast([P, 2, 2, S]),
                                     ALU.mult).then_inc(dBu_ready.sem, 1)

                def sums(c, v):
                    dve.wait_ge(summed.sem, summed.after(c))
                    for h in range(2):
                        v_.scalar_tensor_tensor(yg[:, h, :], xi[v][:, h, :], Dp[:, h:h + 1], Yp[h][:], ALU.mult, ALU.add).then_inc(finish.sem, 1)

                def gated(c, v):
                    dve.wait_ge(finish.sem, finish.after(c, 2))
                    v_.tensor_tensor(yg[:], yg[:], gate[v][:], ALU.mult).then_inc(finish.sem, 1)

                def update(c):
                    dve.wait_ge(out_ready.sem, out_ready.after(c))
                    dve.wait_ge(x_added.sem, x_added.after(c))
                    x = X[:, ds(c * CH, CH)]
                    v_.tensor_tensor(x, x, Q[0][:], ALU.add).then_inc(x_updated.sem, 1)

                def scan(c, v, more):
                    static = isinstance(c, int)
                    times_b(0, c, v)
                    for n in range(N):
                        q = n % 2
                        dve.wait_ge(dBu_ready.sem, dBu_ready.after(c, n + 1))
                        dve.wait_ge(dA_ready.sem, dA_ready.after(c, n + 1))
                        if n >= 2:
                            dve.wait_ge(hc_ready.sem, hc_ready.after(c, n - 1))
                        v_.tensor_tensor_scan(flat(Hs[q]), flat(dA[n % NA]), flat(dBu[q]), 0.0, ALU.mult, ALU.add).then_inc(scanned.sem, 1)
                        if n == 0 and not (static and c < 1):
                            sums(c - 1, 1 - v)
                        if n + 1 < N:
                            times_b(n + 1, c, v)
                        dve.wait_ge(scanned.sem, scanned.after(c, n + 1))
                        dve.wait_ge(c_ready.sem, c_ready.after(c, n + 1))
                        if n >= 2:
                            dve.wait_ge(summed.sem, summed.after(c, n - 1))
                        v_.tensor_tensor(both(HC[q][:]), Hs[q][:, :, :, 1:L], seqs(Cp[q][:]).unsqueeze(1).to_broadcast([P, 2, 2, S]),
                                         ALU.mult).then_inc(hc_ready.sem, 1)
                        if more:
                            inputs(n, c + 1, 1 - v)
                        if more > 1:
                            scales_of(n, c + 2)
                        if not (static and c < 1):
                            if n == 0:
                                gated(c - 1, 1 - v)
                            if n == 1:
                                update(c - 1)

                chunks(dve, scan, inputs, stats=scales_of)
                sums(NCH - 1, 1)
                gated(NCH - 1, 1)
                update(NCH - 1)


def build(nc, a, out):
    XG0 = nc.dram_tensor("rows0", [NT * P, D + 1], F32, kind="Internal").ap()
    XG1 = nc.dram_tensor("rows1", [NT * P, D], F32, kind="Internal").ap()
    Y0 = nc.dram_tensor("out_rows0", [NT * P, D], F32, kind="Internal").ap()
    Y1 = nc.dram_tensor("out_rows1", [NT * P, D], F32, kind="Internal").ap()
    with ExitStack() as outer:
        g = Maker(nc, outer, "g_")
        X = g.sb("X", [P, T * D])
        mean, scales = g.sb("mean", [P, T]), g.sb("scales", [P, 2, T])
        ident = g.sb("ident", [P, P])
        tri, ones = g.sb("tri", [P, P], BF16), g.sb("ones", [P, P], BF16)
        rev = g.sb("rev", [P, E])
        row_of_tile = g.sb("row_of_tile", [1, NT])
        Z = g.sb("Z", [P, D + 1])
        rt = Routing(g)
        LGT = g.sb("LGT", [P, T, E])
        w1 = MixtureWeights(g, "m1_", a, None, "w_router1", "gate_b1", ("w_up1", "w_down1"), T, H1, ("b_up1", "b_down1"))
        w_in, conv_w, conv_b = g.sb("w_in", [P, 4 * P]), g.sb("conv_w", [P, 2, 4]), g.sb("conv_b", [P, 2])
        w_lr, w_bc, w_dt = g.sb("w_lr", [P, 2, DT]), g.sb("w_bc", [P, 2, 6 * N]), g.sb("w_dt", [DT, DI])
        dt_b, A, Dp, w_out = g.sb("dt_b", [P, 2]), g.sb("A", [P, 2, N]), g.sb("Dp", [P, 2]), g.sb("w_out", [P, 2, D])
        norm_w = g.sb("norm_w", [P, 1])
        sel = g.sb("sel", [6 * N, 2 * N, P], BF16)
        ss_pairs = [(w_in[:], a["w_in"]), (conv_w[:], a["conv_w"]), (conv_b[:], a["conv_b"]), (w_lr[:], a["w_lr"]),
                    (w_bc[:], a["w_bc"]), (w_dt[:], a["w_dt"]), (dt_b[:], a["dt_b"]), (A[:], a["A_log"]),
                    (Dp[:], a["Dp"]), (w_out[:], a["w_out"]), (norm_w[:], a["norm_w"]), (sel[:], a["sel"])]
        cleared, zeroed = g.sem("cleared"), g.sig("zeroed", 16)
        x_loaded, first_loaded, ss_loaded = g.sig("x_loaded", 16), g.sig("first_loaded", 16), g.sig("ss_loaded", 16)
        chain = g.sig("chain")
        stat_signals = (chain, g.sig("shifted"), g.sig("rooted"))
        front = outer.enter_context(ExitStack())
        w0 = MixtureWeights(Maker(nc, front, "g_"), "m0_", a, "norm0", "w_router0", None, ("w_up0", "w_down0"), 0, H0, None)
        with ExitStack() as ctx:
            m = Maker(nc, ctx, "a_")
            w = m.sb("w", [P, 9 * P + IH])
            bias, b_iw, rope = m.sb("bias", [P, 8]), m.sb("b_iw", [P, IH]), m.sb("rope", [P, 2 * S])
            b_o = m.sb("b_o", [P, D])
            xd = a["x"].rearrange("(t p) d -> p t d", p=P)
            first = [(ident[:], a["ident"]), (tri[:], a["tri"]), (ones[:], a["ones"]), (rev[:], a["rev"]),
                     (row_of_tile[:], a["row_of_tile"]),
                     (w[:], a["w_attn"]), (bias[:], a["b_attn"]), (b_iw[:], a["b_iw"]), (rope[:], a["rope"]),
                     (b_o[:], a["b_o"])]
            with nc.Block() as block:
                @block.gpsimd
                def _(pool):
                    nc.gpsimd.memset(Z[:], 0.0).then_inc(cleared, 1)

                @block.sync
                def _(sp):
                    for t in range(0, T, 8):
                        sp.dma_start(X[:, t * D:(t + 8) * D].rearrange("p (t d) -> p t d", d=D), xd[:, t:t + 8, :]).then_inc(x_loaded.sem, 16)
                    for dst, src in first:
                        sp.dma_start(dst, src).then_inc(first_loaded.sem, 16)
                    sp.wait_ge(x_loaded.sem, x_loaded.after(T // 8 - 1))
                    for dst, src in w0.pairs:
                        sp.dma_start(dst, src).then_inc(w0.loaded.sem, 16)
                    sp.wait_ge(cleared, 1)
                    for XG in (XG0, XG1):
                        sp.dma_start(XG.rearrange("(t p) d -> p t d", p=P),
                                     Z[:, 0:XG.shape[1]].unsqueeze(1).to_broadcast([P, NT, XG.shape[1]])).then_inc(zeroed.sem, 16)
                    for dst, src in ss_pairs:
                        sp.dma_start(dst, src).then_inc(ss_loaded.sem, 16)
                    for dst, src in w1.pairs:
                        sp.dma_start(dst, src).then_inc(w1.loaded.sem, 16)
            row_stats(nc, "n0_", *stat_signals, X, mean, scales, None)
            wait_loaded(nc, first_loaded, len(first))
            attention(nc, X, mean, scales, ident, w, bias, b_iw, rope)
            with nc.Block() as block:
                @block.vector
                def _(dve):
                    x = X[:].rearrange("p (t d) -> p t d", d=D)
                    nc.vector.tensor_tensor(x, x, b_o[:].unsqueeze(1).to_broadcast([P, T, D]), ALU.add)
        wait_loaded(nc, zeroed, 2)

        def mixture(tag, w, XG, Y, skip, gated, out):
            with ExitStack() as ctx:
                m = Maker(nc, ctx, tag)
                wait_loaded(nc, w.loaded, len(w.pairs))
                XS = m.sb("XS", [P, T, XG.shape[1]])
                XL = m.sb("XL", [P, T * D]) if skip else None
                router(nc, tag + "r_", X, XL, XS, skip, mean, scales, w.ns is not None, w.ns, w.wr, ident, LGT)
                route(nc, tag + "q_", chain, LGT, w.gb, rt, tri, ones, rev, None, row_of_tile)
                experts(nc, tag + "x_", X, XS, rt, XG, Y, w.n_shared, w.ns, w.wu, w.wd, w.H, gated, w.bu, w.bd, ident)
                if out is not None:
                    combine(nc, tag + "c_", X, rt, Y, out)

        row_stats(nc, "n1_", *stat_signals, X, mean, scales, 1e-6)
        mixture("m0_", w0, XG0, Y0, True, True, None)
        front.close()
        with ExitStack() as ctx:
            m = Maker(nc, ctx, "s_")
            powered = m.sem("powered")
            w_conv = m.sb("w_conv", [P, 2, 4, P])
            wait_loaded(nc, ss_loaded, len(ss_pairs))
            with nc.Block() as block:
                @block.scalar
                def _(act):
                    nc.scalar.activation(A[:], A[:], ACT.Exp).then_inc(powered, 1)

                @block.vector
                def _(dve):
                    for h in range(2):
                        for q in range(4):
                            nc.vector.tensor_scalar(w_conv[:, h, q, :], ident[:], conv_w[:, h, q:q + 1], None, ALU.mult)
                    dve.wait_ge(powered, 1)
                    nc.vector.tensor_scalar(A[:], A[:], -1.0, None, ALU.mult)
            state_space(nc, X, rt, Y0, mean, scales, ident, norm_w, w_in, w_conv, conv_b, w_lr, w_bc, w_dt, dt_b, A, Dp, w_out, sel)
        row_stats(nc, "n3_", *stat_signals, X, mean, scales, None)
        mixture("m1_", w1, XG1, Y1, False, False, out)


def kernel(**inputs):
    import ml_dtypes
    import concourse.bacc as bacc
    from concourse.bass_utils import run_bass_kernel_spmd as run

    i = {k: np.asarray(v) for k, v in inputs.items()}
    f = np.float32
    c = np.ascontiguousarray

    def rows(v):
        return np.broadcast_to(v.reshape(1, -1), (P, v.size))

    def halves(v):
        return v.reshape((2, P) + v.shape[1:]).swapaxes(0, 1)

    wqkv, bqkv = i["L0_attn_w_qkv"], i["L0_attn_b_qkv"]
    swap = np.roll(np.arange(D), -(D // 2))
    q, k, v = wqkv[0:D], wqkv[D:2 * D], wqkv[2 * D:3 * D]
    bq, bk, bv = bqkv[0:D], bqkv[D:2 * D], bqkv[2 * D:3 * D]
    wiq, wik = i["L0_attn_w_iq"], i["L0_attn_w_ik"]
    biq, bik = i["L0_attn_b_iq"], i["L0_attn_b_ik"]
    w_attn = np.concatenate([q, k, q[swap], k[swap], wiq, wik, wik, v, i["L0_attn_w_iw"], i["L0_attn_w_o"]], 0).T
    b_attn = np.stack([bq, bk, bq[swap], bk[swap], biq[0:D], biq[D:2 * D], np.concatenate([bik, bik]), bv], 1)
    half = D // 2
    inv_freq = (f(1.0) / f(10000.0) ** (np.arange(half, dtype=f) / f(half))).astype(f)
    ang = (np.arange(S, dtype=f)[:, None] * inv_freq[None, :]).astype(f)
    cos, sin = np.cos(ang).T.astype(f), np.sin(ang).T.astype(f)
    rope = np.concatenate([np.concatenate([cos, cos], 0), np.concatenate([-sin, sin], 0)], 1)
    sel = np.zeros((6 * N, 2 * N, P), ml_dtypes.bfloat16)
    for n in range(2 * N):
        sel[n::2 * N, n, :] = 1
    xp = i["L1_attn_x_proj_w"]
    bc = xp[:, DT:DT + 2 * N]
    w13 = np.concatenate([np.concatenate([i["L1_ffn_w1"], i["L1_ffn_w3"]], 2),
                          np.concatenate([i["L1_ffn_sw1"], i["L1_ffn_sw3"]], 1)[None]], 0)
    b13 = np.concatenate([np.concatenate([i["L1_ffn_b1"], i["L1_ffn_b3"]], 1),
                          np.concatenate([i["L1_ffn_sb1"], i["L1_ffn_sb3"]], 0)[None]], 0)
    arrays = {
        "x": i["L0_attn_x"].reshape(B * S, D),
        "ident": np.eye(P, dtype=f),
        "tri": np.triu(np.ones((P, P), f), 1).astype(ml_dtypes.bfloat16),
        "ones": np.ones((P, P), ml_dtypes.bfloat16),
        "rev": rows(np.arange(E, 0, -1).astype(f)),
        "row_of_tile": np.arange(NT, dtype=f).reshape(1, NT),
        "w_attn": w_attn, "b_attn": b_attn, "b_iw": rows(i["L0_attn_b_iw"]), "rope": rope, "b_o": rows(i["L0_attn_b_o"]),
        "norm0": i["L0_ffn_norm_scale"].reshape(P, 1),
        "w_router0": i["L0_ffn_w_router"].T,
        "w_up0": i["L0_ffn_w_up"].transpose(2, 0, 1).reshape(D, E * 2 * H0),
        "w_down0": i["L0_ffn_w_down"].transpose(0, 2, 1),
        "w_in": i["L1_attn_in_proj_w"],
        "conv_w": halves(i["L1_attn_conv_w"][:, 0, :]),
        "conv_b": halves(i["L1_attn_conv_b"]),
        "w_lr": halves(xp[:, 0:DT]),
        "w_bc": halves(np.concatenate([bc, bc, bc], 1)),
        "w_dt": i["L1_attn_dt_proj_w"],
        "dt_b": halves(i["L1_attn_dt_proj_b"]),
        "A_log": halves(i["L1_attn_A_log"]),
        "Dp": halves(i["L1_attn_D"]),
        "w_out": halves(i["L1_attn_out_proj_w"]),
        "norm_w": i["L1_attn_norm_w"].reshape(P, 1),
        "sel": sel,
        "w_router1": i["L1_ffn_gate_w"].T,
        "gate_b1": rows(i["L1_ffn_gate_b"]),
        "w_up1": w13.transpose(1, 0, 2).reshape(D, (E + 1) * 2 * H1),
        "w_down1": np.concatenate([i["L1_ffn_w2"], i["L1_ffn_sw2"][None]], 0),
        "b_up1": rows(b13), "b_down1": rows(np.concatenate([i["L1_ffn_b2"], i["L1_ffn_sb2"][None]], 0)),
    }
    nc = bacc.Bacc("TRN2", target_bir_lowering=False, num_devices=1)
    arrays = {"in_" + n: c(v) for n, v in arrays.items()}
    a = {n[3:]: nc.dram_tensor(n, v.shape, mybir.dt.from_np(v.dtype), kind="ExternalInput").ap() for n, v in arrays.items()}
    out = nc.dram_tensor("out", [B * S, D], F32, kind="ExternalOutput").ap()
    build(nc, a, out)
    r = run(nc, [arrays], core_ids=[0])
    return r.results[0]["out"].reshape(B, S, D)
```

```python
import math
from contextlib import ExitStack

import numpy as np
import concourse.bass as bass
from concourse import mybir

F32 = mybir.dt.float32
BF16 = mybir.dt.bfloat16
I32 = mybir.dt.int32
ALU = mybir.AluOpType
ACT = mybir.ActivationFunctionType
AX = mybir.AxisListType

B, S, D = 16, 256, 128
P = 128
T = B * S // P
TOPK = 32
IH, ID = 4, 64
E = 8
H0, H1 = 352, 176
HT = T // 2
NH = 2 * HT + E
NT = 2 * NH
DI, N, DT = 256, 16, 64
BIG = 3.0e38
EPS = 1e-5
ds = bass.ds


class Signal:

    def __init__(self, sem, per):
        self.sem, self.per, self.base = sem, per, 0

    def after(self, unit, k=None):
        return self.base + unit * self.per + (self.per if k is None else k)

    def over(self, units):
        self.base += units * self.per


class Chain:

    def __init__(self, eng, done):
        self.eng, self.done = eng, done

    def __call__(self, ins):
        ins.then_inc(self.done.sem, 1)
        self.eng.wait_ge(self.done.sem, self.done.after(0))
        self.done.over(1)


class Maker:
    def __init__(self, nc, ctx, tag):
        self.nc, self.ctx, self.tag = nc, ctx, tag

    def sb(self, name, shape, dt=F32):
        return self.ctx.enter_context(self.nc.sbuf_tensor(self.tag + name, shape, dt))

    def ps(self, name, shape, dt=F32):
        return self.ctx.enter_context(self.nc.psum_tensor(self.tag + name, shape, dt))

    def sem(self, name):
        return self.ctx.enter_context(self.nc.semaphore(self.tag + name))

    def sig(self, name, per=1):
        return Signal(self.sem(name), per)


def wait_loaded(nc, loaded, count):
    with nc.Block() as block:
        @block.sync
        def _(sp):
            sp.wait_ge(loaded.sem, loaded.after(count - 1))


def row_stats(nc, tag, chain, shifted, rooted, X, mean, scales, eps2, loads=None, x_loaded=(), shift=None):
    n = 1 if eps2 is None else 2
    with ExitStack() as ctx:
        m = Maker(nc, ctx, tag)
        st, mv = m.sb("st", [P, T, 6]), m.sb("mv", [P, T, 2])
        ve, t2 = m.sb("ve", [P, n, T]), m.sb("t2", [P, n, T])
        with nc.Block() as block:
            if loads is not None:
                @block.sync
                def _(sp):
                    loads(sp)

            @block.vector
            def _(dve):
                link = Chain(dve, chain)
                for t in range(T):
                    if x_loaded and t % (T // len(x_loaded)) == 0:
                        dve.wait_ge(x_loaded[t * len(x_loaded) // T], 16)
                    ins = nc.vector.bn_stats(st[:, t, :], X[:, t * D:(t + 1) * D])
                link(ins)
                for t in range(T):
                    ins = nc.vector.bn_aggr(mv[:, t, :], st[:, t, :])
                link(ins)
                if n == 2:
                    nc.vector.tensor_scalar(ve[:, 1, :], mv[:, :, 1], 1.0 + eps2, eps2 * EPS, ALU.mult, ALU.add)
                nc.vector.tensor_scalar(ve[:, 0, :], mv[:, :, 1], EPS, None, ALU.add).then_inc(shifted.sem, 1)
                nc.vector.tensor_copy(mean[:], mv[:, :, 0])
                out = scales[:, 0:n, :]
                dve.wait_ge(rooted.sem, rooted.after(0))
                link(nc.vector.reciprocal(out, t2[:]))
                link(nc.vector.tensor_tensor(t2[:], out, out, ALU.mult))
                link(nc.vector.tensor_tensor(t2[:], t2[:], ve[:], ALU.mult))
                link(nc.vector.tensor_scalar(t2[:], t2[:], -0.5, 1.5, ALU.mult, ALU.add))
                link(nc.vector.tensor_tensor(out, out, t2[:], ALU.mult))
                if shift is not None:
                    nc.vector.scalar_tensor_tensor(shift[:], mean[:], -1.0, scales[:, 0, :], ALU.mult, ALU.mult)

            @block.scalar
            def _(act):
                act.wait_ge(shifted.sem, shifted.after(0))
                nc.scalar.activation(t2[:], ve[:], ACT.Sqrt).then_inc(rooted.sem, 1)
        shifted.over(1)
        rooted.over(1)


def attention(nc, X, shift, scales, ident, w, bias, b_iw, b_o, rope, loads, clear):
    with ExitStack() as ctx:
        m = Maker(nc, ctx, "at_")
        W2 = 2 * P
        Xn = [m.sb(f"Xn{v}", [P, W2]) for v in range(2)]
        xT = [m.sb(f"xT{v}", [P, W2]) for v in range(2)]
        RP = [m.sb(f"RP{v}", [P, 4 * S]) for v in range(2)]
        QK = [m.sb(f"QK{v}", [P, 2 * S]) for v in range(2)]
        IQ = [m.sb(f"IQ{v}", [P, 2 * S]) for v in range(2)]
        IKV = [m.sb(f"IKV{v}", [P, 2 * S]) for v in range(2)]
        VO = [m.sb(f"VO{q}", [P, 2 * D]) for q in range(4)]
        IW = [m.sb(f"IW{v}", [P, 2, IH]) for v in range(2)]
        R = [m.sb(f"R{t}", [P, IH * S]) for t in range(2)]
        WK = [m.sb(f"WK{v}", [P, 2 * S]) for v in range(2)]
        MK = [m.sb(f"MK{v}", [P, 2 * S]) for v in range(2)]
        PR = [m.sb(f"PR{v}", [P, 2 * S]) for v in range(2)]
        PT = [m.sb(f"PT{v}", [P, 2 * S]) for v in range(2)]
        M8 = m.sb("M8", [P, 2, 8])
        mx = [m.sb(f"mx{v}", [P, 2]) for v in range(2)]
        rsum = [m.sb(f"rsum{v}", [P, 2]) for v in range(2)]
        rinv = [m.sb(f"rinv{v}", [P, 2]) for v in range(2)]
        bank = [m.ps(f"b{k}", [P, 512]) for k in range(5)]
        SC0 = m.ps("SC0", [P, 1024])
        LG = m.ps("LG", [P, 512])
        b0, b12a, b12b, b3, b4 = bank
        scale = float(1.0 / np.sqrt(np.float32(D)))

        xn_ready = m.sig("xn_ready", 2)
        xT_ready = m.sig("xT_ready")
        xT_copied = m.sig("xT_copied")
        qk_ready = m.sig("qk_ready")
        iq_ready = m.sig("iq_ready")
        ikv_ready = m.sig("ikv_ready")
        rope_parts = m.sig("rope_parts", 4)
        qk_sum = m.sig("qk_sum")
        iq_copied = m.sig("iq_copied", 2)
        ikv_copied = m.sig("ikv_copied", 2)
        vo_ready = m.sig("vo_ready")
        vo_copied = m.sig("vo_copied")
        iw_copied = m.sig("iw_copied")
        scores_ready = m.sig("scores_ready", 2)
        relu_ready = m.sig("relu_ready", 2)
        logits_ready = m.sig("logits_ready")
        idx = m.sig("idx", 8)
        topk = m.sig("topk", 16)
        penalty = m.sig("penalty")
        masked = m.sig("masked", 2)
        negmax = m.sig("negmax")
        probs_ready = m.sig("probs_ready", 2)
        rinv_ready = m.sig("rinv_ready")
        pT_ready = m.sig("pT_ready")
        pT_copied = m.sig("pT_copied")
        av_ready = m.sig("av_ready")
        x_updated = m.sig("x_updated", 2)
        passed = m.sem("passed")
        skipped, b_added = m.sem("skipped"), m.sig("b_added")

        def steps(eng, step):
            step(0, 0, True, False, False)
            step(1, 1, True, True, False)
            with eng.Fori(0, (B - 4) // 4) as i:
                for k in range(4):
                    step(4 * i + 2 + k, (2 + k) % 4, True, True, True)
            step(B - 2, 2, True, True, True)
            step(B - 1, 3, True, True, True)
            step(B, 0, False, True, True)
            step(B + 1, 1, False, False, True)

        def col(k):
            return w[:, k * P:(k + 1) * P]

        with nc.Block() as block:
            @block.sync
            def _(sp):
                loads(sp)

            @block.tensor
            def _(pe):
                def step(s, q, front, middle, tail):
                    v = q % 2
                    first = isinstance(s, int)
                    if front:
                        pe.wait_ge(xn_ready.sem, xn_ready.after(s))
                        if not (first and s < 1):
                            pe.wait_ge(iw_copied.sem, iw_copied.after(s - 1))
                        for t in range(2):
                            ins = nc.tensor.transpose(b0[:, t * P:(t + 1) * P], Xn[v][:, t * P:(t + 1) * P], ident[:])
                        ins.then_inc(xT_ready.sem, 1)
                        pe.wait_ge(xT_copied.sem, xT_copied.after(s))
                        if not (first and s < 1):
                            pe.wait_ge(relu_ready.sem, relu_ready.after(s - 1, 2))
                        for k in range(4):
                            dst = (b12a, b12b)[k // 2][:, k % 2 * S:(k % 2 + 1) * S]
                            ins = nc.tensor.matmul(dst, col(k), xT[v][:], start=True, stop=True)
                        ins.then_inc(qk_ready.sem, 1)
                        if not (first and s < 3):
                            pe.wait_ge(pT_copied.sem, pT_copied.after(s - 3))
                        for k in range(2):
                            ins = nc.tensor.matmul(b3[:, k * S:(k + 1) * S], col(4 + k), xT[v][:], start=True, stop=True)
                        ins.then_inc(iq_ready.sem, 1)
                        for k in range(2):
                            ins = nc.tensor.matmul(b0[:, k * S:(k + 1) * S], col(6 + k), xT[v][:], start=True, stop=True)
                        ins.then_inc(ikv_ready.sem, 1)
                    if middle:
                        u = 1 - v
                        pe.wait_ge(qk_sum.sem, qk_sum.after(s - 1))
                        if not (first and s < 2):
                            pe.wait_ge(masked.sem, masked.after(s - 2))
                        for t in range(2):
                            ins = nc.tensor.matmul(LG[:, t * S:(t + 1) * S], QK[u][:, t * P:(t + 1) * P],
                                                   QK[u][:, S:2 * S], start=True, stop=True)
                        ins.then_inc(logits_ready.sem, 1)
                    if front:
                        pe.wait_ge(ikv_copied.sem, ikv_copied.after(s))
                        for t in range(2):
                            nc.tensor.matmul(b0[:, t * D:(t + 1) * D], IKV[v][:, S + t * P:S + (t + 1) * P],
                                             w[:, 8 * P + IH:9 * P + IH], start=True, stop=True)
                        for t in range(2):
                            ins = nc.tensor.matmul(b0[:, W2 + t * IH:W2 + (t + 1) * IH], xT[v][:, t * P:(t + 1) * P],
                                                   w[:, 8 * P:8 * P + IH], start=True, stop=True)
                        ins.then_inc(vo_ready.sem, 1)
                        pe.wait_ge(iq_copied.sem, iq_copied.after(s))
                    for t in range(2):
                        if front:
                            if t == 0:
                                if not (first and s < 1):
                                    pe.wait_ge(relu_ready.sem, relu_ready.after(s - 1, 1))
                            else:
                                pe.wait_ge(rope_parts.sem, rope_parts.after(s))
                            for h in range(IH):
                                r, c = h % 2 * ID, h // 2 * S
                                dst = SC0[:, h % 2 * 512 + c:h % 2 * 512 + c + S] if t == 0 else (b12a, b12b)[h % 2][:, c:c + S]
                                ins = nc.tensor.matmul(dst, IQ[v][r:r + ID, h // 2 * S + t * P:h // 2 * S + (t + 1) * P],
                                                       IKV[v][r:r + ID, 0:S], start=True, stop=True)
                            ins.then_inc(scores_ready.sem, 1)
                        if tail and t == 0:
                            pe.wait_ge(probs_ready.sem, probs_ready.after(s - 2))
                            for r in range(2):
                                for c in range(2):
                                    ins = nc.tensor.transpose(b3[:, c * S + r * P:c * S + (r + 1) * P],
                                                              PR[v][:, r * S + c * P:r * S + (c + 1) * P], ident[:])
                            ins.then_inc(pT_ready.sem, 1)
                    if tail:
                        pe.wait_ge(pT_copied.sem, pT_copied.after(s - 2))
                        if not (first and s < 3):
                            pe.wait_ge(x_updated.sem, x_updated.after(s - 3))
                        for t in range(2):
                            for c in range(2):
                                ins = nc.tensor.matmul(b4[:, t * D:(t + 1) * D], PT[v][:, c * S + t * P:c * S + (t + 1) * P],
                                                       VO[(q + 2) % 4][:, c * D:(c + 1) * D], start=c == 0, stop=c == 1)
                        ins.then_inc(av_ready.sem, 1)

                steps(pe, step)

            @block.scalar
            def _(act):
                def normalise(s, v):
                    for t in range(2):
                        nc.scalar.activation(Xn[v][:, t * D:(t + 1) * D], X[:, ds(s * W2 + t * D, D)], ACT.Identity,
                                             bias=shift[:, ds(s * 2 + t, 1)],
                                             scale=scales[:, 0, ds(s * 2 + t, 1)]).then_inc(xn_ready.sem, 1)

                normalise(0, 0)

                def step(s, q, front, middle, tail):
                    v = q % 2
                    first = isinstance(s, int)
                    if front:
                        act.wait_ge(xT_ready.sem, xT_ready.after(s))
                        nc.scalar.activation(xT[v][:], b0[:, 0:W2], ACT.Copy).then_inc(xT_copied.sem, 1)
                        act.wait_ge(iq_ready.sem, iq_ready.after(s))
                        for k in range(2):
                            nc.scalar.activation(IQ[v][:, k * S:(k + 1) * S], b3[:, k * S:(k + 1) * S], ACT.Identity,
                                                 bias=bias[:, 4 + k:5 + k]).then_inc(iq_copied.sem, 1)
                        act.wait_ge(ikv_ready.sem, ikv_ready.after(s))
                        for k in range(2):
                            nc.scalar.activation(IKV[v][:, k * S:(k + 1) * S], b0[:, k * S:(k + 1) * S], ACT.Identity,
                                                 bias=bias[:, 6 + k:7 + k]).then_inc(ikv_copied.sem, 1)
                        act.wait_ge(vo_ready.sem, vo_ready.after(s))
                        nc.scalar.activation(VO[q][:], b0[:, 0:W2], ACT.Copy).then_inc(vo_copied.sem, 1)
                        if not (first and s == B - 1):
                            normalise(s + 1, 1 - v)
                    if tail:
                        act.wait_ge(negmax.sem, negmax.after(s - 2))
                        for t in range(2):
                            nc.scalar.activation(PR[v][:, t * S:(t + 1) * S], MK[v][:, t * S:(t + 1) * S], ACT.Exp,
                                                 bias=mx[v][:, t:t + 1], scale=scale,
                                                 accum_out=rsum[v][:, t:t + 1]).then_inc(probs_ready.sem, 1)
                    for t in range(2):
                        if front:
                            act.wait_ge(scores_ready.sem, scores_ready.after(s, t + 1))
                            if not (first and s < 1):
                                act.wait_ge(idx.sem, idx.after(s - 1, 7 + t))
                            if t == 0:
                                nc.scalar.activation(R[t][:], SC0[:], ACT.Relu).then_inc(relu_ready.sem, 1)
                            else:
                                nc.scalar.activation(R[t][:, 0:512], b12a[:], ACT.Relu)
                                nc.scalar.activation(R[t][:, 512:1024], b12b[:], ACT.Relu).then_inc(relu_ready.sem, 1)
                        if tail and t == 0:
                            act.wait_ge(pT_ready.sem, pT_ready.after(s - 2))
                            nc.scalar.activation(PT[v][:], b3[:], ACT.Copy).then_inc(pT_copied.sem, 1)

                steps(act, step)

            @block.vector
            def _(dve):
                def rotate(s, v):
                    dve.wait_ge(qk_ready.sem, qk_ready.after(s))
                    for k in range(4):
                        nc.vector.scalar_tensor_tensor(RP[v][:, k * S:(k + 1) * S],
                                                       (b12a, b12b)[k // 2][:, k % 2 * S:(k % 2 + 1) * S],
                                                       bias[:, k:k + 1], rope[:, k // 2 * S:(k // 2 + 1) * S],
                                                       ALU.add, ALU.mult).then_inc(rope_parts.sem, 1)

                def head_weights(s, v):
                    dve.wait_ge(vo_copied.sem, vo_copied.after(s))
                    nc.vector.tensor_tensor(IW[v][:], b0[:, W2:W2 + 2 * IH].rearrange("p (t h) -> p t h", h=IH),
                                            b_iw[:, :].unsqueeze(1).to_broadcast([P, 2, IH]), ALU.add).then_inc(iw_copied.sem, 1)

                def index_scores(s, v):
                    dve.wait_ge(iw_copied.sem, iw_copied.after(s))
                    for h in range(IH):
                        for t in range(2):
                            dst = WK[v][:, t * S:(t + 1) * S]
                            src = R[t][:, h % 2 * 512 + h // 2 * S:h % 2 * 512 + (h // 2 + 1) * S]
                            if h == 0:
                                dve.wait_ge(relu_ready.sem, relu_ready.after(s, t + 1))
                                ins = nc.vector.tensor_scalar(dst, src, IW[v][:, t, h:h + 1], None, ALU.mult)
                            else:
                                dve.wait_ge(idx.sem, idx.after(s, 2 * h - 1 + t))
                                ins = nc.vector.scalar_tensor_tensor(dst, src, IW[v][:, t, h:h + 1], dst, ALU.mult, ALU.add)
                            ins.then_inc(idx.sem, 1)

                def choose(s, v, rounds):
                    for k in rounds:
                        for t in range(2):
                            dst = WK[v][:, t * S:(t + 1) * S]
                            if k == 0:
                                dve.wait_ge(idx.sem, idx.after(s, 7 + t))
                                dve.sem_inc(passed, 1)
                            else:
                                dve.wait_ge(topk.sem, topk.after(s, 4 * k - 1 + t))
                                dve.sem_inc(passed, 1)
                            nc.vector.max(M8[:, t, :], dst).then_inc(topk.sem, 1)
                        for t in range(2):
                            dst = WK[v][:, t * S:(t + 1) * S]
                            dve.wait_ge(topk.sem, topk.after(s, 4 * k + 1 + t))
                            dve.sem_inc(passed, 1)
                            nc.vector.match_replace(dst, M8[:, t, :], dst, -BIG).then_inc(topk.sem, 1)

                def mask(s, v):
                    dve.wait_ge(topk.sem, topk.after(s))
                    nc.vector.tensor_scalar(WK[v][:], WK[v][:], -BIG, -BIG, ALU.is_gt, ALU.mult).then_inc(penalty.sem, 1)
                    dve.wait_ge(penalty.sem, penalty.after(s))
                    dve.wait_ge(logits_ready.sem, logits_ready.after(s))
                    dve.sem_inc(passed, 1)
                    for t in range(2):
                        c = slice(t * S, (t + 1) * S)
                        nc.vector.tensor_tensor_reduce(MK[v][:, c], WK[v][:, c], LG[:, c], 1.0, -BIG, ALU.add, ALU.max,
                                                       accum_out=mx[v][:, t:t + 1]).then_inc(masked.sem, 1)
                    dve.wait_ge(masked.sem, masked.after(s))
                    nc.vector.tensor_scalar(mx[v][:], mx[v][:], -scale, None, ALU.mult).then_inc(negmax.sem, 1)

                def update(s, v):
                    dve.wait_ge(probs_ready.sem, probs_ready.after(s))
                    nc.vector.reciprocal(rinv[v][:], rsum[v][:]).then_inc(rinv_ready.sem, 1)
                    dve.wait_ge(rinv_ready.sem, rinv_ready.after(s))
                    dve.wait_ge(av_ready.sem, av_ready.after(s))
                    dve.wait_ge(b_added.sem, b_added.after(s))
                    for t in range(2):
                        x = X[:, ds(s * W2 + t * D, D)]
                        nc.vector.scalar_tensor_tensor(x, b4[:, t * D:(t + 1) * D], rinv[v][:, t:t + 1], x,
                                                       ALU.mult, ALU.add).then_inc(x_updated.sem, 1)

                def step(s, q, front, middle, tail):
                    v = q % 2
                    u = 1 - v
                    if middle:
                        index_scores(s - 1, u)
                        choose(s - 1, u, range(0, 1))
                    if front:
                        rotate(s, v)
                    if middle:
                        choose(s - 1, u, range(1, 3))
                    if middle:
                        choose(s - 1, u, range(3, TOPK // 8))
                    if front:
                        head_weights(s, v)
                    if middle:
                        mask(s - 1, u)
                    if tail:
                        update(s - 2, v)

                steps(dve, step)

            @block.gpsimd
            def _(pool):
                clear()

                def step(s, q, front, middle, tail):
                    v = q % 2
                    if front:
                        pool.wait_ge(xn_ready.sem, xn_ready.after(s))
                        pool.sem_inc(skipped, 1)
                        x = X[:, ds(s * W2, W2)].rearrange("p (t d) -> p t d", d=D)
                        nc.gpsimd.tensor_tensor(x, x, b_o[:].unsqueeze(1).to_broadcast([P, 2, D]), ALU.add).then_inc(b_added.sem, 1)
                        pool.wait_ge(rope_parts.sem, rope_parts.after(s))
                        if not (isinstance(s, int) and s < 2):
                            pool.wait_ge(logits_ready.sem, logits_ready.after(s - 2))
                        nc.gpsimd.tensor_tensor(QK[v][:], RP[v][:, 0:2 * S], RP[v][:, 2 * S:4 * S], ALU.add).then_inc(qk_sum.sem, 1)

                steps(pool, step)


class MixtureWeights:

    def __init__(self, g, tag, a, norm, w_router, gate_b, weights, n_shared, H, biases):
        self.H, self.n_shared = H, n_shared
        self.loaded = g.sig(tag + "loaded", 16)
        NC = -(-H // P)
        ne = E + bool(n_shared)
        self.wr = g.sb(tag + "wr", [P, E])
        self.step, self.bias_step = 2 * H + NC * D, 2 * H + D
        self.w = g.sb(tag + "w", [P, ne * self.step])
        each = self.w[:].rearrange("p (e n) -> p e n", e=ne)
        self.pairs = [(self.wr[:], a[w_router]), (each[:, :, 0:2 * H], a[weights[0]])]
        tail = H - (NC - 1) * P
        src = a[weights[1]]
        for c in range(NC):
            n = P if c < NC - 1 else tail
            self.pairs.append((each[0:n, :, 2 * H + c * D:2 * H + (c + 1) * D], src[:, c * P:c * P + n, :].rearrange("e p d -> p e d")))
        self.ns = self.gb = self.b = None
        if norm:
            self.ns = g.sb(tag + "ns", [P, 1])
            self.pairs.append((self.ns[:], a[norm]))
        if gate_b:
            self.gb = g.sb(tag + "gb", [P, E])
            self.pairs.append((self.gb[:], a[gate_b]))
        if biases:
            self.b = g.sb(tag + "b", [P, ne * self.bias_step])
            self.pairs.append((self.b[:], a[biases]))


class Routing:

    def __init__(self, m):
        self.c = [m.sb(f"c{k}", [P, T]) for k in range(2)]
        self.slot = [m.sb(f"slot{k}", [P, T], I32) for k in range(2)]
        self.tile_weights = m.sb("tile_weights", [1, NT], I32)
        self.tile_biases = m.sb("tile_biases", [1, NT], I32)


def route(nc, tag, chain, signals, LGT, w, rt, tri, ones, rev, masks, tile_of_half):
    with ExitStack() as ctx:
        m = Maker(nc, ctx, tag)
        shape = [P, T, E]
        ex, pr, eq, eq1 = m.sb("ex", shape), m.sb("pr", shape), m.sb("eq", shape), m.sb("eq1", shape)
        oh = [m.sb(f"oh{k}", shape) for k in range(2)]
        mt = m.sb("mt", shape, BF16)
        kb = m.sb("kb", shape)
        tot, run, base = m.sb("tot", [P, E, T]), m.sb("run", [P, E, T]), m.sb("base", [P, E, T])
        mx, mx1, sm = m.sb("mx", [P, T]), m.sb("mx1", [P, T]), m.sb("sm", [P, T])
        n_i, ct, end, st = m.sb("n_i", [P, 2, E], I32), m.sb("ct", [P, 2, E]), m.sb("end", [P, 2, E]), m.sb("st", [P, 2, E])
        cmp = m.sb("cmp", [1, 2, NH, E])
        te = m.sb("te", [1, 2, NH])
        RK = m.ps("RK", [P, T * E])
        TT = m.ps("TT", [P, T * E])
        shifted, powered, marks, ranked = signals

        def each(a):
            return a[:, :].unsqueeze(2).to_broadcast(shape)

        def every(a):
            return a[:, :].unsqueeze(1).to_broadcast(shape)

        def turned(a):
            return a.rearrange("p (t e) -> p e t", e=E)

        with nc.Block() as block:
            @block.vector
            def _(dve):
                v = nc.vector
                link = Chain(dve, chain)

                def softmax():
                    dve.wait_ge(powered.sem, powered.after(0))
                    link(v.tensor_reduce(sm[:], ex[:], AX.X, ALU.add))
                    link(v.reciprocal(sm[:], sm[:]))
                    link(v.tensor_tensor(pr[:], ex[:], each(sm), ALU.mult))

                link(v.tensor_reduce(mx[:], LGT[:], AX.X, ALU.max))
                v.tensor_tensor(ex[:], LGT[:], each(mx), ALU.subtract).then_inc(shifted.sem, 1)
                key = LGT
                if w.gb is not None:
                    softmax()
                    link(v.tensor_tensor(kb[:], pr[:], every(w.gb), ALU.add))
                    link(v.tensor_reduce(mx[:], kb[:], AX.X, ALU.max))
                    key = kb
                for k in range(2):
                    link(v.tensor_tensor(eq[:], key[:], each(mx), ALU.is_equal))
                    link(v.tensor_tensor(eq[:], eq[:], every(rev), ALU.mult))
                    link(v.tensor_reduce(mx[:], eq[:], AX.X, ALU.max))
                    link(v.tensor_tensor(oh[k][:], eq[:], each(mx), ALU.is_equal))
                    if k == 0:
                        link(v.scalar_tensor_tensor(kb[:], oh[0][:], -BIG, key[:], ALU.mult, ALU.add))
                        key = kb
                        link(v.tensor_reduce(mx[:], kb[:], AX.X, ALU.max))
                v.tensor_tensor(mt[:], oh[0][:], oh[1][:], ALU.add).then_inc(marks.sem, 1)
                if w.gb is None:
                    softmax()
                v.tensor_tensor(eq[:], pr[:], oh[0][:], ALU.mult)
                link(v.tensor_tensor(eq1[:], pr[:], oh[1][:], ALU.mult))
                v.tensor_reduce(rt.c[0][:], eq[:], AX.X, ALU.add)
                v.tensor_reduce(rt.c[1][:], eq1[:], AX.X, ALU.add)
                dve.wait_ge(ranked.sem, ranked.after(0))
                link(v.tensor_copy(tot[:], turned(TT[:])))
                link(v.tensor_tensor_scan(run[:].rearrange("p e t -> p (e t)"), masks[:, 0:E * T],
                                          tot[:].rearrange("p e t -> p (e t)"), 0.0, ALU.mult, ALU.add))
                last = run[:].rearrange("p e (h t) -> p h e t", h=2)[:, :, :, HT - 1]
                v.tensor_tensor(base[:], run[:], tot[:], ALU.subtract)
                link(v.tensor_scalar(n_i[:], last, float(P - 1), None, ALU.add))
                link(v.tensor_scalar(n_i[:], n_i[:], int(math.log2(P)), None, ALU.arith_shift_right))
                link(v.tensor_copy(ct[:], n_i[:]))
                v.tensor_tensor(base[:], base[:], turned(RK[:]), ALU.add)
                link(v.tensor_tensor_scan(end[:].rearrange("p h e -> p (h e)"), masks[:, E * T:E * T + 2 * E],
                                          ct[:].rearrange("p h e -> p (h e)"), 0.0, ALU.mult, ALU.add))
                link(v.tensor_tensor(st[:], end[:], ct[:], ALU.subtract))
                link(v.tensor_scalar(st[:, 0, :], st[:, 0, :], float(P), None, ALU.mult))
                link(v.tensor_scalar(st[:, 1, :], st[:, 1, :], float(P), float(NH * P), ALU.mult, ALU.add))
                for h in range(2):
                    ins = v.tensor_tensor(base[:, :, h * HT:(h + 1) * HT], base[:, :, h * HT:(h + 1) * HT],
                                          st[:, h, :].unsqueeze(2).to_broadcast([P, E, HT]), ALU.add)
                link(ins)
                at = base[:].rearrange("p e t -> p t e")
                v.tensor_tensor(eq[:], oh[0][:], at, ALU.mult)
                link(v.tensor_tensor(eq1[:], oh[1][:], at, ALU.mult))
                v.tensor_reduce(mx[:], eq[:], AX.X, ALU.add)
                link(v.tensor_reduce(mx1[:], eq1[:], AX.X, ALU.add))
                v.tensor_copy(rt.slot[0][:], mx[:])
                v.tensor_copy(rt.slot[1][:], mx1[:])
                for h in range(2):
                    ins = v.tensor_tensor(cmp[:, h], end[0:1, h, :].unsqueeze(1).to_broadcast([1, NH, E]),
                                          tile_of_half[:, :].unsqueeze(2).to_broadcast([1, NH, E]), ALU.is_le)
                link(ins)
                link(v.tensor_reduce(te[:], cmp[:], AX.X, ALU.add))
                for dst, step in ((rt.tile_weights, w.step), (rt.tile_biases, w.bias_step)):
                    v.tensor_scalar(dst[:].rearrange("p (h t) -> p h t", h=2), te[:], float(E - 1), float(step), ALU.min, ALU.mult)

            @block.scalar
            def _(act):
                act.wait_ge(shifted.sem, shifted.after(0))
                nc.scalar.activation(ex[:], ex[:], ACT.Exp).then_inc(powered.sem, 1)

            @block.tensor
            def _(pe):
                pe.wait_ge(marks.sem, marks.after(0))
                flat = mt[:].rearrange("p t e -> p (t e)")
                nc.tensor.matmul(RK[:], tri[:], flat, start=True, stop=True)
                nc.tensor.matmul(TT[:], ones[:], flat, start=True, stop=True).then_inc(ranked.sem, 1)
    for signal in signals:
        signal.over(1)


def router(nc, tag, signals, X, XL, XS, add_skip, mean, scales, rms, scale_col, w_router, ident, LGT):
    G = 4
    with ExitStack() as ctx:
        m = Maker(nc, ctx, tag)
        xT = [m.sb(f"xT{v}", [P, G * P]) for v in range(2)]
        TP = [m.ps(f"TP{v}", [P, G * P]) for v in range(2)]
        RP = [m.ps(f"RP{v}", [P, G * E]) for v in range(2)]
        rows = m.sig("rows", 2 * G if add_skip else G)
        added, turned, copied, scored, kept, staged = signals
        ST = [m.sb(f"ST{v}", [P, G * P]) for v in range(2)]
        GN = T // G
        AHEAD = 4

        with nc.Block() as block:
            @block.vector
            def _(dve):
                def keep(g, v):
                    dve.wait_ge(scored.sem, scored.after(g))
                    nc.vector.tensor_copy(LGT[:, ds(g * G, G), :], RP[v][:].rearrange("p (t e) -> p t e", e=E)).then_inc(kept.sem, 1)

                def rows_of(g):
                    for t in range(G):
                        x = X[:, ds((g * G + t) * D, D)]
                        st = ds(g * G + t, 1)
                        if add_skip:
                            nc.vector.tensor_scalar(XL[:, ds((g * G + t) * D, D)], x, mean[:, st], scales[:, 0, st],
                                                    ALU.subtract, ALU.mult).then_inc(rows.sem, 1)
                        nc.vector.tensor_scalar(XS[:, ds(g * G + t, 1), 0:D], x.unsqueeze(1), mean[:, st], scales[:, int(rms), st],
                                                ALU.subtract, ALU.mult).then_inc(rows.sem, 1)

                for g in range(AHEAD):
                    rows_of(g)
                with dve.Fori(0, (GN - AHEAD) // 2) as i:
                    for v in range(2):
                        rows_of(2 * i + AHEAD + v)
                        keep(2 * i + v, v)
                for g in range(GN - AHEAD, GN):
                    keep(g, g % 2)

            @block.gpsimd
            def _(pool):
                if add_skip:
                    with pool.Fori(0, GN) as g:
                        pool.wait_ge(rows.sem, rows.after(g))
                        x = X[:, ds(g * G * D, G * D)]
                        nc.gpsimd.tensor_tensor(x, x, XL[:, ds(g * G * D, G * D)], ALU.add).then_inc(added.sem, 1)

            @block.tensor
            def _(pe):
                def turn(g, v, first=False):
                    pe.wait_ge(staged.sem, staged.after(g))
                    if not first:
                        pe.wait_ge(copied.sem, copied.after(g - 2))
                    for t in range(G):
                        ins = nc.tensor.transpose(TP[v][:, t * P:(t + 1) * P], ST[v][:, t * P:(t + 1) * P], ident[:])
                    ins.then_inc(turned.sem, 1)

                def score(g, v, first=False):
                    pe.wait_ge(copied.sem, copied.after(g))
                    if not first:
                        pe.wait_ge(kept.sem, kept.after(g - 2))
                    for t in range(G):
                        ins = nc.tensor.matmul(RP[v][:, t * E:(t + 1) * E], xT[v][:, t * P:(t + 1) * P], w_router[:],
                                               start=True, stop=True)
                    ins.then_inc(scored.sem, 1)

                turn(0, 0, True)
                turn(1, 1, True)
                score(0, 0, True)
                turn(2, 0)
                score(1, 1, True)
                with pe.Fori(0, (GN - 4) // 2) as i:
                    for v in range(2):
                        turn(2 * i + 3 + v, 1 - v)
                        score(2 * i + 2 + v, v)
                turn(GN - 1, 1)
                score(GN - 2, 0)
                score(GN - 1, 1)

            @block.scalar
            def _(act):
                def stage(g, v, first=False):
                    act.wait_ge(rows.sem, rows.after(g))
                    if not first:
                        act.wait_ge(turned.sem, turned.after(g - 2))
                    nc.scalar.activation(ST[v][:].rearrange("p (t d) -> p t d", d=D), XS[:, ds(g * G, G), 0:D], ACT.Copy).then_inc(staged.sem, 1)

                def copy(g, v, first=False):
                    act.wait_ge(turned.sem, turned.after(g))
                    if not first:
                        act.wait_ge(scored.sem, scored.after(g - 2))
                    if scale_col is not None:
                        ins = nc.scalar.activation(xT[v][:], TP[v][:], ACT.Copy, scale=scale_col[:, 0:1])
                    else:
                        ins = nc.scalar.activation(xT[v][:], TP[v][:], ACT.Copy)
                    ins.then_inc(copied.sem, 1)

                stage(0, 0, True)
                stage(1, 1, True)
                for g in range(2):
                    copy(g, g, True)
                    stage(g + 2, g)
                with act.Fori(0, (GN - 4) // 2) as i:
                    for v in range(2):
                        copy(2 * i + 2 + v, v)
                        stage(2 * i + 4 + v, v)
                for g in range(GN - 2, GN):
                    copy(g, g % 2)
    for signal in signals:
        signal.over(GN)


def experts(nc, tag, X, XS, rt, XG, Y, out, n_early, w, gated, ident):
    n_shared, scale_col, H = w.n_shared, w.ns, w.H
    NX = NT + n_shared
    N0 = 5 * n_shared // 8
    chunks = [(c, min(P, H - c)) for c in range(0, H, P)]
    NC = len(chunks)
    WU = 2 * H
    two = WU > 512
    U = 4
    LAG = 8
    R = 4 * U

    class Tile:

        def __init__(self, j, v, w, shared, shared_before, late, known, name):
            self.j, self.v, self.w, self.shared, self.shared_before = j, v, w, shared, shared_before
            self.i = (j - NT if late else j) if shared else j - N0
            self.known, self.name = known, name

        def has(self, back):
            return self.known is None or self.known >= back

        def raised(self, back):
            if self.known is not None:
                return ((self.known - back) // U + 1) * 16
            return (self.j - back - self.v) * (16 // U) + 16

    def is_shared(j):
        return j < N0 or j >= N0 + NT

    def known_tile(j):
        return Tile(j, j % U, j % R, is_shared(j), is_shared(max(j - U, 0)), j >= N0 + NT, j, j) if 0 <= j < NX else None

    with ExitStack() as ctx:
        m = Maker(nc, ctx, tag)
        G = [m.sb(f"G{v}", [P, D + 1]) for v in range(U)]
        gT = [m.sb(f"gT{v}", [P, P]) for v in range(2)]
        hid = [m.sb(f"hid{v}", [P, H]) for v in range(2)]
        sg = [m.sb(f"sg{v}", [P, WU]) for v in range(2)]
        hT = [m.sb(f"hT{v}", [P, NC * P]) for v in range(2)]
        YO = [m.sb(f"YO{v}", [P, D]) for v in range(U)]
        UP = [m.ps(f"UP{v}", [P, 1024 if two else 512]) for v in range(2)]
        TP = m.ps("TP", [P, 512])
        HP = m.ps("HP", [P, 512])
        DP = [m.ps(f"DP{v}", [P, 512]) for v in range(2)]
        weight = m.sb("weight", [P, R])
        sent, reweighted, placed = m.sem("sent"), m.sem("reweighted"), m.sem("placed")
        fetched = m.sem("fetched")
        W = 4
        got = [m.sem(f"got{q}") for q in range(HT // W if out is not None else 0)]
        pairs = m.sb("pairs", [P, HT * D]) if out is not None else None
        if out is None:
            early = m.sem("early")
        else:
            y_summed, biased, x_added = m.sig("y_summed"), m.sig("biased"), m.sig("x_added")
            joined, x_joined, last_joined = m.sem("joined"), m.sem("x_joined"), m.sem("last_joined")
            out_stored, last_stored = m.sem("out_stored"), m.sem("last_stored")
        arrived = [m.sem(f"arrived{v}") for v in range(U)]
        stored = [m.sem(f"stored{v}") for v in range(U)]
        turned = m.sig("turned")
        t_copied = m.sig("t_copied")
        up_ready = m.sig("up_ready")
        multiplied = m.sig("multiplied")
        silu_ready = m.sig("silu_ready")
        h_ready = multiplied if gated else silu_ready
        h_turned = m.sig("h_turned")
        h_copied = m.sig("h_copied")
        down_ready = m.sig("down_ready")
        y_ready = m.sig("y_ready")
        up_cols = [(0, 0, H), (512, H, H)] if two else [(0, 0, WU)]
        def place_of(eng, t, held, last):
            table, step = (rt.tile_weights, w.step) if eng is nc.tensor else (rt.tile_biases, w.bias_step)
            if t.shared:
                return E * step
            e = held.pop(t.name, None)
            if e is None:
                e = eng.value_load(table[0:1, ds(t.i, 1)], min_val=0, max_val=(E - 1) * step)
            if not last:
                held[t.name] = e
            return e

        up_free = multiplied if gated else biased
        down_free = y_ready if gated else y_summed

        with nc.Block() as block:
            def walk(eng, step):
                def straight(first, end):
                    held = {}
                    for s in range(first, end):
                        step(lambda lag: known_tile(s - lag), held)

                straight(0, U + LAG)
                at = U + LAG
                for end in ([N0, N0 + NT, NX] if n_shared else [NX]):
                    full = (end - at) // R
                    shared = bool(n_shared) and end != N0 + NT
                    if full > 0:
                        with eng.Fori(0, full) as i:
                            held = {}
                            for q in range(R):
                                step(lambda lag: Tile(at + i * R + (q - lag), (at + q - lag) % U, (at + q - lag) % R,
                                                      shared, shared, end == NX, None, q - lag), held)
                        at += full * R
                    if end != NX:
                        straight(at, end + LAG + U)
                        at = end + LAG + U
                straight(at, NX + LAG)

            @block.sync
            def _(sp):
                def fetch(t):
                    j, v = t.j, t.v
                    if t.has(U):
                        if gated:
                            sp.wait_ge(multiplied.sem, multiplied.after(j - U))
                        else:
                            sp.wait_ge(t_copied.sem, t_copied.after(j - U))
                    if t.shared:
                        sp.dma_start(G[v][:, 0:D].unsqueeze(1), XS[:, ds(t.i, 1), 0:D]).then_inc(arrived[v], 16)
                    else:
                        sp.sem_inc(fetched, 1)
                        sp.wait_ge(placed, t.i + 1)
                        sp.dma_start(G[v][:], XG[ds(t.i * P, P), :]).then_inc(arrived[v], 16)

                def store(t):
                    j, v = t.j, t.v
                    sp.wait_ge(y_ready.sem, y_ready.after(t.i))
                    sp.dma_start(Y[ds(t.i * P, P), :], YO[v][:]).then_inc(stored[v], 16)

                def step(tile, held):
                    if tile(0):
                        fetch(tile(0))
                    if tile(LAG) and not tile(LAG).shared:
                        store(tile(LAG))

                walk(sp, step)
                for v in range(U):
                    sp.wait_ge(stored[v], 16 * ((NT - 1 - v) // U + 1))
                if out is not None:
                    for q in range(HT // W):
                        t = HT + q * W
                        sp.wait_ge(last_joined, q + 1)
                        sp.dma_start(out.rearrange("(t p) d -> p t d", p=P)[:, t:t + W, :],
                                     X[:, t * D:(t + W) * D].rearrange("p (t d) -> p t d", d=D)).then_inc(last_stored, 16)
                    sp.wait_ge(last_stored, 16 * (HT // W))

            @block.gpsimd
            def _(pool):
                for h in range(2):
                    tiles = range(h * HT, (h + 1) * HT)
                    for k in range(2):
                        if k == 1:
                            pool.wait_ge(sent, 16 * HT * (2 * h + 1))
                        nc.gpsimd.tensor_copy(XS[:, h * HT:(h + 1) * HT, D], rt.c[k][:, h * HT:(h + 1) * HT]).then_inc(reweighted, 1)
                        pool.wait_ge(reweighted, 2 * h + k + 1)
                        for t in tiles:
                            nc.gpsimd.indirect_dma_start(XG, bass.IndirectOffsetOnAxis(rt.slot[k][:, t:t + 1], 0),
                                                         XS[:, t, :], None).then_inc(sent, 16)
                    pool.wait_ge(sent, 16 * HT * (2 * h + 2))
                    pool.sem_inc(placed, NH)
                if out is None:
                    for v in range(U):
                        pool.wait_ge(stored[v], 16 * (NH // U))
                    for k in range(2):
                        for t in range(n_early):
                            nc.gpsimd.indirect_dma_start(X[:, t * D:(t + 1) * D], None, Y[0:NH * P, :],
                                                         bass.IndirectOffsetOnAxis(rt.slot[k][:, t:t + 1], 0),
                                                         compute_op=ALU.add).then_inc(early, 16)
                        pool.wait_ge(early, 16 * n_early * (k + 1))
                else:
                    rows = out.rearrange("(t p) d -> p t d", p=P)
                    for h in range(2):
                        tiles = range(h * HT, (h + 1) * HT)
                        for v in range(U):
                            pool.wait_ge(stored[v], 16 * (NH // U) * (h + 1))
                        if h == 1:
                            pool.wait_ge(x_joined, HT // W)
                        for k in range(2):
                            if k == 1:
                                pool.wait_ge(joined, 16 * HT * (h + 1))
                            for t in tiles:
                                q = t - h * HT
                                nc.gpsimd.indirect_dma_start(pairs[:, q * D:(q + 1) * D], None, Y[0:(h + 1) * NH * P, :],
                                                             bass.IndirectOffsetOnAxis(rt.slot[k][:, t:t + 1], 0),
                                                             compute_op=ALU.add if k else ALU.bypass).then_inc(got[q // W] if k else joined, 16)
                        if h == 1:
                            break
                        for t in tiles[::W]:
                            q = t - h * HT
                            pool.wait_ge(got[q // W], 16 * W)
                            pool.wait_ge(x_added.sem, x_added.after(t + W - 1))
                            x = X[:, t * D:(t + W) * D]
                            nc.gpsimd.tensor_tensor(x, x, pairs[:, q * D:(q + W) * D], ALU.add).then_inc(x_joined, 1)
                            pool.wait_ge(x_joined, t // W + 1)
                            nc.gpsimd.dma_start(rows[:, t:t + W, :], x.rearrange("p (t d) -> p t d", d=D)).then_inc(out_stored, 16)
                    pool.wait_ge(out_stored, 16 * (HT // W))

            @block.tensor
            def _(pe):
                def turn(t):
                    j, v = t.j, t.v
                    pe.wait_ge(arrived[v], t.raised(0))
                    if t.has(1):
                        pe.wait_ge(t_copied.sem, t_copied.after(j - 1))
                    nc.tensor.transpose(TP[:, 0:P], G[v][:, 0:D], ident[:]).then_inc(turned.sem, 1)

                def up(t, held):
                    j, v = t.j, t.v
                    e = place_of(nc.tensor, t, held, False)
                    pe.wait_ge(t_copied.sem, t_copied.after(j))
                    if t.has(2):
                        pe.wait_ge(up_free.sem, up_free.after(j - 2))
                    for at, c, n in up_cols:
                        ins = nc.tensor.matmul(UP[v % 2][:, at:at + n], gT[v % 2][:], w.w[:, ds(e + c, n)],
                                               start=True, stop=True)
                    ins.then_inc(up_ready.sem, 1)

                def turn_h(t):
                    j, v = t.j, t.v
                    pe.wait_ge(h_ready.sem, h_ready.after(j))
                    if t.has(1):
                        pe.wait_ge(h_copied.sem, h_copied.after(j - 1))
                    for c, (c0, n) in enumerate(chunks):
                        ins = nc.tensor.transpose(HP[0:n, c * P:(c + 1) * P], hid[v % 2][:, c0:c0 + n], ident[:])
                    ins.then_inc(h_turned.sem, 1)

                def down(t, held):
                    j, v = t.j, t.v
                    e = place_of(nc.tensor, t, held, True)
                    pe.wait_ge(h_copied.sem, h_copied.after(j))
                    if t.has(2):
                        pe.wait_ge(down_free.sem, down_free.after(j - 2))
                    for c, (c0, n) in enumerate(chunks):
                        ins = nc.tensor.matmul(DP[v % 2][:, 0:D], hT[v % 2][0:n, c * P:(c + 1) * P],
                                               w.w[0:n, ds(e + WU + c * D, D)], start=c == 0, stop=c == NC - 1)
                    ins.then_inc(down_ready.sem, 1)

                def step(tile, held):
                    if tile(3):
                        turn(tile(3))
                    if tile(4):
                        up(tile(4), held)
                    if tile(6):
                        down(tile(6), held)
                    if tile(5):
                        turn_h(tile(5))

                walk(pe, step)

            @block.scalar
            def _(act):
                def copy_t(t):
                    j, v = t.j, t.v
                    act.wait_ge(turned.sem, turned.after(j))
                    if not gated and not t.shared:
                        nc.scalar.activation(weight[:, t.w:t.w + 1], G[v][:, D:D + 1], ACT.Copy)
                    if t.has(2):
                        act.wait_ge(up_ready.sem, up_ready.after(j - 2))
                    if scale_col is not None:
                        ins = nc.scalar.activation(gT[v % 2][:], TP[:, 0:P], ACT.Copy, scale=scale_col[:, 0:1])
                    else:
                        ins = nc.scalar.activation(gT[v % 2][:], TP[:, 0:P], ACT.Copy)
                    ins.then_inc(t_copied.sem, 1)

                def silu(t):
                    j, v = t.j, t.v
                    if gated:
                        act.wait_ge(up_ready.sem, up_ready.after(j))
                        if t.has(2):
                            act.wait_ge(multiplied.sem, multiplied.after(j - 2))
                        ins = nc.scalar.activation(sg[v % 2][:, 0:H], UP[v % 2][:, 512:512 + H], ACT.Silu)
                    else:
                        act.wait_ge(multiplied.sem, multiplied.after(j))
                        if t.has(2):
                            act.wait_ge(h_turned.sem, h_turned.after(j - 2))
                        ins = nc.scalar.activation(hid[v % 2][:], sg[v % 2][:, 0:H], ACT.Silu)
                    ins.then_inc(silu_ready.sem, 1)

                def copy_h(t):
                    j, v = t.j, t.v
                    act.wait_ge(h_turned.sem, h_turned.after(j))
                    if t.has(2):
                        act.wait_ge(down_ready.sem, down_ready.after(j - 2))
                    for c, (c0, n) in enumerate(chunks):
                        if n == P:
                            continue
                        ins = nc.scalar.activation(hT[v % 2][0:n, c * P:(c + 1) * P], HP[0:n, c * P:(c + 1) * P], ACT.Copy)
                    full = H // P * P
                    ins = nc.scalar.activation(hT[v % 2][:, 0:full], HP[:, 0:full], ACT.Copy)
                    ins.then_inc(h_copied.sem, 1)

                def weigh(t):
                    act.wait_ge(y_summed.sem, y_summed.after(t.j))
                    nc.scalar.activation(YO[t.v][:], YO[t.v][:], ACT.Copy, scale=weight[:, t.w:t.w + 1]).then_inc(y_ready.sem, 1)

                def step(tile, held):
                    if tile(3):
                        copy_t(tile(3))
                    if tile(7) and not tile(7).shared and not gated:
                        weigh(tile(7))
                    if tile(4):
                        silu(tile(4))
                    if tile(5):
                        copy_h(tile(5))

                walk(act, step)

            @block.vector
            def _(dve):
                def multiply(t, held):
                    j, v = t.j, t.v
                    if gated:
                        dve.wait_ge(silu_ready.sem, silu_ready.after(j))
                        if t.has(2):
                            dve.wait_ge(h_turned.sem, h_turned.after(j - 2))
                        nc.vector.scalar_tensor_tensor(hid[v % 2][:], UP[v % 2][:, 0:H], G[v][:, D:D + 1], sg[v % 2][:, 0:H],
                                                       ALU.mult, ALU.mult).then_inc(multiplied.sem, 1)
                    else:
                        e = place_of(nc.vector, t, held, False)
                        dve.wait_ge(up_ready.sem, up_ready.after(j))
                        if t.has(2):
                            dve.wait_ge(silu_ready.sem, silu_ready.after(j - 2))
                        nc.vector.tensor_tensor(sg[v % 2][:], UP[v % 2][:, 0:WU], w.b[:, ds(e, WU)], ALU.add).then_inc(biased.sem, 1)
                        dve.wait_ge(biased.sem, biased.after(j))
                        nc.vector.tensor_tensor(sg[v % 2][:, 0:H], sg[v % 2][:, 0:H], sg[v % 2][:, H:WU], ALU.mult).then_inc(multiplied.sem, 1)

                def output(t, held):
                    j, v = t.j, t.v
                    e = None if w.b is None else place_of(nc.vector, t, held, True)
                    dve.wait_ge(down_ready.sem, down_ready.after(j))
                    if t.has(U) and not t.shared_before:
                        dve.wait_ge(stored[v], t.raised(N0 + U))
                    elif t.has(U):
                        dve.wait_ge(x_added.sem, x_added.after(t.i - U if t.shared else N0 - U + t.known % U))
                    if w.b is None:
                        nc.vector.tensor_copy(YO[v][:], DP[v % 2][:, 0:D]).then_inc(y_ready.sem, 1)
                    elif t.shared:
                        nc.vector.tensor_tensor(YO[v][:], DP[v % 2][:, 0:D], w.b[:, ds(e + WU, D)], ALU.add).then_inc(y_summed.sem, 1)
                        dve.wait_ge(y_summed.sem, y_summed.after(j))
                        x = X[:, ds(t.i * D, D)]
                        nc.vector.tensor_tensor(x, x, YO[v][:], ALU.add).then_inc(x_added.sem, 1)
                    else:
                        nc.vector.tensor_tensor(YO[v][:], DP[v % 2][:, 0:D], w.b[:, ds(e + WU, D)], ALU.add).then_inc(y_summed.sem, 1)

                def step(tile, held):
                    if tile(4):
                        multiply(tile(4), held)
                    if tile(6):
                        output(tile(6), held)

                walk(dve, step)
                if out is not None:
                    for q in range(HT // W):
                        t = HT + q * W
                        dve.wait_ge(got[q], 2 * 16 * W)
                        dve.wait_ge(x_added.sem, x_added.after(t + W - 1))
                        x = X[:, t * D:(t + W) * D]
                        nc.vector.tensor_tensor(x, x, pairs[:, q * W * D:(q + 1) * W * D], ALU.add).then_inc(last_joined, 1)


def state_space(nc, X, rt, Y, mean, scales, ident, norm_w, w_in, w_conv, conv_b, w_lr, w_bc, w_dt, dt_b, A, Dp, w_out, sel):
    CH = 2 * S
    NCH = B * S // CH
    G = CH // P
    L = S + 1
    NA = 4
    K = 3
    with ExitStack() as ctx:
        m = Maker(nc, ctx, "ss_")
        XL, XS = m.sb("XL", [P, CH]), m.sb("XS", [P, CH])
        st, mv = m.sb("st", [P, G, 6]), m.sb("mv", [P, G, 2])
        ve, lv, nw = m.sb("ve", [P, 2, G]), m.sb("lv", [P, 2, G]), m.sb("nw", [P, 2, G])
        xT = m.sb("xT", [P, CH])
        xpad = m.sb("xpad", [P, 2, 2, K + S])
        xi = [m.sb(f"xi{v}", [P, 2, CH]) for v in range(2)]
        gate = [m.sb(f"gate{v}", [P, 2, CH]) for v in range(2)]
        delta = [m.sb(f"delta{v}", [P, 2, CH]) for v in range(2)]
        du = [m.sb(f"du{v}", [P, 2, CH]) for v in range(2)]
        part = [m.sb(f"part{v}", [3 * 2 * N, CH], BF16) for v in range(2)]
        lr = m.sb("lr", [DT, CH])
        p1, p2 = m.sb("p1", [3 * 2 * N, CH], BF16), m.sb("p2", [3 * 2 * N, CH], BF16)
        r1 = m.sb("r1", [3 * 2 * N, CH])
        ez, ln, tz = m.sb("ez", [P, 2, CH]), m.sb("ln", [P, 2, CH]), m.sb("tz", [P, 2, CH])
        dA = [m.sb(f"dA{v}", [P, 2, 2, L]) for v in range(NA)]
        dBu = [m.sb(f"dBu{v}", [P, 2, 2, L]) for v in range(2)]
        Hs = [m.sb(f"Hs{v}", [P, 2, 2, L]) for v in range(2)]
        HC = [m.sb(f"HC{v}", [P, 2, CH]) for v in range(2)]
        yg = m.sb("yg", [P, 2, CH])
        Yp = [m.ps(f"Y{h}", [P, CH]) for h in range(2)]
        Bp = [m.ps(f"B{v}", [P, CH]) for v in range(2)]
        Cp = [m.ps(f"C{v}", [P, CH]) for v in range(2)]
        Q = [m.ps(f"Q{v}", [P, CH]) for v in range(2)]

        slot = [m.sb(f"slot{k}", [P, G], I32) for k in range(2)]
        pair = m.sb("pair", [P, CH])
        shift = m.sb("shift", [P, 2, T])
        dve_passed = m.sem("dve_passed")
        passed, joined = m.sem("passed"), m.sig("joined")
        cleared = m.sem("cleared")
        slots_ready = m.sig("slots_ready", 2)
        gathered = m.sig("gathered", 2 * G * 16)
        stats = m.sig("stats", 10)
        log_ready, root_ready = m.sig("log_ready"), m.sig("root_ready")
        rows = m.sig("rows", 2 * G)
        x_added = m.sig("x_added")
        turned, xT_copied = m.sig("turned"), m.sig("xT_copied")
        in_ready = m.sig("in_ready", 4)
        in_copied = m.sig("in_copied", 4)
        conv_ready = m.sig("conv_ready", 2)
        xi_ready = m.sig("xi_ready", 2)
        gate_ready = m.sig("gate_ready")
        dbl_ready = m.sig("dbl_ready", 2)
        lr_copied = m.sig("lr_copied")
        p1_copied = m.sig("p1_copied", 2)
        r1_ready = m.sig("r1_ready")
        p2_copied = m.sig("p2_copied", 2)
        r2_ready = m.sig("r2_ready")
        split = m.sig("split")
        dt_ready = m.sig("dt_ready", 2)
        z_copied = m.sig("z_copied", 4)
        ez_ready = m.sig("ez_ready")
        tz_ready = m.sig("tz_ready")
        ln_ready = m.sig("ln_ready")
        softplus = m.sig("softplus", 3)
        du_ready = m.sig("du_ready")
        b_ready, c_ready = m.sig("b_ready", N), m.sig("c_ready", N)
        dA_ready = m.sig("dA_ready", N)
        dBu_ready = m.sig("dBu_ready", N)
        scanned = m.sig("scanned", N)
        hc_ready = m.sig("hc_ready", N)
        summed = m.sig("summed", N)
        finish = m.sig("finish", 3)
        out_ready = m.sig("out_ready")
        x_updated = m.sig("x_updated")

        def seqs(a):
            return a.rearrange("p (s t) -> p s t", s=2)

        def both(a):
            return a.rearrange("p h (s t) -> p h s t", s=2)

        def flat(a):
            return a[:].rearrange("p h s t -> p (h s t)")

        def no_stats(k, c):
            pass

        def chunks(eng, scan, inputs, first=None, stats=no_stats):
            for k in range(N):
                stats(k, 0)
            stats(0, 1)
            for k in range(N):
                inputs(k, 0, 0)
            for k in range(1, N):
                stats(k, 1)
            if first is not None:
                first()
            scan(0, 0, 2)
            with eng.Fori(0, (NCH - 4) // 2) as i:
                scan(2 * i + 1, 1, 2)
                scan(2 * i + 2, 0, 2)
            scan(NCH - 3, 1, 2)
            scan(NCH - 2, 0, 1)
            scan(NCH - 1, 1, 0)

        with nc.Block() as block:
            @block.tensor
            def _(pe):
                pe.wait_ge(cleared, NA + 3)

                def inputs(k, c, v):
                    static = isinstance(c, int)
                    if k == 1:
                        pe.wait_ge(rows.sem, rows.after(c))
                        if not (static and c < 1):
                            pe.wait_ge(z_copied.sem, z_copied.after(c - 1))
                        for t in range(G):
                            ins = nc.tensor.transpose(Q[1][:, t * P:(t + 1) * P], XS[:, t * P:(t + 1) * P], ident[:])
                        ins.then_inc(turned.sem, 1)
                    if k == 2:
                        pe.wait_ge(xT_copied.sem, xT_copied.after(c))
                        if not (static and c < 2):
                            pe.wait_ge(x_updated.sem, x_updated.after(c - 2))
                        for q in range(2):
                            nc.tensor.matmul(Q[q][:], w_in[:, q * P:(q + 1) * P], xT[:], start=True, stop=True).then_inc(in_ready.sem, 1)
                    if k == 3:
                        for q in range(2, 4):
                            pe.wait_ge(in_copied.sem, in_copied.after(c, q - 1))
                            nc.tensor.matmul(Q[q - 2][:], w_in[:, q * P:(q + 1) * P], xT[:], start=True, stop=True).then_inc(in_ready.sem, 1)
                    if k in (5, 6):
                        h = k - 5
                        pe.wait_ge(in_copied.sem, in_copied.after(c, 3 + h))
                        for q in range(K + 1):
                            ins = nc.tensor.matmul(Q[h][:], w_conv[:, h, q, :], xpad[:, h, :, q:q + S], start=q == 0, stop=q == K)
                        ins.then_inc(conv_ready.sem, 1)
                    if k == 8:
                        pe.wait_ge(xi_ready.sem, xi_ready.after(c))
                        for h in range(2):
                            ins = nc.tensor.matmul(Q[0][0:DT, :], w_lr[:, h, :], xi[v][:, h, :], start=h == 0, stop=h == 1)
                        ins.then_inc(dbl_ready.sem, 1)
                        for h in range(2):
                            ins = nc.tensor.matmul(Q[1][0:6 * N, :], w_bc[:, h, :], xi[v][:, h, :], start=h == 0, stop=h == 1)
                        ins.then_inc(dbl_ready.sem, 1)
                    if k == 10:
                        pe.wait_ge(lr_copied.sem, lr_copied.after(c))
                        nc.tensor.matmul(Q[0][:], w_dt[:, 0:P], lr[:], start=True, stop=True).then_inc(dt_ready.sem, 1)
                        pe.wait_ge(r1_ready.sem, r1_ready.after(c))
                        nc.tensor.matmul(Q[1][:], w_dt[:, P:2 * P], lr[:], start=True, stop=True).then_inc(dt_ready.sem, 1)

                def spread_b(n, c, v):
                    if n >= 2:
                        pe.wait_ge(dBu_ready.sem, dBu_ready.after(c, n - 1))
                    elif not (isinstance(c, int) and c < 1):
                        pe.wait_ge(dBu_ready.sem, dBu_ready.after(c - 1, N - 1 + n))
                    nc.tensor.matmul(Bp[n % 2][:], sel[:, n, :], part[v][:], start=True, stop=True).then_inc(b_ready.sem, 1)

                def spread_c(n, c, v):
                    if n >= 2:
                        pe.wait_ge(hc_ready.sem, hc_ready.after(c, n - 1))
                    elif not (isinstance(c, int) and c < 1):
                        pe.wait_ge(hc_ready.sem, hc_ready.after(c - 1, N - 1 + n))
                    nc.tensor.matmul(Cp[n % 2][:], sel[:, N + n, :], part[v][:], start=True, stop=True).then_inc(c_ready.sem, 1)

                def output(c):
                    pe.wait_ge(finish.sem, finish.after(c))
                    for t in range(G):
                        for h in range(2):
                            ins = nc.tensor.matmul(Q[0][:, t * D:(t + 1) * D], yg[:, h, t * P:(t + 1) * P],
                                                   w_out[:, h, :], start=h == 0, stop=h == 1)
                    ins.then_inc(out_ready.sem, 1)

                def scan(c, v, more):
                    static = isinstance(c, int)
                    for n in range(N):
                        if n == N - 2 and more:
                            pe.wait_ge(split.sem, split.after(c + 1))
                        if n + 2 < N:
                            spread_b(n + 2, c, v)
                        elif more:
                            spread_b(n + 2 - N, c + 1, 1 - v)
                        if n + 1 < N:
                            spread_c(n + 1, c, v)
                        elif more:
                            spread_c(0, c + 1, 1 - v)
                        if more:
                            inputs(n, c + 1, 1 - v)
                        if n == 0 and not (static and c < 1):
                            pe.wait_ge(finish.sem, finish.after(c - 1, 2))
                        pe.wait_ge(hc_ready.sem, hc_ready.after(c, n + 1))
                        for h in range(2):
                            ins = nc.tensor.matmul(Yp[h][:], ident[:], HC[n % 2][:, h, :], start=n == 0, stop=n == N - 1)
                        ins.then_inc(summed.sem, 1)
                        if n == 0 and not (static and c < 1):
                            pe.wait_ge(z_copied.sem, z_copied.after(c))
                            output(c - 1)

                def first():
                    pe.wait_ge(split.sem, split.after(0))
                    spread_b(0, 0, 0)
                    spread_b(1, 0, 0)
                    spread_c(0, 0, 0)

                chunks(pe, scan, inputs, first)
                output(NCH - 1)

            @block.scalar
            def _(act):
                def inputs(k, c, v):
                    if k == 0:
                        if not (isinstance(c, int) and c < 1):
                            act.wait_ge(x_added.sem, x_added.after(c - 1))
                            act.wait_ge(turned.sem, turned.after(c - 1))
                        act.wait_ge(stats.sem, stats.after(c))
                        for t in range(G):
                            for q, dst in enumerate((XL, XS)):
                                nc.scalar.activation(dst[:, t * D:(t + 1) * D], X[:, ds(c * CH + t * D, D)], ACT.Identity,
                                                     bias=shift[:, q, ds(c * G + t, 1)],
                                                     scale=scales[:, q, ds(c * G + t, 1)]).then_inc(rows.sem, 1)
                    if k == 2:
                        act.wait_ge(turned.sem, turned.after(c))
                        nc.scalar.activation(xT[:], Q[1][:], ACT.Copy, scale=norm_w[:, 0:1]).then_inc(xT_copied.sem, 1)
                    if k in (3, 4):
                        for q in range(2 * k - 6, 2 * k - 4):
                            act.wait_ge(in_ready.sem, in_ready.after(c, q + 1))
                            dst = xpad[:, q, :, K:K + S] if q < 2 else seqs(gate[v][:, q - 2, :])
                            nc.scalar.activation(dst, seqs(Q[q % 2][:]), ACT.Copy).then_inc(in_copied.sem, 1)
                    if k == 7:
                        for h in range(2):
                            act.wait_ge(conv_ready.sem, conv_ready.after(c, h + 1))
                            nc.scalar.activation(xi[v][:, h, :], Q[h][:], ACT.Silu, bias=conv_b[:, h:h + 1]).then_inc(xi_ready.sem, 1)
                        act.wait_ge(in_copied.sem, in_copied.after(c))
                        nc.scalar.activation(gate[v][:], gate[v][:], ACT.Silu).then_inc(gate_ready.sem, 1)
                    if k == 9:
                        act.wait_ge(dbl_ready.sem, dbl_ready.after(c, 1))
                        nc.scalar.activation(lr[:], Q[0][0:DT, :], ACT.Copy).then_inc(lr_copied.sem, 1)
                        act.wait_ge(dbl_ready.sem, dbl_ready.after(c, 2))
                        nc.scalar.activation(p1[:], Q[1][0:6 * N, :], ACT.Copy).then_inc(p1_copied.sem, 1)
                        nc.scalar.activation(part[v][0:2 * N, :], Q[1][0:2 * N, :], ACT.Copy).then_inc(p1_copied.sem, 1)
                    if k == 10:
                        act.wait_ge(r1_ready.sem, r1_ready.after(c))
                        nc.scalar.activation(p2[:], r1[:], ACT.Copy).then_inc(p2_copied.sem, 1)
                        nc.scalar.activation(part[v][2 * N:4 * N, :], r1[2 * N:4 * N, :], ACT.Copy).then_inc(p2_copied.sem, 1)
                    if k == 12:
                        act.wait_ge(r2_ready.sem, r2_ready.after(c))
                        nc.scalar.activation(part[v][4 * N:6 * N, :], r1[4 * N:6 * N, :], ACT.Copy).then_inc(split.sem, 1)
                    if k == 11:
                        for h in range(2):
                            act.wait_ge(dt_ready.sem, dt_ready.after(c, h + 1))
                            nc.scalar.activation(ez[:, h, :], Q[h][:], ACT.Abs, bias=dt_b[:, h:h + 1]).then_inc(z_copied.sem, 1)
                            nc.scalar.activation(delta[v][:, h, :], Q[h][:], ACT.Relu, bias=dt_b[:, h:h + 1]).then_inc(z_copied.sem, 1)
                        act.wait_ge(z_copied.sem, z_copied.after(c))
                        nc.scalar.activation(ez[:], ez[:], ACT.Exp, scale=-1.0).then_inc(ez_ready.sem, 1)
                        act.wait_ge(ez_ready.sem, ez_ready.after(c))
                        nc.scalar.activation(ln[:], ez[:], ACT.Ln, bias=1.0).then_inc(ln_ready.sem, 1)

                def roots(k, c):
                    if k == 11:
                        act.wait_ge(stats.sem, stats.after(c, 4))
                        nc.scalar.activation(lv[:], ve[:], ACT.Ln).then_inc(log_ready.sem, 1)
                    if k == 12:
                        act.wait_ge(log_ready.sem, log_ready.after(c))
                        nc.scalar.activation(scales[:, :, ds(c * G, G)], lv[:], ACT.Exp, scale=-0.5).then_inc(root_ready.sem, 1)

                def powers(n, c, v):
                    if n >= NA:
                        act.wait_ge(scanned.sem, scanned.after(c, n - NA + 1))
                    elif not (isinstance(c, int) and c < 1):
                        act.wait_ge(scanned.sem, scanned.after(c - 1, N - NA + n + 1))
                    for h in range(2):
                        ins = nc.scalar.activation(dA[n % NA][:, h, :, 1:L], seqs(delta[v][:, h, :]), ACT.Exp, scale=A[:, h, n:n + 1])
                    ins.then_inc(dA_ready.sem, 1)

                def first():
                    act.wait_ge(softplus.sem, softplus.after(0))
                    for n in range(NA - 1):
                        powers(n, 0, 0)

                def scan(c, v, more):
                    for n in range(N):
                        ahead = n + NA - 1
                        if ahead == N and more:
                            act.wait_ge(softplus.sem, softplus.after(c + 1))
                        if ahead < N:
                            powers(ahead, c, v)
                        elif more:
                            powers(ahead - N, c + 1, 1 - v)
                        if more:
                            inputs(n, c + 1, 1 - v)
                        if more > 1:
                            roots(n, c + 2)

                chunks(act, scan, inputs, first, roots)

            @block.gpsimd
            def _(pool):
                nc.gpsimd.memset(xpad[:], 0.0).then_inc(cleared, 1)

                def gather(c):
                    if not (isinstance(c, int) and c < 3):
                        pool.wait_ge(joined.sem, joined.after(c - 3))
                    pool.wait_ge(slots_ready.sem, slots_ready.after(c - 2))
                    pool.sem_inc(passed, 1)
                    for t in range(G):
                        nc.gpsimd.indirect_dma_start(pair[:, t * D:(t + 1) * D], None, Y,
                                                     bass.IndirectOffsetOnAxis(slot[0][:, t:t + 1], 0)).then_inc(gathered.sem, 16)
                    pool.wait_ge(gathered.sem, gathered.after(c - 2, G * 16))
                    pool.sem_inc(passed, 1)
                    for t in range(G):
                        nc.gpsimd.indirect_dma_start(pair[:, t * D:(t + 1) * D], None, Y,
                                                     bass.IndirectOffsetOnAxis(slot[1][:, t:t + 1], 0),
                                                     compute_op=ALU.add).then_inc(gathered.sem, 16)
                    pool.wait_ge(gathered.sem, gathered.after(c - 2))
                    pool.sem_inc(passed, 1)
                    x = X[:, ds(c * CH, CH)]
                    nc.gpsimd.tensor_tensor(x, x, pair[:], ALU.add).then_inc(joined.sem, 1)

                def skip(c):
                    pool.wait_ge(rows.sem, rows.after(c))
                    pool.sem_inc(passed, 1)
                    x = X[:, ds(c * CH, CH)]
                    nc.gpsimd.tensor_tensor(x, x, XL[:], ALU.add).then_inc(x_added.sem, 1)

                def inputs(c, v):
                    pool.wait_ge(p2_copied.sem, p2_copied.after(c))
                    nc.gpsimd.tensor_tensor(r1[:], r1[:], p2[:], ALU.subtract).then_inc(r2_ready.sem, 1)
                    pool.wait_ge(tz_ready.sem, tz_ready.after(c))
                    nc.gpsimd.tensor_tensor(tz[:], ez[:], tz[:], ALU.subtract).then_inc(softplus.sem, 1)
                    pool.wait_ge(softplus.sem, softplus.after(c, 1))
                    nc.gpsimd.tensor_tensor(delta[v][:], delta[v][:], tz[:], ALU.add).then_inc(softplus.sem, 1)
                    pool.wait_ge(softplus.sem, softplus.after(c, 2))
                    pool.wait_ge(ln_ready.sem, ln_ready.after(c))
                    nc.gpsimd.tensor_tensor(delta[v][:], delta[v][:], ln[:], ALU.add).then_inc(softplus.sem, 1)
                    pool.wait_ge(softplus.sem, softplus.after(c))
                    nc.gpsimd.tensor_tensor(du[v][:], delta[v][:], xi[v][:], ALU.mult).then_inc(du_ready.sem, 1)

                for c in range(2):
                    skip(c)
                    if c == 1:
                        gather(2)
                    inputs(c, c)
                with pool.Fori(0, (NCH - 4) // 2) as i:
                    for v in range(2):
                        skip(2 * i + 2 + v)
                        gather(2 * i + 3 + v)
                        inputs(2 * i + 2 + v, v)
                for c in range(NCH - 2, NCH):
                    skip(c)
                    if c + 1 < NCH:
                        gather(c + 1)
                    inputs(c, c % 2)

            @block.vector
            def _(dve):
                v_ = nc.vector
                for v in range(NA):
                    v_.memset(dA[v][:, :, :, 0], 0.0).then_inc(cleared, 1)
                for v in range(2):
                    v_.memset(dBu[v][:, :, :, 0], 0.0).then_inc(cleared, 1)
                dve.wait_ge(cleared, NA + 3)

                def scales_of(k, c):
                    y = scales[:, :, ds(c * G, G)]
                    static = isinstance(c, int)
                    if k == 0 and not (static and c < 2):
                        if not (static and c < 3):
                            dve.wait_ge(gathered.sem, gathered.after(c - 3))
                        for q in range(2):
                            v_.tensor_copy(slot[q][:], rt.slot[q][:, ds(c * G, G)]).then_inc(slots_ready.sem, 1)
                    if k == 7:
                        if not (static and c < 2):
                            dve.wait_ge(joined.sem, joined.after(c - 2))
                        for t in range(G):
                            ins = v_.bn_stats(st[:, t, :], X[:, ds((c * G + t) * D, D)])
                        ins.then_inc(stats.sem, 1)
                    if k == 8:
                        dve.wait_ge(stats.sem, stats.after(c, 1))
                        dve.sem_inc(dve_passed, 1)
                        for t in range(G):
                            ins = v_.bn_aggr(mv[:, t, :], st[:, t, :])
                        ins.then_inc(stats.sem, 1)
                    if k == 9:
                        dve.wait_ge(stats.sem, stats.after(c, 2))
                        v_.tensor_scalar(ve[:, 0, :], mv[:, :, 1], EPS, None, ALU.add).then_inc(stats.sem, 1)
                        v_.tensor_scalar(ve[:, 1, :], mv[:, :, 1], 1.0 + EPS, EPS * EPS, ALU.mult, ALU.add).then_inc(stats.sem, 1)
                        v_.tensor_copy(mean[:, ds(c * G, G)], mv[:, :, 0]).then_inc(stats.sem, 1)
                    if k == 13:
                        dve.wait_ge(root_ready.sem, root_ready.after(c))
                        v_.tensor_tensor(nw[:], y, y, ALU.mult).then_inc(stats.sem, 1)
                        dve.wait_ge(stats.sem, stats.after(c, 6))
                        v_.tensor_tensor(nw[:], nw[:], ve[:], ALU.mult).then_inc(stats.sem, 1)
                    if k == 14:
                        dve.wait_ge(stats.sem, stats.after(c, 7))
                        v_.tensor_scalar(nw[:], nw[:], -0.5, 1.5, ALU.mult, ALU.add).then_inc(stats.sem, 1)
                        dve.wait_ge(stats.sem, stats.after(c, 8))
                        v_.tensor_tensor(y, y, nw[:], ALU.mult).then_inc(stats.sem, 1)
                        dve.wait_ge(stats.sem, stats.after(c, 9))
                        v_.scalar_tensor_tensor(shift[:, :, ds(c * G, G)], mean[:, ds(c * G, G)].unsqueeze(1).to_broadcast([P, 2, G]),
                                                -1.0, y, ALU.mult, ALU.mult).then_inc(stats.sem, 1)

                def inputs(k, c, v):
                    static = isinstance(c, int)
                    if k == 9:
                        dve.wait_ge(p1_copied.sem, p1_copied.after(c))
                        if not (static and c < 1):
                            dve.wait_ge(split.sem, split.after(c - 1))
                        v_.tensor_tensor(r1[:], Q[1][0:6 * N, :], p1[:], ALU.subtract).then_inc(r1_ready.sem, 1)
                    if k == 11:
                        dve.wait_ge(ez_ready.sem, ez_ready.after(c))
                        if not (static and c < 1):
                            dve.wait_ge(softplus.sem, softplus.after(c - 1))
                        v_.tensor_scalar(tz[:], ez[:], 1.0, 1.0, ALU.add, ALU.subtract).then_inc(tz_ready.sem, 1)

                def times_b(n, c, v):
                    q = n % 2
                    if n == 0:
                        dve.wait_ge(du_ready.sem, du_ready.after(c))
                    dve.wait_ge(b_ready.sem, b_ready.after(c, n + 1))
                    v_.tensor_tensor(dBu[q][:, :, :, 1:L], both(du[v][:]), seqs(Bp[q][:]).unsqueeze(1).to_broadcast([P, 2, 2, S]),
                                     ALU.mult).then_inc(dBu_ready.sem, 1)

                def sums(c, v):
                    dve.wait_ge(summed.sem, summed.after(c))
                    for h in range(2):
                        v_.scalar_tensor_tensor(yg[:, h, :], xi[v][:, h, :], Dp[:, h:h + 1], Yp[h][:], ALU.mult, ALU.add).then_inc(finish.sem, 1)

                def gated(c, v):
                    dve.wait_ge(finish.sem, finish.after(c, 2))
                    v_.tensor_tensor(yg[:], yg[:], gate[v][:], ALU.mult).then_inc(finish.sem, 1)

                def update(c):
                    dve.wait_ge(out_ready.sem, out_ready.after(c))
                    dve.wait_ge(x_added.sem, x_added.after(c))
                    x = X[:, ds(c * CH, CH)]
                    v_.tensor_tensor(x, x, Q[0][:], ALU.add).then_inc(x_updated.sem, 1)

                def scan(c, v, more):
                    static = isinstance(c, int)
                    times_b(0, c, v)
                    for n in range(N):
                        q = n % 2
                        dve.wait_ge(dBu_ready.sem, dBu_ready.after(c, n + 1))
                        dve.wait_ge(dA_ready.sem, dA_ready.after(c, n + 1))
                        if n >= 2:
                            dve.wait_ge(hc_ready.sem, hc_ready.after(c, n - 1))
                        v_.tensor_tensor_scan(flat(Hs[q]), flat(dA[n % NA]), flat(dBu[q]), 0.0, ALU.mult, ALU.add).then_inc(scanned.sem, 1)
                        if n == 0 and not (static and c < 1):
                            sums(c - 1, 1 - v)
                        if n + 1 < N:
                            times_b(n + 1, c, v)
                        dve.wait_ge(scanned.sem, scanned.after(c, n + 1))
                        dve.wait_ge(c_ready.sem, c_ready.after(c, n + 1))
                        if n >= 2:
                            dve.wait_ge(summed.sem, summed.after(c, n - 1))
                        v_.tensor_tensor(both(HC[q][:]), Hs[q][:, :, :, 1:L], seqs(Cp[q][:]).unsqueeze(1).to_broadcast([P, 2, 2, S]),
                                         ALU.mult).then_inc(hc_ready.sem, 1)
                        if more:
                            inputs(n, c + 1, 1 - v)
                        if more > 1:
                            scales_of(n, c + 2)
                        if not (static and c < 1):
                            if n == 0:
                                gated(c - 1, 1 - v)
                            if n == 1:
                                update(c - 1)

                chunks(dve, scan, inputs, stats=scales_of)
                sums(NCH - 1, 1)
                gated(NCH - 1, 1)
                update(NCH - 1)


def build(nc, a, out):
    XG0 = nc.dram_tensor("rows0", [NT * P, D + 1], F32, kind="Internal").ap()
    XG1 = nc.dram_tensor("rows1", [NT * P, D + 1], F32, kind="Internal").ap()
    Y0 = nc.dram_tensor("out_rows0", [NT * P, D], F32, kind="Internal").ap()
    Y1 = nc.dram_tensor("out_rows1", [NT * P, D], F32, kind="Internal").ap()
    with ExitStack() as outer:
        g = Maker(nc, outer, "g_")
        X = g.sb("X", [P, T * D])
        mean, scales = g.sb("mean", [P, T]), g.sb("scales", [P, 2, T])
        ident = g.sb("ident", [P, P])
        tri, ones = g.sb("tri", [P, P], BF16), g.sb("ones", [P, P], BF16)
        rev = g.sb("rev", [P, E])
        masks = g.sb("masks", [P, E * T + 2 * E])
        tile_of_half = g.sb("tile_of_half", [1, NH])
        Z = g.sb("Z", [P, D + 1])
        rt = Routing(g)
        LGT = g.sb("LGT", [P, T, E])
        w1 = MixtureWeights(g, "m1_", a, None, "w_router1", "gate_b1", ("w_up1", "w_down1"), T, H1, "b1")
        w_in, conv_w, conv_b = g.sb("w_in", [P, 4 * P]), g.sb("conv_w", [P, 2, 4]), g.sb("conv_b", [P, 2])
        w_lr, w_bc, w_dt = g.sb("w_lr", [P, 2, DT]), g.sb("w_bc", [P, 2, 6 * N]), g.sb("w_dt", [DT, DI])
        dt_b, A, Dp, w_out = g.sb("dt_b", [P, 2]), g.sb("A", [P, 2, N]), g.sb("Dp", [P, 2]), g.sb("w_out", [P, 2, D])
        norm_w = g.sb("norm_w", [P, 1])
        sel = g.sb("sel", [6 * N, 2 * N, P], BF16)
        ss_pairs = [(w_in[:], a["w_in"]), (conv_w[:], a["conv_w"]), (conv_b[:], a["conv_b"]), (w_lr[:], a["w_lr"]),
                    (w_bc[:], a["w_bc"]), (w_dt[:], a["w_dt"]), (dt_b[:], a["dt_b"]), (A[:], a["A_log"]),
                    (Dp[:], a["Dp"]), (w_out[:], a["w_out"]), (norm_w[:], a["norm_w"]), (sel[:], a["sel"])]
        cleared, zeroed = g.sem("cleared"), g.sig("zeroed", 16)
        x_loaded = [g.sem(f"x_loaded{k}") for k in range(4)]
        first_loaded, ss_loaded = g.sig("first_loaded", 16), g.sig("ss_loaded", 16)
        chain = g.sig("chain")
        router_signals = [g.sig("r_" + n) for n in ("added", "turned", "copied", "scored", "kept", "staged")]
        route_signals = [g.sig("q_" + n) for n in ("shifted", "powered", "marks", "ranked")]
        stat_signals = (chain, g.sig("shifted"), g.sig("rooted"))
        front = outer.enter_context(ExitStack())
        w0 = MixtureWeights(Maker(nc, front, "g_"), "m0_", a, "norm0", "w_router0", None, ("w_up0", "w_down0"), 0, H0, None)
        with ExitStack() as ctx:
            m = Maker(nc, ctx, "a_")
            w = m.sb("w", [P, 9 * P + IH])
            bias, b_iw, rope = m.sb("bias", [P, 8]), m.sb("b_iw", [P, IH]), m.sb("rope", [P, 2 * S])
            b_o, shift = m.sb("b_o", [P, D]), m.sb("shift", [P, T])
            xd = a["x"].rearrange("(t p) d -> p t d", p=P)
            first = [(ident[:], a["ident"]), (tri[:], a["tri"]), (ones[:], a["ones"]), (rev[:], a["rev"]),
                     (masks[:], a["masks"]), (tile_of_half[:], a["tile_of_half"]),
                     (w[:], a["w_attn"]), (bias[:], a["b_attn"]), (b_iw[:], a["b_iw"]), (rope[:], a["rope"]),
                     (b_o[:], a["b_o"])]
            def first_loads(sp):
                n = T // len(x_loaded)
                for t in range(0, T, n):
                    sp.dma_start(X[:, t * D:(t + n) * D].rearrange("p (t d) -> p t d", d=D), xd[:, t:t + n, :]).then_inc(x_loaded[t // n], 16)
                for dst, src in first:
                    sp.dma_start(dst, src).then_inc(first_loaded.sem, 16)

            def clear():
                nc.gpsimd.memset(Z[:], 0.0).then_inc(cleared, 1)

            def later_loads(sp):
                for dst, src in w0.pairs:
                    sp.dma_start(dst, src).then_inc(w0.loaded.sem, 16)
                sp.wait_ge(cleared, 1)
                for XG in (XG0, XG1):
                    sp.dma_start(XG.rearrange("(t p) d -> p t d", p=P),
                                 Z[:, 0:XG.shape[1]].unsqueeze(1).to_broadcast([P, NT, XG.shape[1]])).then_inc(zeroed.sem, 16)
                for dst, src in ss_pairs:
                    sp.dma_start(dst, src).then_inc(ss_loaded.sem, 16)
                for dst, src in w1.pairs:
                    sp.dma_start(dst, src).then_inc(w1.loaded.sem, 16)

            row_stats(nc, "n0_", *stat_signals, X, mean, scales, None, first_loads, x_loaded, shift)
            wait_loaded(nc, first_loaded, len(first))
            attention(nc, X, shift, scales, ident, w, bias, b_iw, b_o, rope, later_loads, clear)
        wait_loaded(nc, zeroed, 2)

        def mixture(tag, w, XG, Y, skip, gated, out):
            with ExitStack() as ctx:
                m = Maker(nc, ctx, tag)
                wait_loaded(nc, w.loaded, len(w.pairs))
                XS = m.sb("XS", [P, T, XG.shape[1]])
                XL = m.sb("XL", [P, T * D]) if skip else None
                router(nc, tag + "r_", router_signals, X, XL, XS, skip, mean, scales, w.ns is not None, w.ns, w.wr, ident, LGT)
                route(nc, tag + "q_", chain, route_signals, LGT, w, rt, tri, ones, rev, masks, tile_of_half)
                experts(nc, tag + "x_", X, XS, rt, XG, Y, out, 4 * S // P, w, gated, ident)

        row_stats(nc, "n1_", *stat_signals, X, mean, scales, 1e-6)
        mixture("m0_", w0, XG0, Y0, True, True, None)
        front.close()
        with ExitStack() as ctx:
            m = Maker(nc, ctx, "s_")
            powered = m.sem("powered")
            w_conv = m.sb("w_conv", [P, 2, 4, P])
            wait_loaded(nc, ss_loaded, len(ss_pairs))
            with nc.Block() as block:
                @block.scalar
                def _(act):
                    nc.scalar.activation(A[:], A[:], ACT.Exp).then_inc(powered, 1)

                @block.vector
                def _(dve):
                    for h in range(2):
                        for q in range(4):
                            nc.vector.tensor_scalar(w_conv[:, h, q, :], ident[:], conv_w[:, h, q:q + 1], None, ALU.mult)
                    dve.wait_ge(powered, 1)
                    nc.vector.tensor_scalar(A[:], A[:], -1.0, None, ALU.mult)
            state_space(nc, X, rt, Y0, mean, scales, ident, norm_w, w_in, w_conv, conv_b, w_lr, w_bc, w_dt, dt_b, A, Dp, w_out, sel)
        row_stats(nc, "n3_", *stat_signals, X, mean, scales, None)
        mixture("m1_", w1, XG1, Y1, False, False, out)


def kernel(**inputs):
    import ml_dtypes
    import concourse.bacc as bacc
    from concourse.bass_utils import run_bass_kernel_spmd as run

    i = {k: np.asarray(v) for k, v in inputs.items()}
    f = np.float32
    c = np.ascontiguousarray

    def rows(v):
        return np.broadcast_to(v.reshape(1, -1), (P, v.size))

    def halves(v):
        return v.reshape((2, P) + v.shape[1:]).swapaxes(0, 1)

    wqkv, bqkv = i["L0_attn_w_qkv"], i["L0_attn_b_qkv"]
    swap = np.roll(np.arange(D), -(D // 2))
    q, k, v = wqkv[0:D], wqkv[D:2 * D], wqkv[2 * D:3 * D]
    bq, bk, bv = bqkv[0:D], bqkv[D:2 * D], bqkv[2 * D:3 * D]
    wiq, wik = i["L0_attn_w_iq"], i["L0_attn_w_ik"]
    biq, bik = i["L0_attn_b_iq"], i["L0_attn_b_ik"]
    w_attn = np.concatenate([q, k, q[swap], k[swap], wiq, wik, wik, v, i["L0_attn_w_iw"], i["L0_attn_w_o"]], 0).T
    b_attn = np.stack([bq, bk, bq[swap], bk[swap], biq[0:D], biq[D:2 * D], np.concatenate([bik, bik]), bv], 1)
    half = D // 2
    inv_freq = (f(1.0) / f(10000.0) ** (np.arange(half, dtype=f) / f(half))).astype(f)
    ang = (np.arange(S, dtype=f)[:, None] * inv_freq[None, :]).astype(f)
    cos, sin = np.cos(ang).T.astype(f), np.sin(ang).T.astype(f)
    rope = np.concatenate([np.concatenate([cos, cos], 0), np.concatenate([-sin, sin], 0)], 1)
    sel = np.zeros((6 * N, 2 * N, P), ml_dtypes.bfloat16)
    for n in range(2 * N):
        sel[n::2 * N, n, :] = 1
    xp = i["L1_attn_x_proj_w"]
    bc = xp[:, DT:DT + 2 * N]
    w13 = np.concatenate([np.concatenate([i["L1_ffn_w1"], i["L1_ffn_w3"]], 2),
                          np.concatenate([i["L1_ffn_sw1"], i["L1_ffn_sw3"]], 1)[None]], 0)
    b13 = np.concatenate([np.concatenate([i["L1_ffn_b1"], i["L1_ffn_b3"]], 1),
                          np.concatenate([i["L1_ffn_sb1"], i["L1_ffn_sb3"]], 0)[None]], 0)
    arrays = {
        "x": i["L0_attn_x"].reshape(B * S, D),
        "ident": np.eye(P, dtype=f),
        "tri": np.triu(np.ones((P, P), f), 1).astype(ml_dtypes.bfloat16),
        "ones": np.ones((P, P), ml_dtypes.bfloat16),
        "rev": rows(np.arange(E, 0, -1).astype(f)),
        "masks": rows(np.concatenate([np.arange(E * T) % HT != 0, np.arange(2 * E) % E != 0]).astype(f)),
        "tile_of_half": np.arange(NH, dtype=f).reshape(1, NH),
        "w_attn": w_attn, "b_attn": b_attn, "b_iw": rows(i["L0_attn_b_iw"]), "rope": rope, "b_o": rows(i["L0_attn_b_o"]),
        "norm0": i["L0_ffn_norm_scale"].reshape(P, 1),
        "w_router0": i["L0_ffn_w_router"].T,
        "w_up0": i["L0_ffn_w_up"].transpose(2, 0, 1),
        "w_down0": i["L0_ffn_w_down"].transpose(0, 2, 1),
        "w_in": i["L1_attn_in_proj_w"],
        "conv_w": halves(i["L1_attn_conv_w"][:, 0, :]),
        "conv_b": halves(i["L1_attn_conv_b"]),
        "w_lr": halves(xp[:, 0:DT]),
        "w_bc": halves(np.concatenate([bc, bc, bc], 1)),
        "w_dt": i["L1_attn_dt_proj_w"],
        "dt_b": halves(i["L1_attn_dt_proj_b"]),
        "A_log": halves(i["L1_attn_A_log"]),
        "Dp": halves(i["L1_attn_D"]),
        "w_out": halves(i["L1_attn_out_proj_w"]),
        "norm_w": i["L1_attn_norm_w"].reshape(P, 1),
        "sel": sel,
        "w_router1": i["L1_ffn_gate_w"].T,
        "gate_b1": rows(i["L1_ffn_gate_b"]),
        "w_up1": w13.transpose(1, 0, 2),
        "w_down1": np.concatenate([i["L1_ffn_w2"], i["L1_ffn_sw2"][None]], 0),
        "b1": rows(np.concatenate([b13, np.concatenate([i["L1_ffn_b2"], i["L1_ffn_sb2"][None]], 0)], 1)),
    }
    nc = bacc.Bacc("TRN2", target_bir_lowering=False, num_devices=1)
    arrays = {"in_" + n: c(v) for n, v in arrays.items()}
    a = {n[3:]: nc.dram_tensor(n, v.shape, mybir.dt.from_np(v.dtype), kind="ExternalInput").ap() for n, v in arrays.items()}
    out = nc.dram_tensor("out", [B * S, D], F32, kind="ExternalOutput").ap()
    build(nc, a, out)
    r = run(nc, [arrays], core_ids=[0])
    return r.results[0]["out"].reshape(B, S, D)
```
